# Optimizing a Trainium2 kernel written in Bass

```python
import numpy as np
import jax
import jax.numpy as jnp

def _softmax(x, axis=-1):
    return jax.nn.softmax(x, axis=axis)

def _gelu(x):
    return jax.nn.gelu(x, approximate=True)

def _silu(x):
    return jax.nn.silu(x)

def _sigmoid(x):
    return jax.nn.sigmoid(x)

def _layernorm(x, axis=-1, eps=1e-05):
    m = jnp.mean(x, axis=axis, keepdims=True)
    v = jnp.var(x, axis=axis, keepdims=True)
    return (x - m) / jnp.sqrt(v + eps)

def _scatter_add(tgt, idx, src, axis=0):
    return tgt.at[idx].add(src)

def _segment_sum(src, seg, n):
    return jax.ops.segment_sum(src, seg, n)
kernel_name = 'mk_perceiver_d1_seqx_r2_14e91f'

def setup_inputs(seed: int=0):
    np.random.seed(seed)
    _w = jnp.asarray

    def _rec_inputs():
        import jax
        import jax.numpy as jnp
        _rk = jax.random.key(seed)
        x = 0.0002417 + 0.9998 * jax.random.normal(jax.random.fold_in(_rk, 1), (1, 256, 512), jnp.float32)
        _lenS = 256 - jax.random.randint(jax.random.fold_in(_rk, 7), (1,), 0, max(1, 256 // 4) + 1, jnp.int32)
        _lenS2 = 25088 - jax.random.randint(jax.random.fold_in(_rk, 8), (1,), 0, max(1, 25088 // 4) + 1, jnp.int32)
        _ctx_1024P = jax.random.normal(jax.random.fold_in(_rk, 11), (1, 16, 512), jnp.float32)
        _ctx_1024c = jax.random.dirichlet(jax.random.fold_in(_rk, 511), 0.3 * jnp.ones((16,), jnp.float32), (1, 25088))
        _ctx_1024t = jnp.einsum('bsk,bkd->bsd', _ctx_1024c, _ctx_1024P)
        _ctx_1024t = _ctx_1024t * jax.lax.rsqrt(jnp.mean(jnp.square(_ctx_1024t)) + 1e-12) * 0.953939
        ctx_1024 = 7.22013e-05 + 1.00017 * (_ctx_1024t + 0.3 * jax.random.normal(jax.random.fold_in(_rk, 611), (1, 25088, 512), jnp.float32))
        return (x, ctx_1024)
    x, ctx_1024 = _rec_inputs()

    def _L0_xattn_setup():
        import jax, jax.numpy as jnp
        import numpy as np
        N_HEADS = 16
        D_MODEL = 512
        D_HEAD = 64
        B, S = (4, 1024)
        key = jax.random.key(seed)
        kv, kk, kq, kwi, kwo = jax.random.split(key, 5)
        v = jax.random.normal(kv, (B, S, D_MODEL), dtype=jnp.float32)
        k = jax.random.normal(kk, (B, S, D_MODEL), dtype=jnp.float32)
        q = jax.random.normal(kq, (B, S, D_MODEL), dtype=jnp.float32)
        wi = jax.random.normal(kwi, (D_MODEL, D_HEAD), dtype=jnp.float32) * D_MODEL ** (-0.5)
        Wo = jax.random.normal(kwo, (N_HEADS * D_HEAD, D_MODEL), dtype=jnp.float32) * (N_HEADS * D_HEAD) ** (-0.5)
        bo = jnp.zeros((D_MODEL,), dtype=jnp.float32)
        return {'v': v, 'k': k, 'q': q, 'wi': wi, 'Wo': Wo, 'bo': bo}
    _L0_xattn_all = _L0_xattn_setup()
    _L0_xattn_in = {k: v for k, v in _L0_xattn_all.items() if k in ('wi', 'Wo', 'bo')}
    del _L0_xattn_all

    def _L0_attn_setup():
        import jax, jax.numpy as jnp
        import numpy as np
        EMB = 512
        HEADS = 16
        EPS = 1e-05

        def layer_norm(x):
            mu = jnp.mean(x, axis=-1, keepdims=True)
            var = jnp.var(x, axis=-1, keepdims=True)
            return (x - mu) / jnp.sqrt(var + EPS)

        def pattention(x, K, V):
            scale = EMB ** (-0.5)
            a = jax.nn.softmax(scale * jnp.einsum('btc,nc->btn', x, K), axis=-1)
            return jnp.einsum('btn,nc->btc', a, V)

        def causal_sdpa(q, k, v):
            T = q.shape[2]
            d = q.shape[-1]
            scores = jnp.einsum('bhqd,bhkd->bhqk', q, k) / jnp.sqrt(jnp.asarray(d, q.dtype))
            mask = jnp.tril(jnp.ones((T, T), dtype=bool))
            scores = jnp.where(mask, scores, jnp.asarray(-jnp.inf, q.dtype))
            attn = jax.nn.softmax(scores, axis=-1)
            return jnp.einsum('bhqk,bhkd->bhqd', attn, v)
        key = jax.random.key(seed)
        ks = jax.random.split(key, 11)
        B, T, C = (2, 1024, EMB)
        N = 1024 // 2
        inp = {'x': jax.random.normal(ks[0], (B, T, C), dtype=jnp.float32)}
        names = ['qK', 'qV', 'kK', 'kV', 'vK', 'vV', 'pK', 'pV']
        for i, nm in enumerate(names):
            inp[nm] = jax.random.normal(ks[1 + i], (N, C), dtype=jnp.float32)
        inp['fK'] = jax.random.normal(ks[9], (4 * N, C), dtype=jnp.float32)
        inp['fV'] = jax.random.normal(ks[10], (4 * N, C), dtype=jnp.float32)
        return inp
    _L0_attn_all = _L0_attn_setup()
    _L0_attn_in = {k: v for k, v in _L0_attn_all.items() if k in ('qK', 'qV', 'kK', 'kV', 'vK', 'vV', 'pK', 'pV', 'fK', 'fV')}
    del _L0_attn_all

    def _L0_ffn_setup():
        import jax, jax.numpy as jnp
        import numpy as np
        TOP_K = 2
        key = jax.random.key(seed)
        k1, k2, k3, k4 = jax.random.split(key, 4)
        B, T, D, H, E = (2, 1024, 512, 1024, 8)
        x = jax.random.normal(k1, (B, T, D), dtype=jnp.float32)
        w12 = jax.random.normal(k2, (E, 2 * H, D), dtype=jnp.float32) * D ** (-0.5)
        w3 = jax.random.normal(k3, (E, D, H), dtype=jnp.float32) * H ** (-0.5)
        gate_w = jax.random.normal(k4, (E, D), dtype=jnp.float32) * D ** (-0.5)
        return {'x': x, 'w12': w12, 'w3': w3, 'gate_w': gate_w}
    _L0_ffn_all = _L0_ffn_setup()
    _L0_ffn_in = {k: v for k, v in _L0_ffn_all.items() if k in ('w12', 'w3', 'gate_w')}
    del _L0_ffn_all
    return {'x': x, 'ctx_1024': ctx_1024, 'L0_xattn_wi': _L0_xattn_in['wi'], 'L0_xattn_Wo': _L0_xattn_in['Wo'], 'L0_xattn_bo': _L0_xattn_in['bo'], 'L0_attn_qK': _L0_attn_in['qK'], 'L0_attn_qV': _L0_attn_in['qV'], 'L0_attn_kK': _L0_attn_in['kK'], 'L0_attn_kV': _L0_attn_in['kV'], 'L0_attn_vK': _L0_attn_in['vK'], 'L0_attn_vV': _L0_attn_in['vV'], 'L0_attn_pK': _L0_attn_in['pK'], 'L0_attn_pV': _L0_attn_in['pV'], 'L0_attn_fK': _L0_attn_in['fK'], 'L0_attn_fV': _L0_attn_in['fV'], 'L0_ffn_w12': _L0_ffn_in['w12'], 'L0_ffn_w3': _L0_ffn_in['w3'], 'L0_ffn_gate_w': _L0_ffn_in['gate_w']}

def reference(x, ctx_1024, L0_xattn_wi, L0_xattn_Wo, L0_xattn_bo, L0_attn_qK, L0_attn_qV, L0_attn_kK, L0_attn_kV, L0_attn_vK, L0_attn_vV, L0_attn_pK, L0_attn_pV, L0_attn_fK, L0_attn_fV, L0_ffn_w12, L0_ffn_w3, L0_ffn_gate_w):
    import jax
    import jax.numpy as jnp

    def _L0_xattn_ref(v, k, q, wi, Wo, bo):
        import jax, jax.numpy as jnp
        import numpy as np
        N_HEADS = 16
        D_MODEL = 512
        D_HEAD = 64
        B, S = (4, 1024)
        qp = q @ wi
        kp = k @ wi
        vp = v @ wi
        scores = jnp.einsum('bsd,btd->bst', qp, kp) / jnp.sqrt(jnp.asarray(D_HEAD, qp.dtype))
        attn = jax.nn.softmax(scores, axis=-1)
        head = qp + jnp.einsum('bst,btd->bsd', attn, vp)
        concat = jnp.tile(head, (1, 1, N_HEADS))
        return concat @ Wo + bo

    def _L0_attn_ref(x, qK, qV, kK, kV, vK, vV, pK, pV, fK, fV):
        import jax, jax.numpy as jnp
        import numpy as np
        EMB = 512
        HEADS = 16
        EPS = 1e-05

        def layer_norm(x):
            mu = jnp.mean(x, axis=-1, keepdims=True)
            var = jnp.var(x, axis=-1, keepdims=True)
            return (x - mu) / jnp.sqrt(var + EPS)

        def pattention(x, K, V):
            scale = EMB ** (-0.5)
            a = jax.nn.softmax(scale * jnp.einsum('btc,nc->btn', x, K), axis=-1)
            return jnp.einsum('btn,nc->btc', a, V)

        def causal_sdpa(q, k, v):
            T = q.shape[2]
            d = q.shape[-1]
            scores = jnp.einsum('bhqd,bhkd->bhqk', q, k) / jnp.sqrt(jnp.asarray(d, q.dtype))
            mask = jnp.tril(jnp.ones((T, T), dtype=bool))
            scores = jnp.where(mask, scores, jnp.asarray(-jnp.inf, q.dtype))
            attn = jax.nn.softmax(scores, axis=-1)
            return jnp.einsum('bhqk,bhkd->bhqd', attn, v)
        B, T, C = x.shape
        H = HEADS
        D = C // H
        x_in = x
        h = layer_norm(x)
        k = pattention(h, kK, kV)
        q = pattention(h, qK, qV)
        v = pattention(h, vK, vV)
        to_heads = lambda t: t.reshape(B, T, H, D).transpose(0, 2, 1, 3)
        o = causal_sdpa(to_heads(q), to_heads(k), to_heads(v))
        o = o.transpose(0, 2, 1, 3).reshape(B, T, C)
        o = pattention(o, pK, pV)
        x = o + x_in
        x_inter = x
        x = pattention(layer_norm(x), fK, fV)
        return x + x_inter

    def _L0_ffn_ref(x, w12, w3, gate_w):
        import jax, jax.numpy as jnp
        import numpy as np
        TOP_K = 2
        E = gate_w.shape[0]
        H = w3.shape[-1]
        scores = jnp.einsum('btd,ed->bte', x, gate_w)
        topk_scores, topk_idx = jax.lax.top_k(scores, TOP_K)
        topk_probs = jax.nn.softmax(topk_scores, axis=-1)
        total_probs = jnp.sum(jax.nn.one_hot(topk_idx, E, dtype=topk_probs.dtype) * topk_probs[..., None], axis=-2)
        h12 = jnp.einsum('btd,ehd->bteh', x, w12)
        h1, h2 = (h12[..., :H], h12[..., H:])
        hidden = jax.nn.silu(h1) * h2
        expert_out = jnp.einsum('bteh,edh->bted', hidden, w3)
        y = jnp.sum(total_probs[..., None] * expert_out, axis=-2)
        return y
    x = x + _L0_xattn_ref(ctx_1024, ctx_1024, _layernorm(x, axis=-1), L0_xattn_wi, L0_xattn_Wo, L0_xattn_bo)
    x = x + _L0_attn_ref(_layernorm(x, axis=-1), L0_attn_qK, L0_attn_qV, L0_attn_kK, L0_attn_kV, L0_attn_vK, L0_attn_vV, L0_attn_pK, L0_attn_pV, L0_attn_fK, L0_attn_fV)
    x = x + _L0_ffn_ref(_layernorm(x, axis=-1), L0_ffn_w12, L0_ffn_w3, L0_ffn_gate_w)
    return x

_drawn_inputs = setup_inputs


def setup_inputs(seed=0):
    import zlib

    import numpy as np

    out = dict(_drawn_inputs(seed))
    spreads = {'L0_xattn_bo': (0.0, 0.1)}
    factors = {'L0_attn_qK': 8.0,
     'L0_attn_qV': 8.0,
     'L0_attn_kK': 8.0,
     'L0_attn_kV': 8.0,
     'L0_attn_vK': 8.0,
     'L0_attn_vV': 8.0,
     'L0_attn_pK': 8.0,
     'L0_attn_fK': 3.675,
     'L0_attn_fV': 2.734}
    for name, (base, spread) in spreads.items():
        noise = np.random.default_rng([zlib.crc32(name.encode()), seed]).standard_normal(out[name].shape)
        drawn = base * np.exp(spread * noise) if base else spread * noise
        out[name] = jnp.asarray(drawn.astype(out[name].dtype))
    for name, factor in factors.items():
        out[name] = (out[name] * factor).astype(out[name].dtype)
    return out
```

```python
from contextlib import ExitStack

import concourse.bass as bass
from concourse import mybir

F32 = mybir.dt.float32
F32R = mybir.dt.float32r
ALU = mybir.AluOpType
ACT = mybir.ActivationFunctionType
AX = mybir.AxisListType

P = 128
EPS = 1e-5
BIG = 3.0e38


def perceiver_layer(nc, x, ctxT, wi, Wo, bo, qKT, qV, kKT, kV, vKT, vV, pKT, pV, fKT, fV, w12T, w3T, gateT, out):
    T, C = x.shape
    S = ctxT.shape[1]
    DH = wi.shape[1]
    N = qV.shape[0]
    NF = fV.shape[0]
    E, _, H2 = w12T.shape
    H = H2 // 2
    ST = T // P
    KC = C // P
    NT = N // P
    NFT = NF // P
    HT = H // P
    XHEADS = Wo.shape[0] // DH
    HEADS = 16
    D = C // HEADS
    HPC = P // D
    HALF = 512
    STEP = 2 * HALF
    STEPS = S // STEP
    HALF0 = (S - STEPS * STEP) // 2
    LAST = STEPS
    assert HALF0 == 256 and STEPS % 2 == 0 and ST == 2 and KC == 4 and 2 * DH == P
    PSCALE = float(C) ** -0.5
    HSCALE = float(D) ** -0.5
    XSCALE = float(DH) ** -0.5

    with ExitStack() as ctx:
        def sb(name, shape, dt=F32):
            return ctx.enter_context(nc.sbuf_tensor(name, shape, dt))

        def sem(name):
            return ctx.enter_context(nc.semaphore(name))

        bank = [ctx.enter_context(nc.psum_tensor(f"bank{i}", [P, 512], F32))[:] for i in range(4)]
        score_banks = ctx.enter_context(nc.psum_tensor("score_banks", [P, 4, 512], F32))
        kp_bank, turn_bank, of_bank = bank[0], bank[1:3], bank[3]

        w_attn = sb("w_attn", [P, 8, 2048])
        w_ff = sb("w_ff", [P, 2, 8192])
        ctx_buf = sb("ctx_buf", [P, 2, KC, STEP])
        probs = sb("probs", [P, ST, STEP])
        probsT = sb("probsT", [P, 4, 512])
        kv = sb("kv", [P, 2, HALF])
        k_full = kv[:, 0, :]
        k_split = sb("k_split", [P, 2, HALF], F32R)
        v_rows = kv[:, 1, :].rearrange("p (g c) -> p g c", c=P)
        q_hi = sb("q_hi", [P, T], F32R)
        q_lo = sb("q_lo", [P, T], F32R)
        q_full = sb("q_full", [P, T])
        o_acc = sb("o_acc", [P, T])
        wi_sb = sb("wi_sb", [P, KC, DH])
        xres = sb("xres", [P, ST, C])
        hln = sb("hln", [P, ST, C])
        hT = sb("hT", [P, KC, T])
        ident = sb("ident", [P, P])
        ones = sb("ones", [P, P])
        fold = sb("fold", [P, P])
        causal = sb("causal", [P, 2, P])
        diag = sb("diag", [P, ST, P])
        gate_sb = sb("gate_sb", [P, KC, E])
        h0 = kv[:]
        small = sb("small", [P, 512])
        small_used = [0]

        def tiny(n):
            a = small_used[0]
            small_used[0] += n
            assert small_used[0] <= 512
            return small[:, a:a + n]

        stats = [tiny(6) for _ in range(ST)]
        mv = tiny(2 * ST).rearrange("p (s c) -> p s c", c=2)
        std = tiny(ST)
        rstd = tiny(ST)
        eps_col = tiny(1)
        neg_chunk = tiny(ST)
        neg_max = [tiny(ST), tiny(ST)]
        neg_delta = tiny(ST)
        fade = tiny(ST)
        row_sum = tiny(ST)
        denom = tiny(ST)
        rdenom = tiny(ST)
        p_max, p_bias, p_sum, p_rsum = {}, {}, {}, {}
        for m in "kqvpf":
            p_max[m], p_bias[m], p_sum[m], p_rsum[m] = tiny(ST), tiny(ST), tiny(ST), tiny(ST)
        h_max, h_bias, h_sum = (tiny(2 * 16).rearrange("p (r s c) -> p r s c", r=4, s=2) for _ in range(3))
        h_rsum = tiny(2 * 16).rearrange("p (r s c) -> p r s c", r=4, s=2)
        expert_id = tiny(E)
        logits = tiny(ST * E).rearrange("p (s e) -> p s e", s=ST)
        rest = tiny(ST * E).rearrange("p (s e) -> p s e", s=ST)
        cand = tiny(ST * E).rearrange("p (s e) -> p s e", s=ST)
        hot = [tiny(ST * E).rearrange("p (s e) -> p s e", s=ST) for _ in range(2)]
        route = tiny(ST * E).rearrange("p (s e) -> p s e", s=ST)
        top = [tiny(ST) for _ in range(2)]
        pick = tiny(ST)
        gap = tiny(ST)
        second = tiny(ST)
        both = tiny(ST)
        first = tiny(ST)

        key_sb = {m: w_attn[:, 2 * i, :].rearrange("p (k n) -> p k n", k=KC) for i, m in enumerate("kqvp")}
        val_sb = {m: w_attn[:, 2 * i + 1, :].rearrange("p (k n) -> p k n", k=NT) for i, m in enumerate("kqvp")}
        key_sb["f"] = w_ff[:, 0, :].rearrange("p (k n) -> p k n", k=KC)
        val_sb["f"] = w_ff[:, 1, :].rearrange("p (k n) -> p k n", k=NFT)
        wo_sb = w_ff[:, 0, 0:4096].rearrange("p (g n) -> p g n", n=C)
        wo_sum = w_ff[:, 0, 4096:4096 + C]
        wo_dup = w_ff[:, 0, 4096 + C:4096 + 2 * C]
        bo_row = w_ff[0:1, 0, 4096 + 2 * C:4096 + 3 * C]
        ctx_flat = ctx_buf[:].rearrange("p b k t -> p (b k t)")
        E_sb = {m: ctx_flat[:, 1024 * i:1024 * (i + 1)].rearrange("p (s n) -> p s n", s=ST) for i, m in enumerate("kqvp")}
        ET_sb = {m: ctx_flat[:, 4096 + 1024 * (i % 3):4096 + 1024 * (i % 3 + 1)].rearrange("p (n t) -> p n t", t=T)
                 for i, m in enumerate("kqvp")}

        qh = probs[:].rearrange("p s n -> p (s n)")[:, 0:1024].rearrange("p (c t) -> p c t", c=KC)
        kh = probs[:].rearrange("p s n -> p (s n)")[:, 1024:2048].rearrange("p (c t) -> p c t", c=KC)
        vh = probsT[:].rearrange("p g n -> p (g n)")[:, 0:1024].rearrange("p (s n) -> p s n", s=ST)
        o_rows = probsT[:].rearrange("p g n -> p (g n)")[:, 1024:2048].rearrange("p (s n) -> p s n", s=ST)
        hp0 = ctx_flat[:, 0:1024].rearrange("p (b c k) -> p b c k", b=2, c=KC)
        hp1 = ctx_flat[:, 1024:3072].rearrange("p (b c k) -> p b c k", b=2, c=KC)
        hpT = ctx_flat[:, 7168:8192].rearrange("p (b k) -> p b k", b=2)
        fE = ctx_flat[:, 0:4096].rearrange("p (s n) -> p s n", s=ST)
        fET = ctx_flat[:, 4096:8192].rearrange("p (s n t) -> p s n t", s=ST, t=P)
        hid = ctx_flat[:, 0:2048].rearrange("p (j t) -> p j t", t=T)
        sil = ctx_flat[:, 2048:3072].rearrange("p (b t) -> p b t", t=T)

        f_part = tiny(ST * 4).rearrange("p (s n) -> p s n", s=ST)
        f_max = tiny(ST * 4).rearrange("p (s n) -> p s n", s=ST)

        x_in, wi_in, wo_in, bo_in, gate_in = (sem(n) for n in ("x_in", "wi_in", "wo_in", "bo_in", "gate_in"))
        ctx_in = [sem("ctx_in_even"), sem("ctx_in_odd")]
        key_in = {m: sem(f"key_in_{m}") for m in "kqvpf"}
        val_in = {m: sem(f"val_in_{m}") for m in "kqvpf"}
        w12_in = [sem("w12_in_even"), sem("w12_in_odd")]
        w3_in = [sem("w3_in_even"), sem("w3_in_odd")]
        out_done = sem("out_done")
        memset_done, ident_done, ones_done, fold_done, causal_done, ids_done = (
            sem(n) for n in ("memset_done", "ident_done", "ones_done", "fold_done", "causal_done", "ids_done"))
        kp_done, k_hi_done, k_lo_done, k_full_done = (sem(n) for n in ("kp_done", "k_hi_done", "k_lo_done", "k_full_done"))
        scores_ready, chunk_max, max_ready, delta_ready = (sem(n) for n in ("scores_ready", "chunk_max", "max_ready", "delta_ready"))
        probs_ready, fade_ready, diag_ready = sem("probs_ready"), sem("fade_ready"), sem("diag_ready")
        denom_scaled, denom_done = sem("denom_scaled"), sem("denom_done")
        turned, turn_out_act, turn_out_dve = sem("turned"), sem("turn_out_act"), sem("turn_out_dve")
        o_ready, o_faded, o_added = sem("o_ready"), sem("o_faded"), sem("o_added")
        events = {}

        def ev(name):
            if name not in events:
                events[name] = sem(name)
            return events[name]

        def nth(m, st):
            return ST * "kqvp".index(m) + st + 1

        NORMS = ["x", "x1", "h", "f", "e"]
        TURNS = ["xT", "hT", "oT", "fT", "eT"]

        h12_ready, silu_ready, hid_ready = sem("h12_ready"), sem("silu_ready"), sem("hid_ready")
        y_ready = sem("y_ready")

        block = ctx.enter_context(nc.Block())

        ctx_cols = ctxT.rearrange("(k p) t -> p k t", p=P)

        def expert_w(b):
            flat = (w_attn[:].rearrange("p a n -> p (a n)") if b == 0 else w_ff[:].rearrange("p a n -> p (a n)"))
            return (flat[:, 0:KC * H2].rearrange("p (k n) -> p k n", k=KC),
                    flat[:, KC * H2:KC * H2 + HT * C].rearrange("p (k n) -> p k n", k=HT))

        @block.sync
        def _(sp):
            sp.dma_start(wi_sb[:], wi.rearrange("(k p) d -> p k d", p=P)).then_inc(wi_in, 16)
            sp.dma_start(ctx_buf[:, 0, :, 0:2 * HALF0], ctx_cols[:, :, 0:2 * HALF0]).then_inc(ctx_in[0], 16)
            sp.dma_start(xres[:], x.rearrange("(s p) c -> p s c", p=P)).then_inc(x_in, 16)

            def load_step(s, b):
                if not isinstance(s, int) or s >= 2:
                    sp.wait_ge(kp_done, s - 1)
                sp.dma_start(ctx_buf[:, b], ctx_cols[:, :, bass.ds(2 * HALF0 + (s - 1) * STEP, STEP)]).then_inc(ctx_in[b], 16)

            load_step(1, 1)
            sp.dma_start(wo_sb, Wo.rearrange("(g p) n -> p g n", p=P)).then_inc(wo_in, 16)
            sp.dma_start(bo_row[:], bo.rearrange("(a n) -> a n", a=1)).then_inc(bo_in, 16)
            sp.dma_start(gate_sb[:], gateT.rearrange("(k p) e -> p k e", p=P)).then_inc(gate_in, 16)
            load_step(2, 0)
            with sp.Fori(3, LAST, 2) as s:
                load_step(s, 1)
                load_step(s + 1, 0)

            def load_expert(e, b):
                dst = expert_w(b)
                sp.dma_start(dst[0], w12T[bass.ds(e, 1), :, :].rearrange("a (k p) n -> p (a k) n", p=P)).then_inc(w12_in[b], 16)
                sp.dma_start(dst[1], w3T[bass.ds(e, 1), :, :].rearrange("a (k p) n -> p (a k) n", p=P)).then_inc(w3_in[b], 16)

            sp.wait_ge(ev("p_out_ready"), 2)
            load_expert(0, 0)
            sp.wait_ge(ev("f_out_ready"), 2)
            load_expert(1, 1)
            with sp.Fori(2, E - 1, 2) as e:
                sp.wait_ge(y_ready, e - 1)
                load_expert(e, 0)
                sp.wait_ge(y_ready, e)
                load_expert(e + 1, 1)
            for st in range(ST):
                sp.wait_ge(ev("x_added"), ST * (E - 1) + st + 1)
                sp.dma_start(out[st * P:(st + 1) * P, :], xres[:, st, :]).then_inc(out_done, 16)
            sp.wait_ge(out_done, 16 * ST)

        @block.gpsimd
        def _(pool):
            pool.memset(ident[:], 0.0).then_inc(memset_done, 1)
            pool.memset(fold[:], 0.0).then_inc(memset_done, 1)
            pool.memset(causal[:], 0.0).then_inc(memset_done, 1)
            pool.memset(ones[:], 1.0).then_inc(ones_done, 1)
            pool.memset(eps_col, EPS).then_inc(ones_done, 1)
            pool.wait_ge(memset_done, 3)
            pool.affine_select(out=ident[:], in_=ident[:], compare_op=ALU.not_equal, fill=1.0, base=0,
                               pattern=[[-1, P]], channel_multiplier=1).then_inc(ident_done, 1)
            for n, off in enumerate((0, DH, -DH)):
                if n:
                    pool.wait_ge(fold_done, n)
                pool.affine_select(out=fold[:], in_=fold[:], compare_op=ALU.not_equal, fill=1.0, base=off,
                                   pattern=[[-1, P]], channel_multiplier=1).then_inc(fold_done, 1)
            pool.affine_select(out=causal[:, 1, :], in_=causal[:, 1, :], compare_op=ALU.is_ge, fill=-1.0e30, base=0,
                               pattern=[[-1, P]], channel_multiplier=1).then_inc(causal_done, 1)
            for e in range(E):
                pool.memset(expert_id[:, e:e + 1], float(e)).then_inc(ids_done, 1)

            loads = [(d, dst, src) for m, kt, v in (("k", kKT, kV), ("q", qKT, qV), ("v", vKT, vV))
                     for d, dst, src in ((key_in[m], key_sb[m], kt), (val_in[m], val_sb[m], v))]
            for arrived, dst, src in loads:
                pool.dma_start(dst, src.rearrange("(k p) n -> p k n", p=P)).then_inc(arrived, 16)
            pool.wait_ge(ev("xattn_ready"), 2)
            for arrived, dst, src in ((key_in["p"], key_sb["p"], pKT), (val_in["p"], val_sb["p"], pV),
                                      (key_in["f"], key_sb["f"], fKT), (val_in["f"], val_sb["f"], fV)):
                pool.dma_start(dst, src.rearrange("(k p) n -> p k n", p=P)).then_inc(arrived, 16)

        @block.tensor
        def _(pe):
            def kp(s, b, half):
                for k in range(KC):
                    for h in range(2):
                        last = pe.matmul(kp_bank[DH * h:DH * (h + 1), 0:half], wi_sb[:, k, :],
                                         ctx_buf[:, b, k, h * half:(h + 1) * half], start=(k == 0), stop=(k == KC - 1))
                last.then_inc(kp_done, 1)

            def scores(s, half):
                pe.wait_ge(k_hi_done, 2 * s + 2)
                pe.wait_ge(k_lo_done, 2 * s + 2)
                for st in range(ST):
                    for h in range(2):
                        o = score_banks[:, 2 * st + h, 0:half]
                        pe.matmul(o, q_hi[:, st * P:(st + 1) * P], k_split[:, h, 0:half], start=True, stop=False)
                        last = pe.matmul(o, q_lo[:, st * P:(st + 1) * P], k_split[:, h, 0:half], start=False, stop=True)
                    last.then_inc(scores_ready, 1)

            def turn(slot, blocks):
                for c, block_in in enumerate(blocks):
                    last = pe.transpose(turn_bank[slot][:, c * P:(c + 1) * P], block_in, ident[:])
                last.then_inc(turned, 1)

            def step(s, b, first=False, next_half=HALF):
                half = HALF0 if first else HALF
                nt = half // P
                slot = 0 if first else b
                if first:
                    pe.wait_ge(ev("q_high"), 1)
                    pe.wait_ge(ev("q_split"), 2)
                else:
                    pe.wait_ge(probs_ready, 2 * s)
                scores(s, half)
                pe.wait_ge(k_full_done, s + 1)
                if not first:
                    pe.wait_ge(turn_out_dve, 2 * s - 1)
                turn(slot, [k_full[:, j * P:(j + 1) * P] for j in range(nt)])
                if next_half:
                    pe.wait_ge(ctx_in[1 - b], 8 * (s + 1) + (8 if b == 0 else 16))
                    kp(s + 1, 1 - b, next_half)
                pe.wait_ge(probs_ready, 2 * s + 2)

                def turn_probs(g):
                    if first:
                        if g == 1:
                            pe.wait_ge(turn_out_act, 1)
                    elif g == 0:
                        pe.wait_ge(turn_out_act, 3 * s - 1)
                    elif g == 2:
                        pe.wait_ge(turn_out_dve, 2 * s)
                    else:
                        pe.wait_ge(turn_out_act, 3 * s + (g - 1) // 2)
                    turn((slot + 1 + g) % 2, [probs[:, st, h * half + g * P:h * half + (g + 1) * P]
                                              for h in range(2) for st in range(ST)])

                def spread_fade():
                    pe.wait_ge(diag_ready, 2 * s)
                    pe.matmul(of_bank[:, T:2 * T], ones[:], diag[:].rearrange("p s q -> p (s q)"), start=True,
                              stop=True).then_inc(o_ready, 1)

                def pv(g):
                    if g == 0 and not first:
                        pe.wait_ge(o_added, s)
                    if first:
                        if g == 0:
                            pe.wait_ge(turn_out_dve, 1)
                            pe.wait_ge(turn_out_act, 1)
                        else:
                            pe.wait_ge(turn_out_act, 2)
                    elif g % 2 == 0:
                        pe.wait_ge(turn_out_dve, 2 * s + g // 2)
                        if g == 0:
                            pe.wait_ge(turn_out_act, 3 * s)
                    else:
                        pe.wait_ge(turn_out_act, 3 * s + 1 + g // 2)
                    for h in range(2):
                        last = pe.matmul(of_bank[DH * h:DH * (h + 1), 0:T], v_rows[:, g, DH * h:DH * (h + 1)],
                                         probsT[:, g, h * T:(h + 1) * T], start=(g == 0), stop=(g == nt - 1))
                    if first and g == nt - 1:
                        last.then_inc(o_ready, 1)

                turn_probs(0)
                turn_probs(1)
                pv(0)
                for g in range(2, nt):
                    turn_probs(g)
                    pv(g - 1)
                pv(nt - 1)
                if not first:
                    spread_fade()

            def turn_rows(src, banks):
                for k in range(KC):
                    for st in range(ST):
                        last = pe.transpose(banks[k // 2][:, (k % 2) * T + st * P:(k % 2) * T + (st + 1) * P],
                                            src[:, st, k * P:(k + 1) * P], ident[:])
                last.then_inc(ev("rows_turned"), 1)

            SB = [score_banks[:, i, :] for i in range(4)]
            pe.wait_ge(wi_in, 16)
            pe.wait_ge(ctx_in[0], 16)
            kp(0, 0, HALF0)
            pe.wait_ge(ident_done, 1)
            pe.wait_ge(ev("ln_done"), ST * (NORMS.index("x") + 1))
            turn_rows(hln, SB)
            pe.wait_ge(ev("hT_done"), 2 * (TURNS.index("xT") + 1))
            for k in range(KC):
                for h in range(2):
                    last = pe.matmul(turn_bank[0][DH * h:DH * (h + 1), 0:T], wi_sb[:, k, :], hT[:, k, :],
                                     start=(k == 0), stop=(k == KC - 1))
            last.then_inc(ev("q_ready"), 1)
            step(0, 0, first=True)
            with pe.Fori(1, LAST - 1, 2) as s:
                step(s, 1)
                step(s + 1, 0)
            step(LAST - 1, 1)
            step(LAST, 0, next_half=0)

            pe.wait_ge(ev("wo_summed"), 1)
            pe.wait_ge(fold_done, 3)
            pe.matmul(kp_bank[:], fold[:], wo_sum, start=True, stop=True).then_inc(ev("wo_folded"), 1)
            pe.wait_ge(ev("wo_dup_ready"), 1)
            pe.wait_ge(bo_in, 16)
            pe.wait_ge(ones_done, 2)
            for st in range(ST):
                pe.matmul(SB[2 + st], ones[0:1, :], bo_row[:], start=True, stop=False)
                pe.matmul(SB[2 + st], q_full[0:DH, st * P:(st + 1) * P], wo_dup[0:DH, :], start=False, stop=True)
            pe.wait_ge(o_added, LAST + 1)
            for st in range(ST):
                pe.matmul(SB[st], o_acc[:, st * P:(st + 1) * P], wo_dup[:], start=True, stop=True).then_inc(ev("xattn_ready"), 1)

            def key_scores(m, st, bk, n0=0):
                for k in range(KC):
                    last = pe.matmul(bk, hT[:, k, st * P:(st + 1) * P], key_sb[m][:, k, n0:n0 + 512],
                                     start=(k == 0), stop=(k == KC - 1))
                return last

            def turn_key_probs(m, st, bk):
                for n in range(NT):
                    last = pe.transpose(bk[:, n * P:(n + 1) * P], E_sb[m][:, st, n * P:(n + 1) * P], ident[:])
                last.then_inc(ev("key_turned"), 1)

            T6, T7 = bank[2], bank[3]
            B = SB + [bank[0], bank[1]]
            pe.wait_ge(ev("ln_done"), ST * (NORMS.index("h") + 1))
            turn_rows(hln, [T6, T7])
            pe.wait_ge(ev("hT_done"), 2 * (TURNS.index("hT") + 1))

            def scores_of(m, st):
                if st == 0:
                    pe.wait_ge(key_in[m], 16)
                i = 2 * "kqv".index(m) + st
                key_scores(m, st, B[i]).then_inc(ev("key_scores"), 1)

            def turns_of(m, st, free=None):
                pe.wait_ge(ev("key_normed"), nth(m, st))
                if free:
                    pe.wait_ge(ev("key_probsT"), free)
                turn_key_probs(m, st, (T6, T7)[st])

            def features_out(m, banks):
                pe.wait_ge(val_in[m], 16)
                for st in range(ST):
                    pe.wait_ge(ev("key_probsT"), nth(m, st))
                for c in range(KC):
                    for n in range(NT):
                        last = pe.matmul(banks[c // 2][:, (c % 2) * T:(c % 2 + 1) * T], val_sb[m][:, n, c * P:(c + 1) * P],
                                         ET_sb[m][:, n, :], start=(n == 0), stop=(n == NT - 1))
                last.then_inc(ev(f"{m}_out_ready"), 1)

            scores_of("k", 0)
            scores_of("k", 1)
            scores_of("q", 0)
            turns_of("k", 0)
            scores_of("q", 1)
            turns_of("k", 1)
            scores_of("v", 0)
            turns_of("q", 0, nth("k", 0))
            scores_of("v", 1)
            turns_of("q", 1, nth("k", 1))
            features_out("k", B[0:2])
            turns_of("v", 0, nth("q", 0))
            turns_of("v", 1, nth("q", 1))
            features_out("q", B[2:4])
            pe.wait_ge(val_in["v"], 16)
            for st in range(ST):
                pe.wait_ge(ev("key_probsT"), nth("v", st))
                for n in range(NT):
                    last = pe.matmul(B[4 + st], ET_sb["v"][:, n, st * P:(st + 1) * P], val_sb["v"][:, n, :],
                                     start=(n == 0), stop=(n == NT - 1))
                last.then_inc(ev("v_out_ready"), 1)

            def head_scores(r):
                rows = slice(D * r, D * (r + 1))
                if r == 0:
                    pe.wait_ge(ev("kh_done"), 2)
                    pe.wait_ge(ev("qh_done"), 2)
                else:
                    pe.wait_ge(ev("head_masked"), 3 * r)
                for c in range(KC):
                    last = pe.matmul(B[0][:, c * P:(c + 1) * P], qh[rows, c, 0:P], kh[rows, c, 0:P], start=True, stop=True)
                last.then_inc(ev("head_scores"), 1)
                for c in range(KC):
                    last = pe.matmul(B[1 + c // 2][:, (c % 2) * T:(c % 2 + 1) * T], qh[rows, c, P:T], kh[rows, c, :],
                                     start=True, stop=True)
                    if c % 2:
                        last.then_inc(ev("head_scores"), 1)

            def head_turn(i):
                r, c = i // KC, i % KC
                if c == 0:
                    pe.wait_ge(ev("head_probs"), 2 * KC * (r + 1))
                if i >= 2:
                    pe.wait_ge(ev("head_turn_out"), i - 1)
                bk = (T6, T7)[i % 2]
                pe.transpose(bk[:, 0:P], hp0[:, r % 2, c, :], ident[:])
                pe.transpose(bk[:, P:2 * P], hp1[:, r % 2, c, 0:P], ident[:])
                pe.transpose(bk[:, 2 * P:3 * P], hp1[:, r % 2, c, P:2 * P], ident[:]).then_inc(ev("head_turned"), 1)

            def head_out(i):
                r, c = i // KC, i % KC
                pe.wait_ge(ev("head_turn_out"), i + 1)
                if i == 0:
                    pe.wait_ge(ev("vh_done"), 2)
                if c == 0 and r >= 2:
                    pe.wait_ge(ev("o_rows_done"), r - 1)
                ob = B[4 + r % 2][:, 0:2 * P].rearrange("p (s c d) -> p s c d", s=2, c=KC)
                vcol = slice((HPC * c + r) * D, (HPC * c + r + 1) * D)
                pe.matmul(ob[:, 0, c, :], hpT[:, i % 2, 0:P], vh[:, 0, vcol], start=True, stop=True)
                pe.matmul(ob[:, 1, c, :], hpT[:, i % 2, P:2 * P], vh[:, 0, vcol], start=True, stop=False)
                last = pe.matmul(ob[:, 1, c, :], hpT[:, i % 2, 2 * P:3 * P], vh[:, 1, vcol], start=False, stop=True)
                if c == KC - 1:
                    last.then_inc(ev("head_out_ready"), 1)

            head_scores(0)
            for r in range(HPC):
                if r + 1 < HPC:
                    head_scores(r + 1)
                for c in range(KC):
                    i = KC * r + c
                    head_turn(i)
                    if i:
                        head_out(i - 1)
            head_out(HPC * KC - 1)

            pe.wait_ge(ev("o_rows_done"), HPC)
            turn_rows(o_rows, [T6, T7])
            pe.wait_ge(ev("hT_done"), 2 * (TURNS.index("oT") + 1))
            pe.wait_ge(key_in["p"], 16)
            for st in range(ST):
                key_scores("p", st, B[st]).then_inc(ev("key_scores"), 1)
            for st in range(ST):
                turns_of("p", st)
            pe.wait_ge(val_in["p"], 16)
            for st in range(ST):
                pe.wait_ge(ev("key_probsT"), nth("p", st))
                for n in range(NT):
                    last = pe.matmul(B[2 + st], ET_sb["p"][:, n, st * P:(st + 1) * P], val_sb["p"][:, n, :],
                                     start=(n == 0), stop=(n == NT - 1))
                last.then_inc(ev("p_out_ready"), 1)

            pe.wait_ge(ev("ln_done"), ST * (NORMS.index("f") + 1))
            turn_rows(hln, [T6, T7])
            pe.wait_ge(ev("hT_done"), 2 * (TURNS.index("fT") + 1))
            pe.wait_ge(key_in["f"], 16)
            FB = [SB, bank]
            for st in range(ST):
                for n4 in range(4):
                    key_scores("f", st, FB[st][n4][:] if st else FB[st][n4], 512 * n4).then_inc(ev("f_scores"), 1)
            for st in range(ST):
                pe.wait_ge(ev("f_normed"), st + 1)
                for n in range(NFT):
                    last = pe.transpose(FB[st][n // 4][:, (n % 4) * P:(n % 4 + 1) * P], fE[:, st, n * P:(n + 1) * P], ident[:])
                    if n % 4 == 3:
                        last.then_inc(ev("f_turned"), 1)
            pe.wait_ge(val_in["f"], 16)
            for st in range(ST):
                for n in range(NFT):
                    if n % 4 == 0:
                        pe.wait_ge(ev("f_probsT"), 4 * st + n // 4 + 1)
                    last = pe.matmul(FB[0][st], fET[:, st, n, :], val_sb["f"][:, n, :], start=(n == 0), stop=(n == NFT - 1))
                last.then_inc(ev("f_out_ready"), 1)

            pe.wait_ge(ev("ln_done"), ST * (NORMS.index("e") + 1))
            turn_rows(hln, [T6, T7])
            pe.wait_ge(ev("hT_done"), 2 * (TURNS.index("eT") + 1))
            pe.wait_ge(gate_in, 16)
            for st in range(ST):
                for k in range(KC):
                    last = pe.matmul(T6[:, st * E:(st + 1) * E], hT[:, k, st * P:(st + 1) * P], gate_sb[:, k, :],
                                     start=(k == 0), stop=(k == KC - 1))
            last.then_inc(ev("logits_ready"), 1)
            pe.wait_ge(ev("logits_taken"), 1)

            def expert(e, b):
                w12, w3 = expert_w(b)
                yb = [bank[2 * b], bank[2 * b + 1]]
                pe.wait_ge(w12_in[b], 8 * e + (16 if b == 0 else 8))

                def hidden(j):
                    g = HT * e + j
                    if not isinstance(e, int) or g >= 4:
                        pe.wait_ge(hid_ready, g - 3)
                    for part in range(2):
                        for k in range(KC):
                            last = pe.matmul(SB[j % 4][:, part * T:(part + 1) * T],
                                             w12[:, k, part * H + j * P:part * H + (j + 1) * P], hT[:, k, :],
                                             start=(k == 0), stop=(k == KC - 1))
                    last.then_inc(h12_ready, 1)

                def down(j):
                    pe.wait_ge(hid_ready, HT * e + j + 1)
                    if j == 0:
                        pe.wait_ge(w3_in[b], 8 * e + (16 if b == 0 else 8))
                        if not isinstance(e, int) or e >= 2:
                            pe.wait_ge(ev("x_added"), 2 * (e - 1))
                    for st in range(ST):
                        last = pe.matmul(yb[st][:], hid[:, j, st * P:(st + 1) * P], w3[:, j, :],
                                         start=(j == 0), stop=(j == HT - 1))
                    if j == HT - 1:
                        last.then_inc(y_ready, 1)

                for j in range(HT):
                    hidden(j)
                    if j:
                        down(j - 1)
                down(HT - 1)

            expert(0, 0)
            expert(1, 1)
            with pe.Fori(2, E - 1, 2) as e:
                expert(e, 0)
                expert(e + 1, 1)

        @block.scalar
        def _(act):
            def k_high(s, half):
                for h in range(2):
                    rows = slice(DH * h, DH * (h + 1))
                    act.activation(k_split[rows, h, 0:half], kp_bank[rows, 0:half], ACT.Copy).then_inc(k_hi_done, 1)

            def k_copy(half):
                act.activation(k_full[:, 0:half], kp_bank[:, 0:half], ACT.Copy).then_inc(k_full_done, 1)

            def turn_out(slot, dst, n):
                act.activation(dst, turn_bank[slot][:, 0:n], ACT.Copy).then_inc(turn_out_act, 1)

            def step(s, b, first=False, next_half=HALF):
                half = HALF0 if first else HALF
                nt = half // P
                slot = 0 if first else b
                u = 0 if first else 5 * s - 2
                act.wait_ge(turned, u + 1)
                turn_out(slot, v_rows[:, 0:nt, :].rearrange("p g c -> p (g c)"), nt * P)
                act.wait_ge(max_ready, s + 1)
                if not first:
                    act.wait_ge(denom_done, s)
                for st in range(ST):
                    act.activation(probs[:, st, 0:2 * half].rearrange("p (h n) -> p h n", h=2),
                                   score_banks[:, 2 * st:2 * st + 2, 0:half], ACT.Exp, bias=neg_max[b][:, st:st + 1],
                                   accum_out=row_sum[:, st:st + 1]).then_inc(probs_ready, 1)
                if not first:
                    act.wait_ge(delta_ready, s)
                    act.activation(fade, neg_delta, ACT.Exp).then_inc(fade_ready, 1)
                if next_half:
                    act.wait_ge(kp_done, s + 2)
                    k_copy(next_half)
                    k_high(s + 1, next_half)
                act.wait_ge(turned, u + 3)
                turn_out(slot, probsT[:, 1, :], 512)
                if nt == 4:
                    act.wait_ge(turned, u + 5)
                    turn_out(slot, probsT[:, 3, :], 512)

            def layer_norm_std(name):
                act.wait_ge(ev("ln_var"), ST * (NORMS.index(name) + 1))
                act.activation(std, mv[:, :, 1], ACT.Sqrt, bias=eps_col).then_inc(ev("ln_std"), 1)

            def hT_out(name, src):
                act.wait_ge(ev("rows_turned"), TURNS.index(name) + 1)
                act.activation(hT[:, 0:2, :].rearrange("p k t -> p (k t)"), src, ACT.Copy).then_inc(ev("hT_done"), 1)

            SB = [score_banks[:, i, :] for i in range(4)]
            T6, T7 = bank[2], bank[3]
            B = SB + [bank[0][:], bank[1][:]]
            act.wait_ge(ones_done, 2)
            layer_norm_std("x")
            act.wait_ge(kp_done, 1)
            k_copy(HALF0)
            k_high(0, HALF0)
            hT_out("xT", SB[0])
            act.wait_ge(ev("q_ready"), 1)
            act.activation(q_hi[:], turn_bank[0][:, 0:T], ACT.Copy, scale=XSCALE).then_inc(ev("q_high"), 1)
            act.activation(q_full[:], turn_bank[0][:, 0:T], ACT.Copy).then_inc(ev("q_split"), 1)
            step(0, 0, first=True)
            with act.Fori(1, LAST - 1, 2) as s:
                step(s, 1)
                step(s + 1, 0)
            step(LAST - 1, 1)
            step(LAST, 0, next_half=0)

            layer_norm_std("x1")
            layer_norm_std("h")
            hT_out("hT", T6[:])

            def soft_exp(m, st, src):
                act.wait_ge(ev("key_bias"), nth(m, st))
                act.activation(E_sb[m][:, st, :], src, ACT.Exp, bias=p_bias[m][:, st:st + 1], scale=PSCALE,
                               accum_out=p_sum[m][:, st:st + 1]).then_inc(ev("key_exp"), 1)

            def probsT_out(m, st):
                act.wait_ge(ev("key_turned"), nth(m, st))
                act.activation(ET_sb[m][:, :, st * P:(st + 1) * P], (T6, T7)[st][:].rearrange("p (n t) -> p n t", n=NT),
                               ACT.Copy).then_inc(ev("key_probsT"), 1)

            soft_exp("k", 0, B[0])
            soft_exp("k", 1, B[1])
            probsT_out("k", 0)
            soft_exp("q", 0, B[2])
            probsT_out("k", 1)
            soft_exp("q", 1, B[3])
            probsT_out("q", 0)
            soft_exp("v", 0, B[4])
            probsT_out("q", 1)
            soft_exp("v", 1, B[5])
            act.wait_ge(ev("k_out_ready"), 1)
            act.activation(kh[:, 0:2, :].rearrange("p c t -> p (c t)"), B[0], ACT.Copy).then_inc(ev("kh_done"), 1)
            probsT_out("v", 0)
            probsT_out("v", 1)
            act.wait_ge(ev("q_out_ready"), 1)
            act.activation(qh[:, 0:2, :].rearrange("p c t -> p (c t)"), B[2], ACT.Copy).then_inc(ev("qh_done"), 1)
            act.wait_ge(ev("v_out_ready"), 1)
            act.activation(vh[:, 0, :], B[4], ACT.Copy).then_inc(ev("vh_done"), 1)

            def head_turn_out(i):
                act.wait_ge(ev("head_turned"), i + 1)
                if i >= 2 and i % 2 == 0:
                    pass
                act.activation(hpT[:, i % 2, 0:3 * P], (T6, T7)[i % 2][:, 0:3 * P], ACT.Copy).then_inc(ev("head_turn_out"), 1)

            def head_exp(r):
                act.wait_ge(ev("head_bias"), 2 * r + 2)
                for c in range(KC):
                    act.activation(hp0[:, r % 2, c, :], hp0[:, r % 2, c, :], ACT.Exp, bias=h_bias[:, r, 0, c:c + 1], scale=HSCALE,
                                   accum_out=h_sum[:, r, 0, c:c + 1]).then_inc(ev("head_probs"), 1)
                    act.activation(hp1[:, r % 2, c, :], hp1[:, r % 2, c, :], ACT.Exp, bias=h_bias[:, r, 1, c:c + 1], scale=HSCALE,
                                   accum_out=h_sum[:, r, 1, c:c + 1]).then_inc(ev("head_probs"), 1)

            head_exp(0)
            for r in range(HPC):
                for c in range(KC):
                    head_turn_out(KC * r + c)
                if r + 1 < HPC:
                    head_exp(r + 1)

            hT_out("oT", T6[:])
            for st in range(ST):
                soft_exp("p", st, B[st])
            for st in range(ST):
                probsT_out("p", st)
            layer_norm_std("f")
            hT_out("fT", T6[:])
            for st in range(ST):
                act.wait_ge(ev("f_bias"), st + 1)
                fb = (SB, [b[:] for b in bank])[st]
                for n4 in range(4):
                    act.activation(fE[:, st, n4 * 512:(n4 + 1) * 512], fb[n4], ACT.Exp, bias=p_bias["f"][:, st:st + 1],
                                   scale=PSCALE, accum_out=f_part[:, st, n4:n4 + 1]).then_inc(ev("f_exp"), 1)
            for st in range(ST):
                fb = (SB, [b[:] for b in bank])[st]
                for n4 in range(0, 4, 2):
                    act.wait_ge(ev("f_turned"), 4 * st + n4 + 1)
                    if n4 or st:
                        act.wait_ge(ev("f_probsT"), 4 * st + n4)
                    act.activation(fET[:, st, 4 * n4:4 * n4 + 4, :].rearrange("p n t -> p (n t)"), fb[n4], ACT.Copy).then_inc(ev("f_probsT"), 1)
            layer_norm_std("e")
            hT_out("eT", T6[:])
            act.wait_ge(ev("gap_ready"), 1)
            act.activation(second, gap, ACT.Exp).then_inc(ev("second_ready"), 1)

            def expert(e):
                for j in range(HT):
                    g = HT * e + j
                    act.wait_ge(h12_ready, g + 1)
                    if not isinstance(e, int) or g >= 4:
                        act.wait_ge(hid_ready, g - 3)
                    act.activation(sil[:, j % 4, :], SB[j % 4][:, 0:T], ACT.Silu).then_inc(silu_ready, 1)

            expert(0)
            with act.Fori(1, E, 1) as e:
                expert(e)


        @block.vector
        def _(dve):
            dve_steps = ev("dve_steps")
            count = [0]

            def then(ins):
                count[0] += 1
                ins.then_inc(dve_steps, 1)
                dve.wait_ge(dve_steps, count[0])

            def layer_norm(src, name, dst=None):
                for st in range(ST):
                    then(dve.bn_stats(stats[st], src[:, st, :]))
                for st in range(ST):
                    dve.bn_aggr(mv[:, st, :], stats[st]).then_inc(ev("ln_var"), 1)
                dve.wait_ge(ev("ln_std"), NORMS.index(name) + 1)
                then(dve.reciprocal(rstd, std))
                for st in range(ST):
                    dve.tensor_scalar((dst or hln)[:, st, :], src[:, st, :], mv[:, st, 0:1], rstd[:, st:st + 1],
                                      ALU.subtract, ALU.mult).then_inc(ev("ln_done"), 1)

            def hT_out(name, src):
                dve.wait_ge(ev("rows_turned"), TURNS.index(name) + 1)
                dve.tensor_copy(hT[:, 2:4, :].rearrange("p k t -> p (k t)"), src).then_inc(ev("hT_done"), 1)

            def k_low(h, s, half):
                rows, other = slice(DH * h, DH * (h + 1)), slice(DH * (1 - h), DH * (2 - h))
                dve.wait_ge(k_hi_done, 2 * s + h + 1)
                dve.tensor_tensor(k_split[other, h, 0:half], k_full[rows, 0:half], k_split[rows, h, 0:half].bitcast(F32),
                                  ALU.subtract).then_inc(k_lo_done, 1)

            def turn_out(slot, dst):
                dve.tensor_copy(dst, turn_bank[slot][:]).then_inc(turn_out_dve, 1)

            def step(s, b, first=False, next_half=HALF):
                half = HALF0 if first else HALF
                nt = half // P
                slot = 0 if first else b
                u = 0 if first else 5 * s - 2
                for st in range(ST):
                    dve.wait_ge(scores_ready, 2 * s + st + 1)
                    dst = neg_max[b] if first else neg_chunk
                    dve.tensor_reduce(dst[:, st:st + 1], score_banks[:, 2 * st:2 * st + 2, 0:half], AX.XY, ALU.max,
                                      negate=True).then_inc(max_ready if first and st == ST - 1 else chunk_max, 1)
                if not first:
                    dve.wait_ge(chunk_max, 2 * s + 1)
                    dve.tensor_tensor(neg_max[b], neg_max[1 - b], neg_chunk, ALU.min).then_inc(max_ready, 1)
                    dve.wait_ge(max_ready, s + 1)
                    dve.tensor_tensor(neg_delta, neg_max[b], neg_max[1 - b], ALU.subtract).then_inc(delta_ready, 1)
                dve.wait_ge(turned, u + 2)
                turn_out((slot + 1) % 2, probsT[:, 0, :])
                if next_half:
                    k_low(0, s + 1, next_half)
                if nt == 4:
                    dve.wait_ge(turned, u + 4)
                    turn_out((slot + 1) % 2, probsT[:, 2, :])
                if next_half:
                    k_low(1, s + 1, next_half)
                if first:
                    dve.wait_ge(probs_ready, ST)
                    dve.tensor_copy(denom, row_sum).then_inc(denom_done, 1)
                else:
                    dve.wait_ge(fade_ready, s)
                    for st in range(ST):
                        dve.tensor_scalar(diag[:, st, :], ident[:], fade[:, st:st + 1], None, ALU.mult).then_inc(diag_ready, 1)
                    dve.wait_ge(denom_done, s)
                    dve.tensor_tensor(denom, denom, fade, ALU.mult).then_inc(denom_scaled, 1)
                    dve.wait_ge(denom_scaled, s)
                    dve.tensor_tensor(denom, denom, row_sum, ALU.add).then_inc(denom_done, 1)
                dve.wait_ge(o_ready, s + 1)
                if first:
                    dve.tensor_copy(o_acc[:], of_bank[:, 0:T]).then_inc(o_added, 1)
                else:
                    dve.wait_ge(o_added, s)
                    dve.tensor_tensor(o_acc[:], o_acc[:], of_bank[:, T:2 * T], ALU.mult).then_inc(o_faded, 1)
                    dve.wait_ge(o_faded, s)
                    dve.tensor_tensor(o_acc[:], o_acc[:], of_bank[:, 0:T], ALU.add).then_inc(o_added, 1)

            SB = [score_banks[:, i, :] for i in range(4)]
            T6, T7 = bank[2], bank[3]
            B = SB + [bank[0][:], bank[1][:]]
            dve.wait_ge(x_in, 16)
            layer_norm(xres, "x")
            hT_out("xT", SB[1])
            k_low(0, 0, HALF0)
            k_low(1, 0, HALF0)
            dve.wait_ge(ev("q_high"), 1)
            dve.wait_ge(ev("q_split"), 1)
            dve.scalar_tensor_tensor(out=q_lo[:], in0=turn_bank[0][:, 0:T], scalar=XSCALE, in1=q_hi[:].bitcast(F32),
                                     op0=ALU.mult, op1=ALU.subtract).then_inc(ev("q_split"), 1)
            step(0, 0, first=True)
            dve.wait_ge(wo_in, 16)
            dve.tensor_reduce(wo_sum, wo_sb.rearrange("p g n -> p n g"), AX.X, ALU.add).then_inc(ev("wo_summed"), 1)
            with dve.Fori(1, LAST - 1, 2) as s:
                step(s, 1)
                step(s + 1, 0)
            step(LAST - 1, 1)
            step(LAST, 0, next_half=0)

            dve.wait_ge(ev("wo_folded"), 1)
            dve.tensor_copy(wo_dup[:], kp_bank[:]).then_inc(ev("wo_dup_ready"), 1)
            dve.wait_ge(denom_done, LAST + 1)
            then(dve.reciprocal(rdenom, denom))
            for st in range(ST):
                dve.wait_ge(ev("xattn_ready"), st + 1)
                then(dve.scalar_tensor_tensor(out=xres[:, st, :], in0=SB[st], scalar=rdenom[:, st:st + 1], in1=xres[:, st, :],
                                              op0=ALU.mult, op1=ALU.add))
                then(dve.tensor_tensor(xres[:, st, :], xres[:, st, :], SB[2 + st], ALU.add))

            layer_norm(xres, "x1", h0)
            dve.wait_ge(ev("ln_done"), ST * (NORMS.index("x1") + 1))
            layer_norm(h0, "h")
            hT_out("hT", T7[:])

            def soft_max(m, st, src):
                dve.wait_ge(ev("key_scores"), nth(m, st))
                then(dve.tensor_reduce(p_max[m][:, st:st + 1], src, AX.X, ALU.max))
                dve.tensor_scalar(p_bias[m][:, st:st + 1], p_max[m][:, st:st + 1], -PSCALE, None, ALU.mult).then_inc(ev("key_bias"), 1)

            def soft_norm(m, st):
                dve.wait_ge(ev("key_exp"), nth(m, st))
                then(dve.reciprocal(p_rsum[m][:, st:st + 1], p_sum[m][:, st:st + 1]))
                dve.tensor_scalar(E_sb[m][:, st, :], E_sb[m][:, st, :], p_rsum[m][:, st:st + 1], None, ALU.mult).then_inc(ev("key_normed"), 1)

            todo = [(m, st) for m in "kqv" for st in range(ST)]
            for i, (m, st) in enumerate(todo):
                soft_max(m, st, B[i])
                if i:
                    soft_norm(*todo[i - 1])
            soft_norm("v", 1)
            dve.wait_ge(ev("k_out_ready"), 1)
            dve.tensor_copy(kh[:, 2:4, :].rearrange("p c t -> p (c t)"), B[1]).then_inc(ev("kh_done"), 1)
            dve.wait_ge(ev("q_out_ready"), 1)
            dve.tensor_copy(qh[:, 2:4, :].rearrange("p c t -> p (c t)"), B[3]).then_inc(ev("qh_done"), 1)
            dve.wait_ge(ev("v_out_ready"), 2)
            dve.tensor_copy(vh[:, 1, :], B[5]).then_inc(ev("vh_done"), 1)

            def head_softmax(r):
                if r == 0:
                    dve.wait_ge(causal_done, 1)
                if r >= 2:
                    dve.wait_ge(ev("head_turned"), KC * (r - 1))
                dve.wait_ge(ev("head_scores"), 3 * r + 1)
                dve.tensor_tensor(hp0[:, r % 2], B[0].rearrange("p (c k) -> p c k", c=KC),
                                  causal[:, 1:2, :].broadcast_to([P, KC, P]), ALU.add).then_inc(ev("head_masked"), 1)
                for half in range(2):
                    dve.wait_ge(ev("head_scores"), 3 * r + 2 + half)
                    dve.tensor_tensor(hp1[:, r % 2, 2 * half:2 * half + 2, :], B[1 + half].rearrange("p (c k) -> p c k", c=2),
                                      causal[:].rearrange("p b k -> p (b k)").unsqueeze(1).broadcast_to([P, 2, T]),
                                      ALU.add).then_inc(ev("head_masked"), 1)
                dve.wait_ge(ev("head_masked"), 3 * r + 3)
                dve.tensor_reduce(h_max[:, r, 0, :], hp0[:, r % 2], AX.X, ALU.max).then_inc(ev("head_max"), 1)
                dve.tensor_reduce(h_max[:, r, 1, :], hp1[:, r % 2], AX.X, ALU.max).then_inc(ev("head_max"), 1)
                for half in range(2):
                    dve.wait_ge(ev("head_max"), 2 * r + 1 + half)
                    dve.tensor_scalar(h_bias[:, r, half, :], h_max[:, r, half, :], -HSCALE, None, ALU.mult).then_inc(ev("head_bias"), 1)

            def head_rows(r):
                dve.wait_ge(ev("head_probs"), 2 * KC * (r + 1))
                then(dve.reciprocal(h_rsum[:, r], h_sum[:, r]))
                dve.wait_ge(ev("head_out_ready"), r + 1)
                ob = B[4 + r % 2][:, 0:2 * P].rearrange("p (s c d) -> p s c d", s=2, c=KC)
                dst = o_rows.rearrange("p s (c r d) -> p s c r d", c=KC, r=HPC)[:, :, :, r, :]
                for st in range(ST):
                    ins = dve.tensor_tensor(dst[:, st], ob[:, st], h_rsum[:, r, st, :].unsqueeze(2).broadcast_to([P, KC, D]), ALU.mult)
                    if st == ST - 1:
                        ins.then_inc(ev("o_rows_done"), 1)
                    else:
                        then(ins)

            head_softmax(0)
            head_softmax(1)
            for r in range(HPC):
                head_rows(r)
                if r + 2 < HPC:
                    head_softmax(r + 2)

            hT_out("oT", T7[:])
            for st in range(ST):
                soft_max("p", st, B[st])
            for st in range(ST):
                soft_norm("p", st)
            for st in range(ST):
                dve.wait_ge(ev("p_out_ready"), st + 1)
                then(dve.tensor_tensor(h0[:, st, :], h0[:, st, :], B[2 + st], ALU.add))
            layer_norm(h0, "f")
            hT_out("fT", T7[:])
            fb = (SB, [b[:] for b in bank])
            for st in range(ST):
                for n4 in range(4):
                    dve.wait_ge(ev("f_scores"), 4 * st + n4 + 1)
                    then(dve.tensor_reduce(f_max[:, st, n4:n4 + 1], fb[st][n4], AX.X, ALU.max))
                then(dve.tensor_reduce(p_max["f"][:, st:st + 1], f_max[:, st, :], AX.X, ALU.max))
                dve.tensor_scalar(p_bias["f"][:, st:st + 1], p_max["f"][:, st:st + 1], -PSCALE, None, ALU.mult).then_inc(ev("f_bias"), 1)
            for st in range(ST):
                dve.wait_ge(ev("f_exp"), 4 * st + 4)
                then(dve.tensor_reduce(p_sum["f"][:, st:st + 1], f_part[:, st, :], AX.X, ALU.add))
                then(dve.reciprocal(p_rsum["f"][:, st:st + 1], p_sum["f"][:, st:st + 1]))
                dve.tensor_scalar(fE[:, st, :], fE[:, st, :], p_rsum["f"][:, st:st + 1], None, ALU.mult).then_inc(ev("f_normed"), 1)
            for st in range(ST):
                for n4 in range(1, 4, 2):
                    dve.wait_ge(ev("f_turned"), 4 * st + n4 + 1)
                    dve.wait_ge(ev("f_probsT"), 4 * st + n4)
                    dve.tensor_copy(fET[:, st, 4 * n4:4 * n4 + 4, :].rearrange("p n t -> p (n t)"), fb[st][n4]).then_inc(ev("f_probsT"), 1)
            for st in range(ST):
                dve.wait_ge(ev("f_out_ready"), st + 1)
                then(dve.tensor_tensor(h0[:, st, :], h0[:, st, :], fb[0][st], ALU.add))
                then(dve.tensor_tensor(xres[:, st, :], xres[:, st, :], h0[:, st, :], ALU.add))

            layer_norm(xres, "e")
            hT_out("eT", T7[:])

            dve.wait_ge(ev("logits_ready"), 1)
            dve.wait_ge(ids_done, E)
            dve.tensor_copy(logits, T6[:, 0:ST * E].rearrange("p (s e) -> p s e", s=ST)).then_inc(ev("logits_taken"), 1)
            dve.wait_ge(ev("logits_taken"), 1)
            ids = expert_id.unsqueeze(1).broadcast_to([P, ST, E])

            def wide(col):
                return col.unsqueeze(2).broadcast_to([P, ST, E])

            src = logits
            for n in range(2):
                then(dve.tensor_reduce(top[n], src, AX.X, ALU.max))
                then(dve.tensor_tensor(cand, src, wide(top[n]), ALU.is_lt))
                then(dve.scalar_tensor_tensor(out=cand, in0=cand, scalar=float(E), in1=ids, op0=ALU.mult, op1=ALU.add))
                then(dve.tensor_reduce(pick, cand, AX.X, ALU.min))
                then(dve.tensor_tensor(hot[n], ids, wide(pick), ALU.is_equal))
                if n == 0:
                    then(dve.scalar_tensor_tensor(out=rest, in0=hot[0], scalar=-BIG, in1=logits, op0=ALU.mult, op1=ALU.add))
                    src = rest
            dve.tensor_tensor(gap, top[1], top[0], ALU.subtract).then_inc(ev("gap_ready"), 1)
            dve.wait_ge(ev("second_ready"), 1)
            then(dve.tensor_scalar(both, second, 1.0, None, ALU.add))
            then(dve.reciprocal(first, both))
            then(dve.tensor_tensor(second, second, first, ALU.mult))
            then(dve.tensor_tensor(hot[0], hot[0], wide(first), ALU.mult))
            then(dve.tensor_tensor(hot[1], hot[1], wide(second), ALU.mult))
            then(dve.tensor_tensor(route, hot[0], hot[1], ALU.add))

            def gate_hidden(e):
                for j in range(HT):
                    g = HT * e + j
                    dve.wait_ge(silu_ready, g + 1)
                    dve.tensor_tensor(hid[:, j, :], sil[:, j % 4, :], SB[j % 4][:, T:2 * T], ALU.mult).then_inc(hid_ready, 1)

            def add_expert(e, b, col):
                dve.wait_ge(y_ready, e + 1)
                for st in range(ST):
                    if st or not isinstance(e, int) or e:
                        dve.wait_ge(ev("x_added"), 2 * e + st)
                    last = dve.scalar_tensor_tensor(out=xres[:, st, :], in0=bank[2 * b + st][:], scalar=col[:, st, :],
                                                    in1=xres[:, st, :], op0=ALU.mult, op1=ALU.add)
                    last.then_inc(ev("x_added"), 1)

            gate_hidden(0)
            add_expert(0, 0, route[:, :, 0:1])
            gate_hidden(1)
            add_expert(1, 1, route[:, :, 1:2])
            with dve.Fori(2, E - 1, 2) as e:
                gate_hidden(e)
                add_expert(e, 0, route[:, :, bass.ds(e, 1)])
                gate_hidden(e + 1)
                add_expert(e + 1, 1, route[:, :, bass.ds(e + 1, 1)])


def kernel(x, ctx_1024, L0_xattn_wi, L0_xattn_Wo, L0_xattn_bo, L0_attn_qK, L0_attn_qV, L0_attn_kK, L0_attn_kV,
           L0_attn_vK, L0_attn_vV, L0_attn_pK, L0_attn_pV, L0_attn_fK, L0_attn_fV, L0_ffn_w12, L0_ffn_w3, L0_ffn_gate_w):
    import numpy as np
    import concourse.bacc as bacc
    from concourse import mybir as mb
    from concourse.bass_utils import run_bass_kernel_spmd as run

    laid = {
        "x": np.asarray(x)[0], "ctxT": np.asarray(ctx_1024)[0].T, "wi": L0_xattn_wi, "Wo": L0_xattn_Wo, "bo": L0_xattn_bo,
        "qKT": np.asarray(L0_attn_qK).T, "qV": L0_attn_qV, "kKT": np.asarray(L0_attn_kK).T, "kV": L0_attn_kV,
        "vKT": np.asarray(L0_attn_vK).T, "vV": L0_attn_vV, "pKT": np.asarray(L0_attn_pK).T, "pV": L0_attn_pV,
        "fKT": np.asarray(L0_attn_fK).T, "fV": L0_attn_fV, "w12T": np.asarray(L0_ffn_w12).transpose(0, 2, 1),
        "w3T": np.asarray(L0_ffn_w3).transpose(0, 2, 1), "gateT": np.asarray(L0_ffn_gate_w).T,
    }
    nc = bacc.Bacc("TRN2", target_bir_lowering=False, num_devices=1)
    arrays, args = {}, []
    for name, a in laid.items():
        a = np.ascontiguousarray(a)
        arrays["in_" + name] = a
        args.append(nc.dram_tensor("in_" + name, a.shape, mb.dt.from_np(a.dtype), kind="ExternalInput").ap())
    T, C = laid["x"].shape
    args.append(nc.dram_tensor("out_x", (T, C), mb.dt.float32, kind="ExternalOutput").ap())
    perceiver_layer(nc, *args)
    r = run(nc, [arrays], core_ids=[0])
    return r.results[0]["out_x"].reshape(1, T, C)
```

```python
from contextlib import ExitStack

import concourse.bass as bass
from concourse import mybir

F32 = mybir.dt.float32
F32R = mybir.dt.float32r
ALU = mybir.AluOpType
ACT = mybir.ActivationFunctionType
AX = mybir.AxisListType

P = 128
EPS = 1e-5
BIG = 3.0e38


def perceiver_layer(nc, x, ctxT, wi, Wo, bo, qKT, qV, kKT, kV, vKT, vV, pKT, pV, fKT, fV, w12T, w3T, gateT, out):
    T, C = x.shape
    S = ctxT.shape[1]
    DH = wi.shape[1]
    N = qV.shape[0]
    NF = fV.shape[0]
    E, _, H2 = w12T.shape
    H = H2 // 2
    ST = T // P
    KC = C // P
    NT = N // P
    NFT = NF // P
    HT = H // P
    XHEADS = Wo.shape[0] // DH
    HEADS = 16
    D = C // HEADS
    HPC = P // D
    HALF = 512
    STEP = 2 * HALF
    STEPS = S // STEP
    HALF0 = (S - STEPS * STEP) // 2
    LAST = STEPS
    UNIT = KC * N
    SLOTS = 12
    CAP = P
    assert HALF0 == 256 and STEPS % 2 == 0 and ST == 2 and KC == 4 and 2 * DH == P
    PSCALE = float(C) ** -0.5
    HSCALE = float(D) ** -0.5
    XSCALE = float(DH) ** -0.5

    with ExitStack() as ctx:
        def sb(name, shape, dt=F32):
            return ctx.enter_context(nc.sbuf_tensor(name, shape, dt))

        def sem(name):
            return ctx.enter_context(nc.semaphore(name))

        bank = [ctx.enter_context(nc.psum_tensor(f"bank{i}", [P, 512], F32))[:] for i in range(4)]
        score_banks = ctx.enter_context(nc.psum_tensor("score_banks", [P, 4, 512], F32))
        kp_bank, turn_bank, of_bank = bank[0], bank[1:3], bank[3]

        arena = sb("arena", [P, SLOTS + 2, UNIT])
        ctx_buf = arena[:, SLOTS - 2:SLOTS + 2, :].rearrange("p (b h) (k t) -> p b (h k) t", b=2, t=STEP)
        w_split = sb("w_split", [P, 4, 2, UNIT // 2], F32R)
        xg = sb("xg", [P, 2, KC, 2 * P], F32R)
        hidT = sb("hidT", [P, 2, HT, P], F32R)
        probs = sb("probs", [P, ST, STEP])
        probsT = sb("probsT", [P, 4, 512])
        kv = sb("kv", [P, 2, HALF])
        k_full = kv[:, 0, :]
        k_split = w_split[:, 0, 0, :].rearrange("p (h n) -> p h n", h=2)
        v_rows = kv[:, 1, :].rearrange("p (g c) -> p g c", c=P)
        q_hi = hidT[:, 0, 0:2, :].rearrange("p a t -> p (a t)")
        q_lo = hidT[:, 1, 0:2, :].rearrange("p a t -> p (a t)")
        q_full = sb("q_full", [P, T])
        o_acc = sb("o_acc", [P, T])
        wi_sb = sb("wi_sb", [P, KC, DH])
        xres = sb("xres", [P, ST, C])
        hln = sb("hln", [P, ST, C])
        hT = sb("hT", [P, KC, T])
        ident = sb("ident", [P, P])
        ones = sb("ones", [P, P])
        fold = sb("fold", [P, P])
        causal = sb("causal", [P, 2, P])
        diag = sb("diag", [P, ST, P])
        gate_sb = sb("gate_sb", [P, KC, E])
        earlier = sb("earlier", [P, P])
        slot_id = sb("slot_id", [P, P])
        flag = sb("flag", [P, 1], mybir.dt.int32)
        h0 = kv[:]
        small = sb("small", [P, 512])
        small_used = [0]

        def tiny(n):
            a = small_used[0]
            small_used[0] += n
            assert small_used[0] <= 512
            return small[:, a:a + n]

        stats = [tiny(6) for _ in range(ST)]
        mv = tiny(2 * ST).rearrange("p (s c) -> p s c", c=2)
        std = tiny(ST)
        rstd = tiny(ST)
        eps_col = tiny(1)
        neg_chunk = tiny(ST)
        neg_max = [tiny(ST), tiny(ST)]
        neg_delta = tiny(ST)
        fade = tiny(ST)
        row_sum = tiny(ST)
        denom = tiny(ST)
        rdenom = tiny(ST)
        p_max, p_bias, p_sum, p_rsum = {}, {}, {}, {}
        for m in "kqvpf":
            p_max[m], p_bias[m], p_sum[m], p_rsum[m] = tiny(ST), tiny(ST), tiny(ST), tiny(ST)
        h_max, h_bias, h_sum = (tiny(2 * 16).rearrange("p (r s c) -> p r s c", r=4, s=2) for _ in range(3))
        h_rsum = tiny(2 * 16).rearrange("p (r s c) -> p r s c", r=4, s=2)
        expert_id = tiny(E)
        logits = tiny(ST * E).rearrange("p (s e) -> p s e", s=ST)
        rest = tiny(ST * E).rearrange("p (s e) -> p s e", s=ST)
        cand = tiny(ST * E).rearrange("p (s e) -> p s e", s=ST)
        hot = [tiny(ST * E).rearrange("p (s e) -> p s e", s=ST) for _ in range(2)]
        chosen = tiny(ST * E).rearrange("p (s e) -> p s e", s=ST)
        place = tiny(ST * E).rearrange("p (s e) -> p s e", s=ST)
        most = tiny(1)
        route = tiny(ST * E).rearrange("p (s e) -> p s e", s=ST)
        top = [tiny(ST) for _ in range(2)]
        pick = tiny(ST)
        gap = tiny(ST)
        second = tiny(ST)
        both = tiny(ST)
        first = tiny(ST)

        unit_slot = {"kK": 0, "qK": 1, "vK": 2, "kV": 3, "qV": 4, "vV": 5, "pK": 6, "pV": 7}
        key_sb = {m: arena[:, unit_slot[m + "K"], :].rearrange("p (k n) -> p k n", k=KC) for m in "kqvp"}
        val_sb = {m: arena[:, unit_slot[m + "V"], :].rearrange("p (k n) -> p k n", k=NT) for m in "kqvp"}
        FK_SLOTS, FV_SLOTS = (8, 9, 0, 1), (2, 3, 4, 5)
        wo_sb = arena[:, 8:10, :].rearrange("p a (g n) -> p (a g) n", n=C)
        wo_sum, wo_dup, bo_row = arena[:, 7, 0:C], arena[:, 7, C:2 * C], arena[0:1, 7, 2 * C:3 * C]
        ctx_flat = arena[:, SLOTS - 2:SLOTS + 2, :].rearrange("p a n -> p (a n)")
        E_sb = {m: ctx_flat[:, 1024 * i:1024 * (i + 1)].rearrange("p (s n) -> p s n", s=ST) for i, m in enumerate("kqvp")}
        ET_sb = {m: ctx_flat[:, 4096 + 1024 * (i % 3):4096 + 1024 * (i % 3 + 1)].rearrange("p (n t) -> p n t", t=T)
                 for i, m in enumerate("kqvp")}

        qh = probs[:].rearrange("p s n -> p (s n)")[:, 0:1024].rearrange("p (c t) -> p c t", c=KC)
        kh = probs[:].rearrange("p s n -> p (s n)")[:, 1024:2048].rearrange("p (c t) -> p c t", c=KC)
        vh = probsT[:].rearrange("p g n -> p (g n)")[:, 0:1024].rearrange("p (s n) -> p s n", s=ST)
        o_rows = probsT[:].rearrange("p g n -> p (g n)")[:, 1024:2048].rearrange("p (s n) -> p s n", s=ST)
        hp0 = ctx_flat[:, 0:1024].rearrange("p (b c k) -> p b c k", b=2, c=KC)
        hp1 = ctx_flat[:, 1024:3072].rearrange("p (b c k) -> p b c k", b=2, c=KC)
        hpT = ctx_flat[:, 7168:8192].rearrange("p (b k) -> p b k", b=2)
        fE = ctx_flat[:, 0:4096].rearrange("p (s n) -> p s n", s=ST)
        fET = ctx_flat[:, 4096:8192].rearrange("p (s n t) -> p s n t", s=ST, t=P)
        hid = ctx_flat[:, 4096:6144].rearrange("p (j t) -> p j t", t=T)
        sil = ctx_flat[:, 6144:7168].rearrange("p (b t) -> p b t", t=T)
        sel = probs[:].rearrange("p s (e j) -> p s e j", j=CAP)
        selT = probsT[:].rearrange("p g n -> p (g n)").rearrange("p (e s t) -> p e s t", e=E, s=ST)
        sel_w = arena[:, SLOTS, :].rearrange("p (s e j) -> p s e j", s=ST, e=E)
        sil_g = arena[:, SLOTS + 1, 0:1024].rearrange("p (a n) -> p a n", a=2)
        hid_rows = arena[:, SLOTS + 1, 1024:2048].rearrange("p (a n) -> p a n", a=2)
        y_rows = [kv[:, 0, :], kv[:, 1, :]]
        selT_now = [q_full[:].rearrange("p (s t) -> p s t", s=ST), o_acc[:].rearrange("p (s t) -> p s t", s=ST)]

        f_part = tiny(ST * 4).rearrange("p (s n) -> p s n", s=ST)
        f_max = tiny(ST * 4).rearrange("p (s n) -> p s n", s=ST)

        x_in, wi_in, wo_in, bo_in, gate_in = (sem(n) for n in ("x_in", "wi_in", "wo_in", "bo_in", "gate_in"))
        ctx_in = [sem("ctx_in_even"), sem("ctx_in_odd")]
        unit_first_in = [sem(f"unit_first_in_{i}") for i in range(7)]
        unit_in = [sem(f"unit_in_{i}") for i in range(SLOTS)]
        out_done = sem("out_done")
        memset_done, ident_done, ones_done, fold_done, causal_done, ids_done = (
            sem(n) for n in ("memset_done", "ident_done", "ones_done", "fold_done", "causal_done", "ids_done"))
        kp_done, k_hi_done, k_lo_done, k_full_done = (sem(n) for n in ("kp_done", "k_hi_done", "k_lo_done", "k_full_done"))
        scores_ready, chunk_max, max_ready, delta_ready = (sem(n) for n in ("scores_ready", "chunk_max", "max_ready", "delta_ready"))
        probs_ready, fade_ready, diag_ready = sem("probs_ready"), sem("fade_ready"), sem("diag_ready")
        denom_scaled, denom_done = sem("denom_scaled"), sem("denom_done")
        turned, turn_out_act, turn_out_dve = sem("turned"), sem("turn_out_act"), sem("turn_out_dve")
        o_ready, o_faded, o_added = sem("o_ready"), sem("o_faded"), sem("o_added")
        events = {}

        def ev(name):
            if name not in events:
                events[name] = sem(name)
            return events[name]

        def nth(m, st):
            return ST * "kqvp".index(m) + st + 1

        NORMS = ["x", "x1", "h", "f", "e"]
        TURNS = ["xT", "hT", "oT", "fT", "eT"]

        part_high, part_low, part_used = sem("part_high"), sem("part_low"), sem("part_used")
        h12_ready, silu_ready, hid_ready = sem("h12_ready"), sem("silu_ready"), sem("hid_ready")
        y_ready = sem("y_ready")

        block = ctx.enter_context(nc.Block())

        ctx_cols = ctxT.rearrange("(k p) t -> p k t", p=P)

        def expert_slots(b):
            return range(6, 12) if b == 0 else range(6)

        def expert_w(b):
            a = 6 if b == 0 else 0
            return (arena[:, a:a + KC, :], arena[:, a + KC:a + 6, :].rearrange("p a (k n) -> p (a k) n", n=C))

        def expert_arrived(eng, e, b, i):
            before = 32 if b or i in (1, 2, 3) else 16
            eng.wait_ge(unit_in[expert_slots(b)[i]], 8 * (e - b) + before)

        @block.sync
        def _(sp):
            sp.dma_start(wi_sb[:], wi.rearrange("(k p) d -> p k d", p=P)).then_inc(wi_in, 16)
            sp.dma_start(ctx_buf[:, 0, :, 0:2 * HALF0], ctx_cols[:, :, 0:2 * HALF0]).then_inc(ctx_in[0], 16)
            sp.dma_start(xres[:], x.rearrange("(s p) c -> p s c", p=P)).then_inc(x_in, 16)

            def load_step(s, b):
                if not isinstance(s, int) or s >= 2:
                    sp.wait_ge(kp_done, s - 1)
                sp.dma_start(ctx_buf[:, b], ctx_cols[:, :, bass.ds(2 * HALF0 + (s - 1) * STEP, STEP)]).then_inc(ctx_in[b], 16)

            load_step(1, 1)
            sp.dma_start(wo_sb, Wo.rearrange("(g p) n -> p g n", p=P)).then_inc(wo_in, 16)
            sp.dma_start(bo_row, bo.rearrange("(a n) -> a n", a=1)).then_inc(bo_in, 16)
            sp.dma_start(gate_sb[:], gateT.rearrange("(k p) e -> p k e", p=P)).then_inc(gate_in, 16)
            load_step(2, 0)
            with sp.Fori(3, LAST, 2) as s:
                load_step(s, 1)
                load_step(s + 1, 0)

            def load_unit(slot, src):
                sp.dma_start(arena[:, slot, :].rearrange("p (k n) -> p k n", n=src.shape[-1]), src).then_inc(unit_in[slot], 16)

            def rows_of(w, a, n):
                return w[a * P:(a + n) * P, :].rearrange("(k p) n -> p k n", p=P)

            sp.wait_ge(ev("xattn_ready"), 2)
            load_unit(7, rows_of(pV, 0, NT))
            load_unit(8, rows_of(fKT, 0, 1))
            load_unit(9, rows_of(fKT, 1, 1))
            sp.wait_ge(ev("key_scores"), nth("q", 1))
            load_unit(0, rows_of(fKT, 2, 1))
            load_unit(1, rows_of(fKT, 3, 1))
            for i, (used, n) in enumerate((("key_scores", nth("v", 1)), ("k_out_ready", 1), ("q_out_ready", 1), ("v_out_ready", ST))):
                sp.wait_ge(ev(used), n)
                load_unit(FV_SLOTS[i], rows_of(fV, 4 * i, 4))

            def load_expert_unit(e, b, i):
                e_at = bass.ds(e, 1)
                src = w12T[e_at, i * P:(i + 1) * P, :] if i < KC else w3T[e_at, (i - KC) * 4 * P:(i - KC + 1) * 4 * P, :]
                load_unit(expert_slots(b)[i], src.rearrange("a (k p) n -> p (a k) n", p=P))

            for i, (used, n) in enumerate((("key_scores", nth("p", 1)), ("p_out_ready", ST), ("f_scores", 8), ("f_scores", 8))):
                sp.wait_ge(ev(used), n)
                load_expert_unit(0, 0, i)
            sp.wait_ge(ev("f_turned"), 8)
            load_expert_unit(0, 0, 4)
            load_expert_unit(0, 0, 5)
            for i in range(6):
                if i == 2:
                    sp.wait_ge(ev("f_out_ready"), ST)
                load_expert_unit(1, 1, i)
            with sp.Fori(2, E - 1, 2) as e:
                for b in range(2):
                    for i in range(6):
                        sp.wait_ge(part_low, 12 * (e - 2 + b) + 2 * i + 2)
                        load_expert_unit(e + b, b, i)
            for st in range(ST):
                sp.wait_ge(ev("x_added"), ST * (E - 1) + st + 1)
                sp.dma_start(out[st * P:(st + 1) * P, :], xres[:, st, :]).then_inc(out_done, 16)
            sp.wait_ge(out_done, 16 * ST)

        @block.gpsimd
        def _(pool):
            pool.memset(ident[:], 0.0).then_inc(memset_done, 1)
            pool.memset(fold[:], 0.0).then_inc(memset_done, 1)
            pool.memset(causal[:], 0.0).then_inc(memset_done, 1)
            pool.memset(ones[:], 1.0).then_inc(ones_done, 1)
            pool.memset(eps_col, EPS).then_inc(ones_done, 1)
            pool.wait_ge(memset_done, 3)
            pool.affine_select(out=ident[:], in_=ident[:], compare_op=ALU.not_equal, fill=1.0, base=0,
                               pattern=[[-1, P]], channel_multiplier=1).then_inc(ident_done, 1)
            for n, off in enumerate((0, DH, -DH)):
                if n:
                    pool.wait_ge(fold_done, n)
                pool.affine_select(out=fold[:], in_=fold[:], compare_op=ALU.not_equal, fill=1.0, base=off,
                                   pattern=[[-1, P]], channel_multiplier=1).then_inc(fold_done, 1)
            pool.affine_select(out=causal[:, 1, :], in_=causal[:, 1, :], compare_op=ALU.is_ge, fill=-1.0e30, base=0,
                               pattern=[[-1, P]], channel_multiplier=1).then_inc(causal_done, 1)
            pool.memset(earlier[:], 1.0).then_inc(memset_done, 1)
            pool.wait_ge(memset_done, 4)
            pool.affine_select(out=earlier[:], in_=earlier[:], compare_op=ALU.is_ge, fill=0.0, base=-1,
                               pattern=[[1, P]], channel_multiplier=-1).then_inc(ids_done, 1)
            pool.iota(slot_id[:], [[1, P]], base=0, channel_multiplier=0,
                      allow_small_or_imprecise_dtypes=True).then_inc(ids_done, 1)
            for e in range(E):
                pool.memset(expert_id[:, e:e + 1], float(e)).then_inc(ids_done, 1)

            for n, (unit, src) in enumerate((("kK", kKT), ("qK", qKT), ("vK", vKT), ("kV", kV), ("qV", qV), ("vV", vV), ("pK", pKT))):
                pool.wait_ge(kp_done, 3 * n + 3)
                slot = unit_slot[unit]
                pool.dma_start(arena[:, slot, :].rearrange("p (k n) -> p k n", n=src.shape[-1]),
                               src.rearrange("(k p) n -> p k n", p=P)).then_inc(unit_first_in[slot], 16)

        @block.tensor
        def _(pe):
            def kp(s, b, half):
                for k in range(KC):
                    for h in range(2):
                        last = pe.matmul(kp_bank[DH * h:DH * (h + 1), 0:half], wi_sb[:, k, :],
                                         ctx_buf[:, b, k, h * half:(h + 1) * half], start=(k == 0), stop=(k == KC - 1))
                last.then_inc(kp_done, 1)

            def scores(s, half):
                pe.wait_ge(k_hi_done, 2 * s + 2)
                pe.wait_ge(k_lo_done, 2 * s + 2)
                for st in range(ST):
                    for h in range(2):
                        o = score_banks[:, 2 * st + h, 0:half]
                        pe.matmul(o, q_hi[:, st * P:(st + 1) * P], k_split[:, h, 0:half], start=True, stop=False)
                        last = pe.matmul(o, q_lo[:, st * P:(st + 1) * P], k_split[:, h, 0:half], start=False, stop=True)
                    last.then_inc(scores_ready, 1)

            def turn(slot, blocks):
                for c, block_in in enumerate(blocks):
                    last = pe.transpose(turn_bank[slot][:, c * P:(c + 1) * P], block_in, ident[:])
                last.then_inc(turned, 1)

            def step(s, b, first=False, next_half=HALF):
                half = HALF0 if first else HALF
                nt = half // P
                slot = 0 if first else b
                if first:
                    pe.wait_ge(ev("q_high"), 1)
                    pe.wait_ge(ev("q_split"), 2)
                else:
                    pe.wait_ge(probs_ready, 2 * s)
                scores(s, half)
                pe.wait_ge(k_full_done, s + 1)
                if not first:
                    pe.wait_ge(turn_out_dve, 2 * s - 1)
                turn(slot, [k_full[:, j * P:(j + 1) * P] for j in range(nt)])
                if next_half:
                    pe.wait_ge(ctx_in[1 - b], 8 * (s + 1) + (8 if b == 0 else 16))
                    kp(s + 1, 1 - b, next_half)
                pe.wait_ge(probs_ready, 2 * s + 2)

                def turn_probs(g):
                    if first:
                        if g == 1:
                            pe.wait_ge(turn_out_act, 1)
                    elif g == 0:
                        pe.wait_ge(turn_out_act, 3 * s - 1)
                    elif g == 2:
                        pe.wait_ge(turn_out_dve, 2 * s)
                    else:
                        pe.wait_ge(turn_out_act, 3 * s + (g - 1) // 2)
                    turn((slot + 1 + g) % 2, [probs[:, st, h * half + g * P:h * half + (g + 1) * P]
                                              for h in range(2) for st in range(ST)])

                def spread_fade():
                    pe.wait_ge(diag_ready, 2 * s)
                    pe.matmul(of_bank[:, T:2 * T], ones[:], diag[:].rearrange("p s q -> p (s q)"), start=True,
                              stop=True).then_inc(o_ready, 1)

                def pv(g):
                    if g == 0 and not first:
                        pe.wait_ge(o_added, s)
                    if first:
                        if g == 0:
                            pe.wait_ge(turn_out_dve, 1)
                            pe.wait_ge(turn_out_act, 1)
                        else:
                            pe.wait_ge(turn_out_act, 2)
                    elif g % 2 == 0:
                        pe.wait_ge(turn_out_dve, 2 * s + g // 2)
                        if g == 0:
                            pe.wait_ge(turn_out_act, 3 * s)
                    else:
                        pe.wait_ge(turn_out_act, 3 * s + 1 + g // 2)
                    for h in range(2):
                        last = pe.matmul(of_bank[DH * h:DH * (h + 1), 0:T], v_rows[:, g, DH * h:DH * (h + 1)],
                                         probsT[:, g, h * T:(h + 1) * T], start=(g == 0), stop=(g == nt - 1))
                    if first and g == nt - 1:
                        last.then_inc(o_ready, 1)

                turn_probs(0)
                turn_probs(1)
                pv(0)
                for g in range(2, nt):
                    turn_probs(g)
                    pv(g - 1)
                pv(nt - 1)
                if not first:
                    spread_fade()

            def turn_rows(src, banks):
                for k in range(KC):
                    for st in range(ST):
                        last = pe.transpose(banks[k // 2][:, (k % 2) * T + st * P:(k % 2) * T + (st + 1) * P],
                                            src[:, st, k * P:(k + 1) * P], ident[:])
                last.then_inc(ev("rows_turned"), 1)

            SB = [score_banks[:, i, :] for i in range(4)]
            pe.wait_ge(wi_in, 16)
            pe.wait_ge(ctx_in[0], 16)
            kp(0, 0, HALF0)
            pe.wait_ge(ident_done, 1)
            pe.wait_ge(ev("ln_done"), ST * (NORMS.index("x") + 1))
            turn_rows(hln, SB)
            pe.wait_ge(ev("hT_done"), 2 * (TURNS.index("xT") + 1))
            for k in range(KC):
                for h in range(2):
                    last = pe.matmul(turn_bank[0][DH * h:DH * (h + 1), 0:T], wi_sb[:, k, :], hT[:, k, :],
                                     start=(k == 0), stop=(k == KC - 1))
            last.then_inc(ev("q_ready"), 1)
            step(0, 0, first=True)
            with pe.Fori(1, LAST - 1, 2) as s:
                step(s, 1)
                step(s + 1, 0)
            step(LAST - 1, 1)
            step(LAST, 0, next_half=0)

            pe.wait_ge(ev("wo_summed"), 1)
            pe.wait_ge(fold_done, 3)
            pe.matmul(kp_bank[:], fold[:], wo_sum, start=True, stop=True).then_inc(ev("wo_folded"), 1)
            pe.wait_ge(ev("wo_dup_ready"), 1)
            pe.wait_ge(bo_in, 16)
            pe.wait_ge(ones_done, 2)
            for st in range(ST):
                pe.matmul(SB[2 + st], ones[0:1, :], bo_row, start=True, stop=False)
                pe.matmul(SB[2 + st], q_full[0:DH, st * P:(st + 1) * P], wo_dup[0:DH, :], start=False, stop=True)
            pe.wait_ge(o_added, LAST + 1)
            for st in range(ST):
                pe.matmul(SB[st], o_acc[:, st * P:(st + 1) * P], wo_dup, start=True, stop=True).then_inc(ev("xattn_ready"), 1)

            def attn_arrived(unit):
                slot = unit_slot[unit]
                pe.wait_ge(unit_in[slot] if unit == "pV" else unit_first_in[slot], 16)

            def key_scores(m, st, bk):
                for k in range(KC):
                    last = pe.matmul(bk, hT[:, k, st * P:(st + 1) * P], key_sb[m][:, k, :], start=(k == 0), stop=(k == KC - 1))
                last.then_inc(ev("key_scores"), 1)

            def turn_key_probs(m, st, bk):
                for n in range(NT):
                    last = pe.transpose(bk[:, n * P:(n + 1) * P], E_sb[m][:, st, n * P:(n + 1) * P], ident[:])
                last.then_inc(ev("key_turned"), 1)

            T6, T7 = bank[2], bank[3]
            B = SB + [bank[0], bank[1]]
            pe.wait_ge(ev("ln_done"), ST * (NORMS.index("h") + 1))
            turn_rows(hln, [T6, T7])
            pe.wait_ge(ev("hT_done"), 2 * (TURNS.index("hT") + 1))

            def scores_of(m, st):
                if st == 0:
                    attn_arrived(m + "K")
                i = 2 * "kqv".index(m) + st
                key_scores(m, st, B[i])

            def turns_of(m, st, free=None):
                pe.wait_ge(ev("key_normed"), nth(m, st))
                if free:
                    pe.wait_ge(ev("key_probsT"), free)
                turn_key_probs(m, st, (T6, T7)[st])

            def features_out(m, banks):
                attn_arrived(m + "V")
                for st in range(ST):
                    pe.wait_ge(ev("key_probsT"), nth(m, st))
                for c in range(KC):
                    for n in range(NT):
                        last = pe.matmul(banks[c // 2][:, (c % 2) * T:(c % 2 + 1) * T], val_sb[m][:, n, c * P:(c + 1) * P],
                                         ET_sb[m][:, n, :], start=(n == 0), stop=(n == NT - 1))
                last.then_inc(ev(f"{m}_out_ready"), 1)

            scores_of("k", 0)
            scores_of("k", 1)
            scores_of("q", 0)
            turns_of("k", 0)
            scores_of("q", 1)
            turns_of("k", 1)
            scores_of("v", 0)
            turns_of("q", 0, nth("k", 0))
            scores_of("v", 1)
            turns_of("q", 1, nth("k", 1))
            features_out("k", B[0:2])
            turns_of("v", 0, nth("q", 0))
            turns_of("v", 1, nth("q", 1))
            features_out("q", B[2:4])
            attn_arrived("vV")
            for st in range(ST):
                pe.wait_ge(ev("key_probsT"), nth("v", st))
                for n in range(NT):
                    last = pe.matmul(B[4 + st], ET_sb["v"][:, n, st * P:(st + 1) * P], val_sb["v"][:, n, :],
                                     start=(n == 0), stop=(n == NT - 1))
                last.then_inc(ev("v_out_ready"), 1)

            def head_scores(r):
                rows = slice(D * r, D * (r + 1))
                if r == 0:
                    pe.wait_ge(ev("kh_done"), 2)
                    pe.wait_ge(ev("qh_done"), 2)
                else:
                    pe.wait_ge(ev("head_masked"), 3 * r)
                for c in range(KC):
                    last = pe.matmul(B[0][:, c * P:(c + 1) * P], qh[rows, c, 0:P], kh[rows, c, 0:P], start=True, stop=True)
                last.then_inc(ev("head_scores"), 1)
                for c in range(KC):
                    last = pe.matmul(B[1 + c // 2][:, (c % 2) * T:(c % 2 + 1) * T], qh[rows, c, P:T], kh[rows, c, :],
                                     start=True, stop=True)
                    if c % 2:
                        last.then_inc(ev("head_scores"), 1)

            def head_turn(i):
                r, c = i // KC, i % KC
                if c == 0:
                    pe.wait_ge(ev("head_probs"), 2 * KC * (r + 1))
                if i >= 2:
                    pe.wait_ge(ev("head_turn_out"), i - 1)
                bk = (T6, T7)[i % 2]
                pe.transpose(bk[:, 0:P], hp0[:, r % 2, c, :], ident[:])
                pe.transpose(bk[:, P:2 * P], hp1[:, r % 2, c, 0:P], ident[:])
                pe.transpose(bk[:, 2 * P:3 * P], hp1[:, r % 2, c, P:2 * P], ident[:]).then_inc(ev("head_turned"), 1)

            def head_out(i):
                r, c = i // KC, i % KC
                pe.wait_ge(ev("head_turn_out"), i + 1)
                if i == 0:
                    pe.wait_ge(ev("vh_done"), 2)
                if c == 0 and r >= 2:
                    pe.wait_ge(ev("o_rows_done"), r - 1)
                ob = B[4 + r % 2][:, 0:2 * P].rearrange("p (s c d) -> p s c d", s=2, c=KC)
                vcol = slice((HPC * c + r) * D, (HPC * c + r + 1) * D)
                pe.matmul(ob[:, 0, c, :], hpT[:, i % 2, 0:P], vh[:, 0, vcol], start=True, stop=True)
                pe.matmul(ob[:, 1, c, :], hpT[:, i % 2, P:2 * P], vh[:, 0, vcol], start=True, stop=False)
                last = pe.matmul(ob[:, 1, c, :], hpT[:, i % 2, 2 * P:3 * P], vh[:, 1, vcol], start=False, stop=True)
                if c == KC - 1:
                    last.then_inc(ev("head_out_ready"), 1)

            head_scores(0)
            for r in range(HPC):
                if r + 1 < HPC:
                    head_scores(r + 1)
                for c in range(KC):
                    i = KC * r + c
                    head_turn(i)
                    if i:
                        head_out(i - 1)
            head_out(HPC * KC - 1)

            pe.wait_ge(ev("o_rows_done"), HPC)
            turn_rows(o_rows, [T6, T7])
            pe.wait_ge(ev("hT_done"), 2 * (TURNS.index("oT") + 1))
            attn_arrived("pK")
            for st in range(ST):
                key_scores("p", st, B[st])
            for st in range(ST):
                turns_of("p", st)
            attn_arrived("pV")
            for st in range(ST):
                pe.wait_ge(ev("key_probsT"), nth("p", st))
                for n in range(NT):
                    last = pe.matmul(B[2 + st], ET_sb["p"][:, n, st * P:(st + 1) * P], val_sb["p"][:, n, :],
                                     start=(n == 0), stop=(n == NT - 1))
                last.then_inc(ev("p_out_ready"), 1)

            pe.wait_ge(ev("ln_done"), ST * (NORMS.index("f") + 1))
            turn_rows(hln, [T6, T7])
            pe.wait_ge(ev("hT_done"), 2 * (TURNS.index("fT") + 1))
            for slot in FK_SLOTS:
                pe.wait_ge(unit_in[slot], 16)
            FB = [SB, bank]
            for st in range(ST):
                for n4 in range(4):
                    for k in range(KC):
                        last = pe.matmul(FB[st][n4], hT[:, k, st * P:(st + 1) * P],
                                         arena[:, FK_SLOTS[k], 512 * n4:512 * (n4 + 1)], start=(k == 0), stop=(k == KC - 1))
                    last.then_inc(ev("f_scores"), 1)
            for st in range(ST):
                pe.wait_ge(ev("f_normed"), st + 1)
                for n in range(NFT):
                    last = pe.transpose(FB[st][n // 4][:, (n % 4) * P:(n % 4 + 1) * P], fE[:, st, n * P:(n + 1) * P], ident[:])
                    if n % 4 == 3:
                        last.then_inc(ev("f_turned"), 1)
            for slot in FV_SLOTS:
                pe.wait_ge(unit_in[slot], 16)
            for st in range(ST):
                for n in range(NFT):
                    if n % 4 == 0:
                        pe.wait_ge(ev("f_probsT"), 4 * st + n // 4 + 1)
                    last = pe.matmul(FB[0][st], fET[:, st, n, :], arena[:, FV_SLOTS[n // 4], (n % 4) * C:(n % 4 + 1) * C],
                                     start=(n == 0), stop=(n == NFT - 1))
                last.then_inc(ev("f_out_ready"), 1)

            pe.wait_ge(ev("ln_done"), ST * (NORMS.index("e") + 1))
            turn_rows(hln, [T6, T7])
            pe.wait_ge(ev("hT_done"), 2 * (TURNS.index("eT") + 1))
            pe.wait_ge(gate_in, 16)
            for st in range(ST):
                for k in range(KC):
                    last = pe.matmul(T6[:, st * E:(st + 1) * E], hT[:, k, st * P:(st + 1) * P], gate_sb[:, k, :],
                                     start=(k == 0), stop=(k == KC - 1))
            last.then_inc(ev("logits_ready"), 1)
            pe.wait_ge(ev("logits_taken"), 1)

            pe.wait_ge(ev("chosen_ready"), 1)
            counts = T6[:, ST * E:(2 * ST + 1) * E].rearrange("p (s e) -> p s e", e=E)
            pe.matmul(counts[:, 0, :], earlier[:], chosen[:, 0, :], start=True, stop=True)
            pe.matmul(counts[:, 1, :], ones[:], chosen[:, 0, :], start=True, stop=False)
            pe.matmul(counts[:, 1, :], earlier[:], chosen[:, 1, :], start=False, stop=True)
            pe.matmul(counts[:, 2, :], ones[:], chosen[:, 0, :], start=True, stop=False)
            pe.matmul(counts[:, 2, :], ones[:], chosen[:, 1, :], start=False, stop=True).then_inc(ev("counted"), 1)

            def dense_expert(e, b):
                w12, w3 = expert_w(b)
                yb = [bank[2 * b], bank[2 * b + 1]]
                for i in range(6):
                    expert_arrived(pe, e, b, i)

                def hidden(j):
                    g = HT * e + j
                    if not isinstance(e, int) or g >= 4:
                        pe.wait_ge(hid_ready, g - 3)
                    for part in range(2):
                        col = 1024 * (j // 4) + 512 * part + (j % 4) * P
                        for k in range(KC):
                            last = pe.matmul(SB[j % 4][:, part * T:(part + 1) * T], w12[:, k, col:col + P], hT[:, k, :],
                                             start=(k == 0), stop=(k == KC - 1))
                    last.then_inc(h12_ready, 1)

                def down(j):
                    pe.wait_ge(hid_ready, HT * e + j + 1)
                    if j == 0 and (not isinstance(e, int) or e >= 2):
                        pe.wait_ge(ev("x_added"), 2 * (e - 1))
                    for st in range(ST):
                        last = pe.matmul(yb[st][:], hid[:, j, st * P:(st + 1) * P], w3[:, j, :],
                                         start=(j == 0), stop=(j == HT - 1))
                    if j == HT - 1:
                        last.then_inc(y_ready, 1)

                for j in range(HT):
                    hidden(j)
                    if j:
                        down(j - 1)
                down(HT - 1)

            turn_b, y_b, acc_b = bank[0], bank[1], bank[2:4]

            def gather(e):
                for k in range(KC):
                    for st in range(ST):
                        last = pe.matmul(SB[k // 2][:, (k % 2) * 2 * CAP:(k % 2 + 1) * 2 * CAP], hln[:, st, k * P:(k + 1) * P],
                                         sel[:, st, bass.ds(e, 2), :].rearrange("p e j -> p (e j)"),
                                         start=(st == 0), stop=(st == ST - 1))
                last.then_inc(ev("gathered"), 2)

            def scatter(e, b, start=False, stop=False):
                pe.wait_ge(ev("y_out"), e + 1)
                pe.wait_ge(ev("selT_staged"), e + 1)
                for st in range(ST):
                    last = pe.matmul(acc_b[st], selT_now[b][:, st, :], y_rows[b], start=start, stop=stop)
                last.then_inc(ev("scattered"), 1)

            def sparse_expert(e, b, first=False, last_one=False):
                pe.wait_ge(ev("xg_low"), e - b + 2)
                if not first:
                    pe.wait_ge(ev("hid_made"), 2 * e)
                x_hi, x_lo = (xg[:, part, :, b * CAP:(b + 1) * CAP] for part in range(2))
                for i in range(2 * KC):
                    k, half = i // 2, i % 2
                    pe.wait_ge(part_low, 12 * e + i + 1)
                    w = w_split[:, i % 4]
                    for n, (lhs, part) in enumerate(((x_hi, 0), (x_hi, 1), (x_lo, 0))):
                        for h in range(2):
                            last = pe.matmul(SB[2 * half + h], lhs[:, k, :], w[:, part, 512 * h:512 * (h + 1)],
                                             start=(k == 0 and n == 0), stop=(k == KC - 1 and n == 2))
                    last.then_inc(part_used, 1)

                def turn_hidden(half):
                    pe.wait_ge(ev("hid_made"), 2 * e + half + 1)
                    if not (first and half == 0):
                        pe.wait_ge(ev("hidT_low"), 2 * e + half)
                    for c in range(4):
                        last = pe.transpose(turn_b[:, c * P:(c + 1) * P], hid_rows[:, half, c * P:(c + 1) * P], ident[:])
                    last.then_inc(ev("hid_turned"), 1)

                turn_hidden(0)
                if not first:
                    scatter(e - 1, 1 - b, start=isinstance(e, int) and e == 1)
                turn_hidden(1)
                if b == 1 and not last_one:
                    gather(e + 1)
                for i in range(2 * KC, 12):
                    pe.wait_ge(part_low, 12 * e + i + 1)
                    if i % 2 == 0:
                        pe.wait_ge(ev("hidT_low"), 2 * e + (i - 8) // 2 + 1)
                    if i == 8 and not first:
                        pe.wait_ge(ev("y_out"), e)
                    w = w_split[:, i % 4].rearrange("p a (j n) -> p a j n", n=C)
                    for jj in range(2):
                        j = 2 * (i - 8) + jj
                        for n, (a, part) in enumerate(((0, 0), (0, 1), (1, 0))):
                            last = pe.matmul(y_b, hidT[:, a, j, :], w[:, part, jj, :], start=(j == 0 and n == 0),
                                             stop=(j == HT - 1 and n == 2))
                    last.then_inc(part_used, 1)

            pe.wait_ge(ev("flag_ready"), 1)
            crowded = pe.value_load(flag[0:1, 0:1], min_val=0, max_val=1)
            with pe.If(crowded < 1):
                pe.wait_ge(ev("sel_ready"), 1)
                gather(0)
                pe.wait_ge(ev("sel_ready"), 3)
                for g in range(4):
                    for c in range(4):
                        e, st = (4 * g + c) // ST, c % ST
                        last = pe.transpose(bank[g][:, c * P:(c + 1) * P], sel_w[:, st, e, :], ident[:])
                    last.then_inc(ev("sel_turned"), 1)
                pe.wait_ge(ev("selT_out"), 4)
                sparse_expert(0, 0, first=True)
                sparse_expert(1, 1)
                with pe.Fori(2, E - 3, 2) as e:
                    sparse_expert(e, 0)
                    sparse_expert(e + 1, 1)
                sparse_expert(E - 2, 0)
                sparse_expert(E - 1, 1, last_one=True)
                scatter(E - 1, 1, stop=True)
            with pe.Else():
                dense_expert(0, 0)
                dense_expert(1, 1)
                with pe.Fori(2, E - 1, 2) as e:
                    dense_expert(e, 0)
                    dense_expert(e + 1, 1)

        @block.scalar
        def _(act):
            def k_high(s, half):
                for h in range(2):
                    rows = slice(DH * h, DH * (h + 1))
                    act.activation(k_split[rows, h, 0:half], kp_bank[rows, 0:half], ACT.Copy).then_inc(k_hi_done, 1)

            def k_copy(half):
                act.activation(k_full[:, 0:half], kp_bank[:, 0:half], ACT.Copy).then_inc(k_full_done, 1)

            def turn_out(slot, dst, n):
                act.activation(dst, turn_bank[slot][:, 0:n], ACT.Copy).then_inc(turn_out_act, 1)

            def step(s, b, first=False, next_half=HALF):
                half = HALF0 if first else HALF
                nt = half // P
                slot = 0 if first else b
                u = 0 if first else 5 * s - 2
                act.wait_ge(turned, u + 1)
                turn_out(slot, v_rows[:, 0:nt, :].rearrange("p g c -> p (g c)"), nt * P)
                act.wait_ge(max_ready, s + 1)
                if not first:
                    act.wait_ge(denom_done, s)
                for st in range(ST):
                    act.activation(probs[:, st, 0:2 * half].rearrange("p (h n) -> p h n", h=2),
                                   score_banks[:, 2 * st:2 * st + 2, 0:half], ACT.Exp, bias=neg_max[b][:, st:st + 1],
                                   accum_out=row_sum[:, st:st + 1]).then_inc(probs_ready, 1)
                if not first:
                    act.wait_ge(delta_ready, s)
                    act.activation(fade, neg_delta, ACT.Exp).then_inc(fade_ready, 1)
                if next_half:
                    act.wait_ge(kp_done, s + 2)
                    k_copy(next_half)
                    k_high(s + 1, next_half)
                act.wait_ge(turned, u + 3)
                turn_out(slot, probsT[:, 1, :], 512)
                if nt == 4:
                    act.wait_ge(turned, u + 5)
                    turn_out(slot, probsT[:, 3, :], 512)

            def layer_norm_std(name):
                act.wait_ge(ev("ln_var"), ST * (NORMS.index(name) + 1))
                act.activation(std, mv[:, :, 1], ACT.Sqrt, bias=eps_col).then_inc(ev("ln_std"), 1)

            def hT_out(name, src):
                act.wait_ge(ev("rows_turned"), TURNS.index(name) + 1)
                act.activation(hT[:, 0:2, :].rearrange("p k t -> p (k t)"), src, ACT.Copy).then_inc(ev("hT_done"), 1)

            SB = [score_banks[:, i, :] for i in range(4)]
            T6, T7 = bank[2], bank[3]
            B = SB + [bank[0][:], bank[1][:]]
            act.wait_ge(ones_done, 2)
            layer_norm_std("x")
            act.wait_ge(kp_done, 1)
            k_copy(HALF0)
            k_high(0, HALF0)
            hT_out("xT", SB[0])
            act.wait_ge(ev("q_ready"), 1)
            act.activation(q_hi, turn_bank[0][:, 0:T], ACT.Copy, scale=XSCALE).then_inc(ev("q_high"), 1)
            act.activation(q_full[:], turn_bank[0][:, 0:T], ACT.Copy).then_inc(ev("q_split"), 1)
            step(0, 0, first=True)
            with act.Fori(1, LAST - 1, 2) as s:
                step(s, 1)
                step(s + 1, 0)
            step(LAST - 1, 1)
            step(LAST, 0, next_half=0)

            layer_norm_std("x1")
            layer_norm_std("h")
            hT_out("hT", T6[:])

            def soft_exp(m, st, src):
                act.wait_ge(ev("key_bias"), nth(m, st))
                act.activation(E_sb[m][:, st, :], src, ACT.Exp, bias=p_bias[m][:, st:st + 1], scale=PSCALE,
                               accum_out=p_sum[m][:, st:st + 1]).then_inc(ev("key_exp"), 1)

            def probsT_out(m, st):
                act.wait_ge(ev("key_turned"), nth(m, st))
                act.activation(ET_sb[m][:, :, st * P:(st + 1) * P], (T6, T7)[st][:].rearrange("p (n t) -> p n t", n=NT),
                               ACT.Copy).then_inc(ev("key_probsT"), 1)

            soft_exp("k", 0, B[0])
            soft_exp("k", 1, B[1])
            probsT_out("k", 0)
            soft_exp("q", 0, B[2])
            probsT_out("k", 1)
            soft_exp("q", 1, B[3])
            probsT_out("q", 0)
            soft_exp("v", 0, B[4])
            probsT_out("q", 1)
            soft_exp("v", 1, B[5])
            act.wait_ge(ev("k_out_ready"), 1)
            act.activation(kh[:, 0:2, :].rearrange("p c t -> p (c t)"), B[0], ACT.Copy).then_inc(ev("kh_done"), 1)
            probsT_out("v", 0)
            probsT_out("v", 1)
            act.wait_ge(ev("q_out_ready"), 1)
            act.activation(qh[:, 0:2, :].rearrange("p c t -> p (c t)"), B[2], ACT.Copy).then_inc(ev("qh_done"), 1)
            act.wait_ge(ev("v_out_ready"), 1)
            act.activation(vh[:, 0, :], B[4], ACT.Copy).then_inc(ev("vh_done"), 1)

            def head_turn_out(i):
                act.wait_ge(ev("head_turned"), i + 1)
                if i >= 2 and i % 2 == 0:
                    pass
                act.activation(hpT[:, i % 2, 0:3 * P], (T6, T7)[i % 2][:, 0:3 * P], ACT.Copy).then_inc(ev("head_turn_out"), 1)

            def head_exp(r):
                act.wait_ge(ev("head_bias"), 2 * r + 2)
                for c in range(KC):
                    act.activation(hp0[:, r % 2, c, :], hp0[:, r % 2, c, :], ACT.Exp, bias=h_bias[:, r, 0, c:c + 1], scale=HSCALE,
                                   accum_out=h_sum[:, r, 0, c:c + 1]).then_inc(ev("head_probs"), 1)
                    act.activation(hp1[:, r % 2, c, :], hp1[:, r % 2, c, :], ACT.Exp, bias=h_bias[:, r, 1, c:c + 1], scale=HSCALE,
                                   accum_out=h_sum[:, r, 1, c:c + 1]).then_inc(ev("head_probs"), 1)

            head_exp(0)
            for r in range(HPC):
                for c in range(KC):
                    head_turn_out(KC * r + c)
                if r + 1 < HPC:
                    head_exp(r + 1)

            hT_out("oT", T6[:])
            for st in range(ST):
                soft_exp("p", st, B[st])
            for st in range(ST):
                probsT_out("p", st)
            layer_norm_std("f")
            hT_out("fT", T6[:])
            for st in range(ST):
                act.wait_ge(ev("f_bias"), st + 1)
                fb = (SB, [b[:] for b in bank])[st]
                for n4 in range(4):
                    act.activation(fE[:, st, n4 * 512:(n4 + 1) * 512], fb[n4], ACT.Exp, bias=p_bias["f"][:, st:st + 1],
                                   scale=PSCALE, accum_out=f_part[:, st, n4:n4 + 1]).then_inc(ev("f_exp"), 1)
            for st in range(ST):
                fb = (SB, [b[:] for b in bank])[st]
                for n4 in range(0, 4, 2):
                    act.wait_ge(ev("f_turned"), 4 * st + n4 + 1)
                    if n4 or st:
                        act.wait_ge(ev("f_probsT"), 4 * st + n4)
                    act.activation(fET[:, st, 4 * n4:4 * n4 + 4, :].rearrange("p n t -> p (n t)"), fb[n4], ACT.Copy).then_inc(ev("f_probsT"), 1)
            layer_norm_std("e")
            hT_out("eT", T6[:])
            act.wait_ge(ev("gap_ready"), 1)
            act.activation(second, gap, ACT.Exp).then_inc(ev("second_ready"), 1)

            def dense_expert(e):
                for j in range(HT):
                    g = HT * e + j
                    act.wait_ge(h12_ready, g + 1)
                    if not isinstance(e, int) or g >= 4:
                        act.wait_ge(hid_ready, g - 3)
                    act.activation(sil[:, j % 4, :], SB[j % 4][:, 0:T], ACT.Silu).then_inc(silu_ready, 1)

            turn_b, y_b = bank[0], bank[1]

            def high(e, b, i):
                if i % 2 == 0:
                    expert_arrived(act, e, b, i // 2)
                if not isinstance(e, int) or e or i >= 4:
                    act.wait_ge(part_used, 12 * e + i - 3)
                raw = arena[:, expert_slots(b)[i // 2], (i % 2) * 1024:(i % 2 + 1) * 1024]
                act.activation(w_split[:, i % 4, 0, :], raw, ACT.Copy).then_inc(part_high, 1)

            def gathered_high(e):
                act.wait_ge(ev("gathered"), e + 2)
                act.activation(xg[:, 0].rearrange("p k t -> p (k t)"), score_banks[:, 0:2, :].rearrange("p a n -> p (a n)"),
                               ACT.Copy).then_inc(ev("xg_high"), 2)

            def sparse_expert(e, b, last_one=False):
                def silu(half):
                    act.wait_ge(part_used, 12 * e + 7 + half)
                    act.activation(sil_g[:, half, :], SB[2 * half], ACT.Silu).then_inc(silu_ready, 1)

                def hidden_high(half):
                    act.wait_ge(ev("hid_turned"), 2 * e + half + 1)
                    act.activation(hidT[:, 0, 4 * half:4 * half + 4, :].rearrange("p j t -> p (j t)"), turn_b,
                                   ACT.Copy).then_inc(ev("hidT_high"), 1)

                for i in range(4, 10):
                    high(e, b, i)
                silu(0)
                high(e, b, 10)
                silu(1)
                hidden_high(0)
                high(e, b, 11)
                hidden_high(1)
                if b == 1 and not last_one:
                    gathered_high(e + 1)
                if not last_one:
                    for i in range(4):
                        high(e + 1, 1 - b, i)
                act.wait_ge(part_used, 12 * e + 12)
                act.activation(y_rows[b], y_b, ACT.Copy).then_inc(ev("y_out"), 1)
                act.activation(selT_now[b].rearrange("p s t -> p (s t)"),
                               selT[:, bass.ds(e, 1), :, :].rearrange("p e s t -> p (e s t)"),
                               ACT.Copy).then_inc(ev("selT_staged"), 1)

            act.wait_ge(ev("flag_ready"), 1)
            crowded = act.value_load(flag[0:1, 0:1], min_val=0, max_val=1)
            with act.If(crowded < 1):
                for i in range(4):
                    high(0, 0, i)
                gathered_high(0)
                for g in range(0, 4, 2):
                    act.wait_ge(ev("sel_turned"), g + 1)
                    act.activation(selT[:, 2 * g:2 * g + 2].rearrange("p e s t -> p (e s t)"), bank[g],
                                   ACT.Copy).then_inc(ev("selT_out"), 1)
                sparse_expert(0, 0)
                sparse_expert(1, 1)
                with act.Fori(2, E - 3, 2) as e:
                    sparse_expert(e, 0)
                    sparse_expert(e + 1, 1)
                sparse_expert(E - 2, 0)
                sparse_expert(E - 1, 1, last_one=True)
            with act.Else():
                dense_expert(0)
                with act.Fori(1, E, 1) as e:
                    dense_expert(e)

        @block.vector
        def _(dve):
            dve_steps = ev("dve_steps")
            count = [0]

            def then(ins):
                count[0] += 1
                ins.then_inc(dve_steps, 1)
                dve.wait_ge(dve_steps, count[0])

            def layer_norm(src, name, dst=None):
                for st in range(ST):
                    then(dve.bn_stats(stats[st], src[:, st, :]))
                for st in range(ST):
                    dve.bn_aggr(mv[:, st, :], stats[st]).then_inc(ev("ln_var"), 1)
                dve.wait_ge(ev("ln_std"), NORMS.index(name) + 1)
                then(dve.reciprocal(rstd, std))
                for st in range(ST):
                    dve.tensor_scalar((dst or hln)[:, st, :], src[:, st, :], mv[:, st, 0:1], rstd[:, st:st + 1],
                                      ALU.subtract, ALU.mult).then_inc(ev("ln_done"), 1)

            def hT_out(name, src):
                dve.wait_ge(ev("rows_turned"), TURNS.index(name) + 1)
                dve.tensor_copy(hT[:, 2:4, :].rearrange("p k t -> p (k t)"), src).then_inc(ev("hT_done"), 1)

            def k_low(h, s, half):
                rows, other = slice(DH * h, DH * (h + 1)), slice(DH * (1 - h), DH * (2 - h))
                dve.wait_ge(k_hi_done, 2 * s + h + 1)
                dve.tensor_tensor(k_split[other, h, 0:half], k_full[rows, 0:half], k_split[rows, h, 0:half].bitcast(F32),
                                  ALU.subtract).then_inc(k_lo_done, 1)

            def turn_out(slot, dst):
                dve.tensor_copy(dst, turn_bank[slot][:]).then_inc(turn_out_dve, 1)

            def step(s, b, first=False, next_half=HALF):
                half = HALF0 if first else HALF
                nt = half // P
                slot = 0 if first else b
                u = 0 if first else 5 * s - 2
                for st in range(ST):
                    dve.wait_ge(scores_ready, 2 * s + st + 1)
                    dst = neg_max[b] if first else neg_chunk
                    dve.tensor_reduce(dst[:, st:st + 1], score_banks[:, 2 * st:2 * st + 2, 0:half], AX.XY, ALU.max,
                                      negate=True).then_inc(max_ready if first and st == ST - 1 else chunk_max, 1)
                if not first:
                    dve.wait_ge(chunk_max, 2 * s + 1)
                    dve.tensor_tensor(neg_max[b], neg_max[1 - b], neg_chunk, ALU.min).then_inc(max_ready, 1)
                    dve.wait_ge(max_ready, s + 1)
                    dve.tensor_tensor(neg_delta, neg_max[b], neg_max[1 - b], ALU.subtract).then_inc(delta_ready, 1)
                dve.wait_ge(turned, u + 2)
                turn_out((slot + 1) % 2, probsT[:, 0, :])
                if next_half:
                    k_low(0, s + 1, next_half)
                if nt == 4:
                    dve.wait_ge(turned, u + 4)
                    turn_out((slot + 1) % 2, probsT[:, 2, :])
                if next_half:
                    k_low(1, s + 1, next_half)
                if first:
                    dve.wait_ge(probs_ready, ST)
                    dve.tensor_copy(denom, row_sum).then_inc(denom_done, 1)
                else:
                    dve.wait_ge(fade_ready, s)
                    for st in range(ST):
                        dve.tensor_scalar(diag[:, st, :], ident[:], fade[:, st:st + 1], None, ALU.mult).then_inc(diag_ready, 1)
                    dve.wait_ge(denom_done, s)
                    dve.tensor_tensor(denom, denom, fade, ALU.mult).then_inc(denom_scaled, 1)
                    dve.wait_ge(denom_scaled, s)
                    dve.tensor_tensor(denom, denom, row_sum, ALU.add).then_inc(denom_done, 1)
                dve.wait_ge(o_ready, s + 1)
                if first:
                    dve.tensor_copy(o_acc[:], of_bank[:, 0:T]).then_inc(o_added, 1)
                else:
                    dve.wait_ge(o_added, s)
                    dve.tensor_tensor(o_acc[:], o_acc[:], of_bank[:, T:2 * T], ALU.mult).then_inc(o_faded, 1)
                    dve.wait_ge(o_faded, s)
                    dve.tensor_tensor(o_acc[:], o_acc[:], of_bank[:, 0:T], ALU.add).then_inc(o_added, 1)

            SB = [score_banks[:, i, :] for i in range(4)]
            T6, T7 = bank[2], bank[3]
            B = SB + [bank[0][:], bank[1][:]]
            dve.wait_ge(x_in, 16)
            layer_norm(xres, "x")
            hT_out("xT", SB[1])
            k_low(0, 0, HALF0)
            k_low(1, 0, HALF0)
            dve.wait_ge(ev("q_high"), 1)
            dve.wait_ge(ev("q_split"), 1)
            dve.scalar_tensor_tensor(out=q_lo, in0=turn_bank[0][:, 0:T], scalar=XSCALE, in1=q_hi.bitcast(F32),
                                     op0=ALU.mult, op1=ALU.subtract).then_inc(ev("q_split"), 1)
            step(0, 0, first=True)
            dve.wait_ge(wo_in, 16)
            dve.tensor_reduce(wo_sum, wo_sb.rearrange("p g n -> p n g"), AX.X, ALU.add).then_inc(ev("wo_summed"), 1)
            with dve.Fori(1, LAST - 1, 2) as s:
                step(s, 1)
                step(s + 1, 0)
            step(LAST - 1, 1)
            step(LAST, 0, next_half=0)

            dve.wait_ge(ev("wo_folded"), 1)
            dve.tensor_copy(wo_dup, kp_bank[:]).then_inc(ev("wo_dup_ready"), 1)
            dve.wait_ge(denom_done, LAST + 1)
            then(dve.reciprocal(rdenom, denom))
            for st in range(ST):
                dve.wait_ge(ev("xattn_ready"), st + 1)
                then(dve.scalar_tensor_tensor(out=xres[:, st, :], in0=SB[st], scalar=rdenom[:, st:st + 1], in1=xres[:, st, :],
                                              op0=ALU.mult, op1=ALU.add))
                then(dve.tensor_tensor(xres[:, st, :], xres[:, st, :], SB[2 + st], ALU.add))

            layer_norm(xres, "x1", h0)
            dve.wait_ge(ev("ln_done"), ST * (NORMS.index("x1") + 1))
            layer_norm(h0, "h")
            hT_out("hT", T7[:])

            def soft_max(m, st, src):
                dve.wait_ge(ev("key_scores"), nth(m, st))
                then(dve.tensor_reduce(p_max[m][:, st:st + 1], src, AX.X, ALU.max))
                dve.tensor_scalar(p_bias[m][:, st:st + 1], p_max[m][:, st:st + 1], -PSCALE, None, ALU.mult).then_inc(ev("key_bias"), 1)

            def soft_norm(m, st):
                dve.wait_ge(ev("key_exp"), nth(m, st))
                then(dve.reciprocal(p_rsum[m][:, st:st + 1], p_sum[m][:, st:st + 1]))
                dve.tensor_scalar(E_sb[m][:, st, :], E_sb[m][:, st, :], p_rsum[m][:, st:st + 1], None, ALU.mult).then_inc(ev("key_normed"), 1)

            todo = [(m, st) for m in "kqv" for st in range(ST)]
            for i, (m, st) in enumerate(todo):
                soft_max(m, st, B[i])
                if i:
                    soft_norm(*todo[i - 1])
            soft_norm("v", 1)
            dve.wait_ge(ev("k_out_ready"), 1)
            dve.tensor_copy(kh[:, 2:4, :].rearrange("p c t -> p (c t)"), B[1]).then_inc(ev("kh_done"), 1)
            dve.wait_ge(ev("q_out_ready"), 1)
            dve.tensor_copy(qh[:, 2:4, :].rearrange("p c t -> p (c t)"), B[3]).then_inc(ev("qh_done"), 1)
            dve.wait_ge(ev("v_out_ready"), 2)
            dve.tensor_copy(vh[:, 1, :], B[5]).then_inc(ev("vh_done"), 1)

            def head_softmax(r):
                if r == 0:
                    dve.wait_ge(causal_done, 1)
                if r >= 2:
                    dve.wait_ge(ev("head_turned"), KC * (r - 1))
                dve.wait_ge(ev("head_scores"), 3 * r + 1)
                dve.tensor_tensor(hp0[:, r % 2], B[0].rearrange("p (c k) -> p c k", c=KC),
                                  causal[:, 1:2, :].broadcast_to([P, KC, P]), ALU.add).then_inc(ev("head_masked"), 1)
                for half in range(2):
                    dve.wait_ge(ev("head_scores"), 3 * r + 2 + half)
                    dve.tensor_tensor(hp1[:, r % 2, 2 * half:2 * half + 2, :], B[1 + half].rearrange("p (c k) -> p c k", c=2),
                                      causal[:].rearrange("p b k -> p (b k)").unsqueeze(1).broadcast_to([P, 2, T]),
                                      ALU.add).then_inc(ev("head_masked"), 1)
                dve.wait_ge(ev("head_masked"), 3 * r + 3)
                dve.tensor_reduce(h_max[:, r, 0, :], hp0[:, r % 2], AX.X, ALU.max).then_inc(ev("head_max"), 1)
                dve.tensor_reduce(h_max[:, r, 1, :], hp1[:, r % 2], AX.X, ALU.max).then_inc(ev("head_max"), 1)
                for half in range(2):
                    dve.wait_ge(ev("head_max"), 2 * r + 1 + half)
                    dve.tensor_scalar(h_bias[:, r, half, :], h_max[:, r, half, :], -HSCALE, None, ALU.mult).then_inc(ev("head_bias"), 1)

            def head_rows(r):
                dve.wait_ge(ev("head_probs"), 2 * KC * (r + 1))
                then(dve.reciprocal(h_rsum[:, r], h_sum[:, r]))
                dve.wait_ge(ev("head_out_ready"), r + 1)
                ob = B[4 + r % 2][:, 0:2 * P].rearrange("p (s c d) -> p s c d", s=2, c=KC)
                dst = o_rows.rearrange("p s (c r d) -> p s c r d", c=KC, r=HPC)[:, :, :, r, :]
                for st in range(ST):
                    ins = dve.tensor_tensor(dst[:, st], ob[:, st], h_rsum[:, r, st, :].unsqueeze(2).broadcast_to([P, KC, D]), ALU.mult)
                    if st == ST - 1:
                        ins.then_inc(ev("o_rows_done"), 1)
                    else:
                        then(ins)

            head_softmax(0)
            head_softmax(1)
            for r in range(HPC):
                head_rows(r)
                if r + 2 < HPC:
                    head_softmax(r + 2)

            hT_out("oT", T7[:])
            for st in range(ST):
                soft_max("p", st, B[st])
            for st in range(ST):
                soft_norm("p", st)
            for st in range(ST):
                dve.wait_ge(ev("p_out_ready"), st + 1)
                then(dve.tensor_tensor(h0[:, st, :], h0[:, st, :], B[2 + st], ALU.add))
            layer_norm(h0, "f")
            hT_out("fT", T7[:])
            fb = (SB, [b[:] for b in bank])
            for st in range(ST):
                for n4 in range(4):
                    dve.wait_ge(ev("f_scores"), 4 * st + n4 + 1)
                    then(dve.tensor_reduce(f_max[:, st, n4:n4 + 1], fb[st][n4], AX.X, ALU.max))
                then(dve.tensor_reduce(p_max["f"][:, st:st + 1], f_max[:, st, :], AX.X, ALU.max))
                dve.tensor_scalar(p_bias["f"][:, st:st + 1], p_max["f"][:, st:st + 1], -PSCALE, None, ALU.mult).then_inc(ev("f_bias"), 1)
            for st in range(ST):
                dve.wait_ge(ev("f_exp"), 4 * st + 4)
                then(dve.tensor_reduce(p_sum["f"][:, st:st + 1], f_part[:, st, :], AX.X, ALU.add))
                then(dve.reciprocal(p_rsum["f"][:, st:st + 1], p_sum["f"][:, st:st + 1]))
                dve.tensor_scalar(fE[:, st, :], fE[:, st, :], p_rsum["f"][:, st:st + 1], None, ALU.mult).then_inc(ev("f_normed"), 1)
            for st in range(ST):
                for n4 in range(1, 4, 2):
                    dve.wait_ge(ev("f_turned"), 4 * st + n4 + 1)
                    dve.wait_ge(ev("f_probsT"), 4 * st + n4)
                    dve.tensor_copy(fET[:, st, 4 * n4:4 * n4 + 4, :].rearrange("p n t -> p (n t)"), fb[st][n4]).then_inc(ev("f_probsT"), 1)
            for st in range(ST):
                dve.wait_ge(ev("f_out_ready"), st + 1)
                then(dve.tensor_tensor(h0[:, st, :], h0[:, st, :], fb[0][st], ALU.add))
                then(dve.tensor_tensor(xres[:, st, :], xres[:, st, :], h0[:, st, :], ALU.add))

            layer_norm(xres, "e")
            hT_out("eT", T7[:])

            dve.wait_ge(ev("logits_ready"), 1)
            dve.wait_ge(ids_done, E + 2)
            dve.tensor_copy(logits, T6[:, 0:ST * E].rearrange("p (s e) -> p s e", s=ST)).then_inc(ev("logits_taken"), 1)
            dve.wait_ge(ev("logits_taken"), 1)
            ids = expert_id.unsqueeze(1).broadcast_to([P, ST, E])

            def wide(col):
                return col.unsqueeze(2).broadcast_to([P, ST, E])

            src = logits
            for n in range(2):
                then(dve.tensor_reduce(top[n], src, AX.X, ALU.max))
                then(dve.tensor_tensor(cand, src, wide(top[n]), ALU.is_lt))
                then(dve.scalar_tensor_tensor(out=cand, in0=cand, scalar=float(E), in1=ids, op0=ALU.mult, op1=ALU.add))
                then(dve.tensor_reduce(pick, cand, AX.X, ALU.min))
                then(dve.tensor_tensor(hot[n], ids, wide(pick), ALU.is_equal))
                if n == 0:
                    then(dve.scalar_tensor_tensor(out=rest, in0=hot[0], scalar=-BIG, in1=logits, op0=ALU.mult, op1=ALU.add))
                    src = rest
            dve.tensor_tensor(chosen, hot[0], hot[1], ALU.add).then_inc(ev("chosen_ready"), 1)
            dve.tensor_tensor(gap, top[1], top[0], ALU.subtract).then_inc(ev("gap_ready"), 1)
            dve.wait_ge(ev("second_ready"), 1)
            then(dve.tensor_scalar(both, second, 1.0, None, ALU.add))
            then(dve.reciprocal(first, both))
            then(dve.tensor_tensor(second, second, first, ALU.mult))
            then(dve.tensor_tensor(hot[0], hot[0], wide(first), ALU.mult))
            then(dve.tensor_tensor(hot[1], hot[1], wide(second), ALU.mult))
            then(dve.tensor_tensor(route, hot[0], hot[1], ALU.add))

            dve.wait_ge(ev("counted"), 1)
            counts = T6[:, ST * E:(2 * ST + 1) * E].rearrange("p (s e) -> p s e", e=E)
            then(dve.tensor_reduce(most, counts[:, 2, :], AX.X, ALU.max))
            dve.tensor_scalar(flag[:], most, float(CAP), None, ALU.is_gt).then_inc(ev("flag_ready"), 1)
            dve.wait_ge(ev("flag_ready"), 1)
            crowded = dve.value_load(flag[0:1, 0:1], min_val=0, max_val=1)

            def gate_hidden(e):
                for j in range(HT):
                    g = HT * e + j
                    dve.wait_ge(silu_ready, g + 1)
                    dve.tensor_tensor(hid[:, j, :], sil[:, j % 4, :], SB[j % 4][:, T:2 * T], ALU.mult).then_inc(hid_ready, 1)

            def add_expert(e, b, col):
                dve.wait_ge(y_ready, e + 1)
                for st in range(ST):
                    if st or not isinstance(e, int) or e:
                        dve.wait_ge(ev("x_added"), 2 * e + st)
                    last = dve.scalar_tensor_tensor(out=xres[:, st, :], in0=bank[2 * b + st][:], scalar=col[:, st, :],
                                                    in1=xres[:, st, :], op0=ALU.mult, op1=ALU.add)
                    last.then_inc(ev("x_added"), 1)
                dve.memset(most, 0.0).then_inc(part_low, 12)

            turn_b = bank[0]

            def low(e, b, i):
                dve.wait_ge(part_high, 12 * e + i + 1)
                raw = arena[:, expert_slots(b)[i // 2], (i % 2) * 1024:(i % 2 + 1) * 1024]
                dve.tensor_tensor(w_split[:, i % 4, 1, :], raw, w_split[:, i % 4, 0, :].bitcast(F32),
                                  ALU.subtract).then_inc(part_low, 1)

            def gathered_low(e):
                dve.wait_ge(ev("xg_high"), e + 2)
                dve.tensor_tensor(xg[:, 1].rearrange("p k t -> p (k t)"), score_banks[:, 0:2, :].rearrange("p a n -> p (a n)"),
                                  xg[:, 0].rearrange("p k t -> p (k t)").bitcast(F32), ALU.subtract).then_inc(ev("xg_low"), 2)

            def sparse_expert(e, b, last_one=False):
                def gate(half):
                    dve.wait_ge(silu_ready, 2 * e + half + 1)
                    dve.wait_ge(part_used, 12 * e + 7 + half)
                    dve.tensor_tensor(hid_rows[:, half, :], sil_g[:, half, :], SB[2 * half + 1], ALU.mult).then_inc(ev("hid_made"), 1)

                def hidden_low(half):
                    dve.wait_ge(ev("hidT_high"), 2 * e + half + 1)
                    hi, lo = (hidT[:, part, 4 * half:4 * half + 4, :].rearrange("p j t -> p (j t)") for part in range(2))
                    dve.tensor_tensor(lo, turn_b, hi.bitcast(F32), ALU.subtract).then_inc(ev("hidT_low"), 1)

                for i in range(4, 10):
                    low(e, b, i)
                gate(0)
                low(e, b, 10)
                gate(1)
                hidden_low(0)
                low(e, b, 11)
                hidden_low(1)
                if b == 1 and not last_one:
                    gathered_low(e + 1)
                if not last_one:
                    for i in range(4):
                        low(e + 1, 1 - b, i)

            with dve.If(crowded < 1):
                dve.scalar_tensor_tensor(out=place, in0=chosen, scalar=-1000.0, in1=counts[:, 0:2, :], op0=ALU.mult,
                                         op1=ALU.add).then_inc(ev("placed"), 1)
                dve.wait_ge(ev("placed"), 1)
                dve.tensor_scalar(place, place, 1000.0, None, ALU.add).then_inc(ev("placed"), 1)
                dve.wait_ge(ev("placed"), 2)
                for e in range(E):
                    for st in range(ST):
                        last = dve.tensor_scalar(sel[:, st, e, :], slot_id[:], place[:, st, e:e + 1], None, ALU.is_equal)
                    if e in (1, E - 1):
                        last.then_inc(ev("sel_ready"), 1)
                for e in range(E):
                    for st in range(ST):
                        last = dve.tensor_scalar(sel_w[:, st, e, :], slot_id[:], place[:, st, e:e + 1], route[:, st, e:e + 1],
                                                 ALU.is_equal, ALU.mult)
                last.then_inc(ev("sel_ready"), 1)
                for i in range(4):
                    low(0, 0, i)
                gathered_low(0)
                for g in range(1, 4, 2):
                    dve.wait_ge(ev("sel_turned"), g + 1)
                    dve.tensor_copy(selT[:, 2 * g:2 * g + 2].rearrange("p e s t -> p (e s t)"), bank[g]).then_inc(ev("selT_out"), 1)
                sparse_expert(0, 0)
                sparse_expert(1, 1)
                with dve.Fori(2, E - 3, 2) as e:
                    sparse_expert(e, 0)
                    sparse_expert(e + 1, 1)
                sparse_expert(E - 2, 0)
                sparse_expert(E - 1, 1, last_one=True)
                dve.wait_ge(ev("scattered"), E)
                for st in range(ST):
                    dve.tensor_tensor(xres[:, st, :], xres[:, st, :], bank[2 + st], ALU.add).then_inc(
                        ev("x_added"), ST * (E - 1) + 1 if st == 0 else 1)
            with dve.Else():
                for e in range(2):
                    gate_hidden(e)
                    add_expert(e, e, route[:, :, e:e + 1])
                with dve.Fori(2, E - 1, 2) as e:
                    for b in range(2):
                        gate_hidden(e + b)
                        add_expert(e + b, b, route[:, :, bass.ds(e + b, 1)])


def kernel(x, ctx_1024, L0_xattn_wi, L0_xattn_Wo, L0_xattn_bo, L0_attn_qK, L0_attn_qV, L0_attn_kK, L0_attn_kV,
           L0_attn_vK, L0_attn_vV, L0_attn_pK, L0_attn_pV, L0_attn_fK, L0_attn_fV, L0_ffn_w12, L0_ffn_w3, L0_ffn_gate_w):
    import numpy as np
    import concourse.bacc as bacc
    from concourse import mybir as mb
    from concourse.bass_utils import run_bass_kernel_spmd as run

    laid = {
        "x": np.asarray(x)[0], "ctxT": np.asarray(ctx_1024)[0].T, "wi": L0_xattn_wi, "Wo": L0_xattn_Wo, "bo": L0_xattn_bo,
        "qKT": np.asarray(L0_attn_qK).T, "qV": L0_attn_qV, "kKT": np.asarray(L0_attn_kK).T, "kV": L0_attn_kV,
        "vKT": np.asarray(L0_attn_vK).T, "vV": L0_attn_vV, "pKT": np.asarray(L0_attn_pK).T, "pV": L0_attn_pV,
        "fKT": np.asarray(L0_attn_fK).T, "fV": L0_attn_fV,
        "w12T": np.asarray(L0_ffn_w12).reshape(8, 2, 2, 512, 512).transpose(0, 4, 2, 1, 3).reshape(8, 512, 2048),
        "w3T": np.asarray(L0_ffn_w3).transpose(0, 2, 1), "gateT": np.asarray(L0_ffn_gate_w).T,
    }
    nc = bacc.Bacc("TRN2", target_bir_lowering=False, num_devices=1)
    arrays, args = {}, []
    for name, a in laid.items():
        a = np.ascontiguousarray(a)
        arrays["in_" + name] = a
        args.append(nc.dram_tensor("in_" + name, a.shape, mb.dt.from_np(a.dtype), kind="ExternalInput").ap())
    T, C = laid["x"].shape
    args.append(nc.dram_tensor("out_x", (T, C), mb.dt.float32, kind="ExternalOutput").ap())
    perceiver_layer(nc, *args)
    r = run(nc, [arrays], core_ids=[0])
    return r.results[0]["out_x"].reshape(1, T, C)
```

```python
from contextlib import ExitStack

import concourse.bass as bass
from concourse import mybir

F32 = mybir.dt.float32
F32R = mybir.dt.float32r
ALU = mybir.AluOpType
ACT = mybir.ActivationFunctionType
AX = mybir.AxisListType

P = 128
EPS = 1e-5
BIG = 3.0e38
FAR = 1000.0


def perceiver_layer(nc, x, ctxT, wi, Wo, bo, qKT, qV, kKT, kV, vKT, vV, pKT, pV, fKT, fV, w12T, w3T, gateT, out):
    T, C = x.shape
    S = ctxT.shape[1]
    DH = wi.shape[1]
    N = qV.shape[0]
    NF = fV.shape[0]
    E, _, H2 = w12T.shape
    H = H2 // 2
    ST = T // P
    KC = C // P
    NT = N // P
    NFT = NF // P
    HT = H // P
    HEADS = 16
    D = C // HEADS
    HPC = P // D
    HALF = 512
    STEP = 2 * HALF
    STEPS = S // STEP
    HALF0 = (S - STEPS * STEP) // 2
    LAST = STEPS
    UNIT = KC * N
    SLOTS = 12
    CAP = P
    assert HALF0 == 256 and STEPS % 2 == 0 and ST == 2 and KC == 4 and 2 * DH == P
    PSCALE = float(C) ** -0.5
    HSCALE = float(D) ** -0.5
    XSCALE = float(DH) ** -0.5

    with ExitStack() as ctx:
        def sb(name, shape, dt=F32):
            return ctx.enter_context(nc.sbuf_tensor(name, shape, dt))

        def sem(name):
            return ctx.enter_context(nc.semaphore(name))

        bank = [ctx.enter_context(nc.psum_tensor(f"bank{i}", [P, 512], F32))[:] for i in range(4)]
        score_banks = ctx.enter_context(nc.psum_tensor("score_banks", [P, 4, 512], F32))
        kp_bank, turn_bank, of_bank = bank[0], bank[1:3], bank[3]

        def here():
            return (nc.sbuf_base + 31) // 32 * 32

        arena_at = here()
        arena = sb("arena", [P, SLOTS + 2, UNIT])
        ctx_buf = arena[:, SLOTS - 2:SLOTS + 2, :].rearrange("p (b h) (k t) -> p b (h k) t", b=2, t=STEP)
        w_split = sb("w_split", [P, 4, 2, UNIT // 2], F32R)
        xg = sb("xg", [P, 2, KC, 2 * P], F32R)
        hidT = sb("hidT", [P, 2, HT, P], F32R)
        probs_at = here()
        probs = sb("probs", [P, ST, STEP])
        probsT_at = here()
        probsT = sb("probsT", [P, 4, 512])
        kv = sb("kv", [P, 2, HALF])
        k_full = kv[:, 0, :]
        k_split = w_split[:, 0, 0, :].rearrange("p (h n) -> p h n", h=2)
        v_rows = kv[:, 1, :].rearrange("p (g c) -> p g c", c=P)
        q_hi = hidT[:, 0, 0:2, :].rearrange("p a t -> p (a t)")
        q_lo = hidT[:, 1, 0:2, :].rearrange("p a t -> p (a t)")
        q_full = sb("q_full", [P, T])
        o_acc = sb("o_acc", [P, T])
        wi_sb = sb("wi_sb", [P, KC, DH])
        xres = sb("xres", [P, ST, C])
        hln = sb("hln", [P, ST, C])
        hT = sb("hT", [P, KC, T])
        ident = sb("ident", [P, P])
        ones = sb("ones", [P, P])
        fold = sb("fold", [P, P])
        causal = sb("causal", [P, 3, P])
        diag = sb("diag", [P, ST, P])
        gate_sb = sb("gate_sb", [P, KC, E])
        earlier = sb("earlier", [P, P])
        counters = sb("counters", [P, 2, P], F32R)
        chosen = sb("chosen", [P, ST, E], F32R)
        slot_id = sb("slot_id", [P, P])
        flag = sb("flag", [P, 1], mybir.dt.int32)
        h0 = kv[:]
        small = sb("small", [P, 512])
        small_used = [0]

        def over(name, at, shape):
            return nc.alloc_sbuf_tensor_at(name, shape, F32R, offset=at)

        def tiny(n):
            a = small_used[0]
            small_used[0] += n
            assert small_used[0] <= 512
            return small[:, a:a + n]

        stats = [tiny(6) for _ in range(ST)]
        mv = tiny(2 * ST).rearrange("p (s c) -> p s c", c=2)
        std = tiny(ST)
        rstd = tiny(ST)
        eps_col = tiny(1)
        neg_chunk = tiny(ST)
        neg_max = [tiny(ST), tiny(ST)]
        neg_delta = tiny(ST)
        fade = tiny(ST)
        row_sum = tiny(ST)
        denom = tiny(ST)
        rdenom = tiny(ST)
        p_max, p_bias, p_sum, p_rsum = {}, {}, {}, {}
        for m in "kqvpf":
            p_max[m], p_bias[m], p_sum[m], p_rsum[m] = tiny(ST), tiny(ST), tiny(ST), tiny(ST)
        h_max, h_bias, h_sum = (tiny(2 * 16).rearrange("p (r s c) -> p r s c", r=4, s=2) for _ in range(3))
        h_rsum = tiny(2 * 16).rearrange("p (r s c) -> p r s c", r=4, s=2)
        expert_id = tiny(E)
        logits = tiny(ST * E).rearrange("p (s e) -> p s e", s=ST)
        rest = tiny(ST * E).rearrange("p (s e) -> p s e", s=ST)
        cand = tiny(ST * E).rearrange("p (s e) -> p s e", s=ST)
        hot = [tiny(ST * E).rearrange("p (s e) -> p s e", s=ST) for _ in range(2)]
        place = tiny(ST * E).rearrange("p (s e) -> p s e", s=ST)
        most = tiny(1)
        route = tiny(ST * E).rearrange("p (s e) -> p s e", s=ST)
        top = [tiny(ST) for _ in range(2)]
        pick = tiny(ST)
        gap = tiny(ST)
        second = tiny(ST)
        both = tiny(ST)
        first = tiny(ST)

        unit_slot = {"kK": 0, "qK": 1, "vK": 2, "kV": 3, "qV": 4, "vV": 5, "pK": 6, "pV": 7}
        FK_SLOTS, FV_SLOTS = (8, 9, 0, 1), (2, 3, 4, 5)
        wo_sb = arena[:, 8:10, :].rearrange("p a (g n) -> p (a g) n", n=C)
        wo_sum, wo_dup, bo_row = arena[:, 7, 0:C], arena[:, 7, C:2 * C], arena[0:1, 7, 2 * C:3 * C]
        ctx_flat = arena[:, SLOTS - 2:SLOTS + 2, :].rearrange("p a n -> p (a n)")
        E_sb = {m: ctx_flat[:, 1024 * i:1024 * (i + 1)].rearrange("p (s n) -> p s n", s=ST) for i, m in enumerate("kqvp")}
        flat_at = arena_at + 4 * (SLOTS - 2) * UNIT
        ET_at = {"k": 4096, "q": 6144, "v": 0, "p": 4096}
        ET_split = {m: [over(f"ET_{m}{part}", flat_at + 4 * (ET_at[m] + 1024 * part), [P, NT, T])[:] for part in range(2)]
                    for m in "kqvp"}
        hT_split = [over(f"hT{part}", probs_at + 4096 * part, [P, KC, T])[:] for part in range(2)]

        qh = probs[:].rearrange("p s n -> p (s n)")[:, 0:1024].rearrange("p (c t) -> p c t", c=KC)
        kh = probs[:].rearrange("p s n -> p (s n)")[:, 1024:2048].rearrange("p (c t) -> p c t", c=KC)
        vh = probsT[:].rearrange("p g n -> p (g n)")[:, 0:1024].rearrange("p (s n) -> p s n", s=ST)
        hp = ctx_flat[:, 0:3072].rearrange("p (b r k) -> p b r k", b=2, r=HPC)
        hp0, hp1 = hp[:, :, :, 0:P], hp[:, :, :, P:3 * P]
        hpT = ctx_flat[:, 4096:7168].rearrange("p (b r k) -> p b r k", b=2, r=HPC)
        fE = ctx_flat[:, 0:4096].rearrange("p (s n) -> p s n", s=ST)
        fT_hi = over("fT_hi", arena_at + 4 * SLOTS * UNIT, [P, NFT, P])[:]
        fT_lo = over("fT_lo", arena_at + 4 * (SLOTS + 1) * UNIT, [P, NFT, P])[:]
        hid = ctx_flat[:, 4096:6144].rearrange("p (j t) -> p j t", t=T)
        sil = ctx_flat[:, 6144:7168].rearrange("p (b t) -> p b t", t=T)
        sel = over("sel", probs_at, [P, ST, E, CAP])[:]
        selT = over("selT", probsT_at, [P, 2, ST, P])[:]
        sel_now = over("sel_now", probsT_at + 2048, [P, ST, 2, CAP])[:]
        row_hi = over("row_hi", arena_at + 4 * SLOTS * UNIT, [P, ST, C])[:]
        row_lo = over("row_lo", arena_at + 4 * (SLOTS * UNIT + ST * C), [P, ST, C])[:]
        sil_g = arena[:, SLOTS + 1, 0:1024].rearrange("p (a n) -> p a n", a=2)
        hid_rows = arena[:, SLOTS + 1, 1024:2048].rearrange("p (a n) -> p a n", a=2)
        y_hi = over("y_hi", probsT_at + 4096, [P, C])[:]
        y_lo = over("y_lo", probsT_at + 6144, [P, C])[:]
        route_split = sb("route_split", [P, ST, E, 2], F32R)
        place_weight = tiny(2)

        f_part = tiny(ST * 4).rearrange("p (s n) -> p s n", s=ST)
        f_max = tiny(ST * 4).rearrange("p (s n) -> p s n", s=ST)

        x_in, wi_in, wo_in, bo_in, gate_in = (sem(n) for n in ("x_in", "wi_in", "wo_in", "bo_in", "gate_in"))
        ctx_in = [sem("ctx_in_even"), sem("ctx_in_odd")]
        unit_first_in = [sem(f"unit_first_in_{i}") for i in range(7)]
        unit_in = [sem(f"unit_in_{i}") for i in range(SLOTS)]
        out_done = sem("out_done")
        memset_done, ident_done, ones_done, fold_done, causal_done, ids_done = (
            sem(n) for n in ("memset_done", "ident_done", "ones_done", "fold_done", "causal_done", "ids_done"))
        kp_done, k_hi_done, k_lo_done, k_full_done = (sem(n) for n in ("kp_done", "k_hi_done", "k_lo_done", "k_full_done"))
        scores_ready, chunk_max, max_ready, delta_ready = (sem(n) for n in ("scores_ready", "chunk_max", "max_ready", "delta_ready"))
        probs_ready, fade_ready, diag_ready = sem("probs_ready"), sem("fade_ready"), sem("diag_ready")
        denom_scaled, denom_done = sem("denom_scaled"), sem("denom_done")
        turned, turn_out_act, turn_out_dve = sem("turned"), sem("turn_out_act"), sem("turn_out_dve")
        o_ready, o_faded, o_added = sem("o_ready"), sem("o_faded"), sem("o_added")
        events = {}

        def ev(name):
            if name not in events:
                events[name] = sem(name)
            return events[name]

        def nth(m, st):
            return ST * "kqvp".index(m) + st + 1

        TURNS = ["xT", "hT", "oT", "fT", "eT"]

        def normed(name, st):
            return {"x": 0, "x1": 2 + st, "h": 3 + st, "f": 6, "e": 8}[name] + st + 1

        part_high, part_low, part_used = sem("part_high"), sem("part_low"), sem("part_used")
        h12_ready, silu_ready, hid_ready = sem("h12_ready"), sem("silu_ready"), sem("hid_ready")
        y_ready = sem("y_ready")

        block = ctx.enter_context(nc.Block())

        ctx_cols = ctxT.rearrange("(k p) t -> p k t", p=P)

        def expert_slots(b):
            return range(6, 12) if b == 0 else range(6)

        def expert_w(b):
            a = 6 if b == 0 else 0
            return (arena[:, a:a + KC, :], arena[:, a + KC:a + 6, :].rearrange("p a (k n) -> p (a k) n", n=C))

        def hidden_bank(b, half):
            return score_banks[:, 2, :] if half and b == 0 else bank[0][:]

        SPLIT_UNITS = ["kK", "qK", "vK", "kV", "qV", "vV", "pK", "pV"]

        def halves(unit):
            for i in range(2):
                g = 2 * SPLIT_UNITS.index(unit) + i
                yield g, g % 4, arena[:, unit_slot[unit], i * 1024:(i + 1) * 1024]

        def ffk_raw(g):
            return arena[:, FK_SLOTS[g % 4], (g // 4) * 1024:(g // 4 + 1) * 1024]

        def f_place(st, n4):
            return 4 * (n4 // 2) + 2 * st + n4 % 2 + 1

        def ffv_raw(i):
            return arena[:, FV_SLOTS[i // 2], (i % 2) * 1024:(i % 2 + 1) * 1024]

        def expert_arrived(eng, e, b, i):
            before = 32 if b or i in (1, 2, 3) else 16
            eng.wait_ge(unit_in[expert_slots(b)[i]], 8 * (e - b) + before)

        @block.sync
        def _(sp):
            sp.dma_start(wi_sb[:], wi.rearrange("(k p) d -> p k d", p=P)).then_inc(wi_in, 16)
            sp.dma_start(ctx_buf[:, 0, :, 0:2 * HALF0], ctx_cols[:, :, 0:2 * HALF0]).then_inc(ctx_in[0], 16)

            def load_step(s, b):
                if not isinstance(s, int) or s >= 2:
                    sp.wait_ge(kp_done, s - 1)
                sp.dma_start(ctx_buf[:, b], ctx_cols[:, :, bass.ds(2 * HALF0 + (s - 1) * STEP, STEP)]).then_inc(ctx_in[b], 16)

            load_step(1, 1)
            sp.dma_start(wo_sb, Wo.rearrange("(g p) n -> p g n", p=P)).then_inc(wo_in, 16)
            sp.dma_start(bo_row, bo.rearrange("(a n) -> a n", a=1)).then_inc(bo_in, 16)
            sp.dma_start(gate_sb[:], gateT.rearrange("(k p) e -> p k e", p=P)).then_inc(gate_in, 16)
            load_step(2, 0)
            with sp.Fori(3, LAST, 2) as s:
                load_step(s, 1)
                load_step(s + 1, 0)

            def load_unit(slot, src):
                sp.dma_start(arena[:, slot, :].rearrange("p (k n) -> p k n", n=src.shape[-1]), src).then_inc(unit_in[slot], 16)

            def rows_of(w, a, n):
                return w[a * P:(a + n) * P, :].rearrange("(k p) n -> p k n", p=P)

            sp.wait_ge(ev("xattn_ready"), 2 * ST)
            load_unit(7, rows_of(pV, 0, NT))
            load_unit(8, rows_of(fKT, 0, 1))
            load_unit(9, rows_of(fKT, 1, 1))
            sp.wait_ge(ev("key_scores"), nth("q", 1))
            load_unit(0, rows_of(fKT, 2, 1))
            load_unit(1, rows_of(fKT, 3, 1))
            for i, (used, n) in enumerate((("key_scores", nth("v", 1)), ("k_out_ready", 1), ("q_out_ready", 1), ("v_out_ready", ST))):
                sp.wait_ge(ev(used), n)
                load_unit(FV_SLOTS[i], rows_of(fV, 4 * i, 4))

            def load_expert_unit(e, b, i):
                e_at = bass.ds(e, 1)
                src = w12T[e_at, i * P:(i + 1) * P, :] if i < KC else w3T[e_at, (i - KC) * 4 * P:(i - KC + 1) * 4 * P, :]
                load_unit(expert_slots(b)[i], src.rearrange("a (k p) n -> p (a k) n", p=P))

            for i, (used, n) in enumerate((("key_scores", nth("p", 1)), ("p_out_ready", ST), ("f_scores", 8), ("f_scores", 8))):
                sp.wait_ge(ev(used), n)
                load_expert_unit(0, 0, i)
            sp.wait_ge(ev("f_turned"), 8)
            load_expert_unit(0, 0, 4)
            load_expert_unit(0, 0, 5)
            for i in range(6):
                if i == 2:
                    sp.wait_ge(ev("ffv_used"), NFT)
                load_expert_unit(1, 1, i)
            with sp.Fori(2, E - 1, 2) as e:
                for b in range(2):
                    for i in range(6):
                        sp.wait_ge(part_low, 12 * (e - 2 + b) + 2 * i + 2)
                        load_expert_unit(e + b, b, i)
            for st in range(ST):
                sp.wait_ge(ev("x_added"), ST * (E - 1) + st + 1)
                sp.dma_start(out[st * P:(st + 1) * P, :], xres[:, st, :]).then_inc(out_done, 16)
            sp.wait_ge(out_done, 16 * ST)

        @block.gpsimd
        def _(pool):
            pool.memset(ident[:], 0.0).then_inc(memset_done, 1)
            pool.memset(fold[:], 0.0).then_inc(memset_done, 1)
            pool.memset(causal[:], 0.0).then_inc(memset_done, 1)
            pool.memset(ones[:], 1.0).then_inc(ones_done, 1)
            pool.memset(eps_col, EPS).then_inc(ones_done, 1)
            pool.wait_ge(memset_done, 3)
            pool.affine_select(out=ident[:], in_=ident[:], compare_op=ALU.not_equal, fill=1.0, base=0,
                               pattern=[[-1, P]], channel_multiplier=1).then_inc(ident_done, 1)
            for n, off in enumerate((0, DH, -DH)):
                if n:
                    pool.wait_ge(fold_done, n)
                pool.affine_select(out=fold[:], in_=fold[:], compare_op=ALU.not_equal, fill=1.0, base=off,
                                   pattern=[[-1, P]], channel_multiplier=1).then_inc(fold_done, 1)
            for a in (0, 2):
                pool.affine_select(out=causal[:, a, :], in_=causal[:, a, :], compare_op=ALU.is_ge, fill=-1.0e30, base=0,
                                   pattern=[[-1, P]], channel_multiplier=1).then_inc(causal_done, 1)
            pool.memset(earlier[:], 1.0).then_inc(memset_done, 1)
            pool.wait_ge(memset_done, 4)
            pool.affine_select(out=earlier[:], in_=earlier[:], compare_op=ALU.is_ge, fill=0.0, base=-1,
                               pattern=[[1, P]], channel_multiplier=-1).then_inc(ids_done, 1)
            pool.iota(slot_id[:], [[1, P]], base=-int(FAR), channel_multiplier=0,
                      allow_small_or_imprecise_dtypes=True).then_inc(ids_done, 1)
            for e in range(E):
                pool.memset(expert_id[:, e:e + 1], float(e)).then_inc(ids_done, 1)

            for n, (unit, src) in enumerate((("kK", kKT), ("qK", qKT), ("vK", vKT), ("kV", kV), ("qV", qV), ("vV", vV), ("pK", pKT))):
                if n == 1:
                    pool.wait_ge(wo_in, 16)
                    pool.tensor_tensor(wo_sb[:, 0:4, :], wo_sb[:, 0:4, :], wo_sb[:, 4:8, :], ALU.add).then_inc(ev("wo_summed"), 1)
                    pool.wait_ge(ev("wo_summed"), 1)
                    pool.tensor_tensor(wo_sb[:, 0:2, :], wo_sb[:, 0:2, :], wo_sb[:, 2:4, :], ALU.add).then_inc(ev("wo_summed"), 1)
                    pool.wait_ge(ev("wo_summed"), 2)
                    pool.tensor_tensor(wo_sum, wo_sb[:, 0, :], wo_sb[:, 1, :], ALU.add).then_inc(ev("wo_summed"), 1)
                pool.wait_ge(kp_done, 3 * n + 3)
                slot = unit_slot[unit]
                pool.dma_start(arena[:, slot, :].rearrange("p (k n) -> p k n", n=src.shape[-1]),
                               src.rearrange("(k p) n -> p k n", p=P)).then_inc(unit_first_in[slot], 16)

            for st in range(ST):
                pool.wait_ge(ev("rows_high"), st + 1)
                pool.tensor_tensor(row_lo[:, st, :], hln[:, st, :], row_hi[:, st, :].bitcast(F32),
                                   ALU.subtract).then_inc(ev("rows_low"), 1)

        @block.tensor
        def _(pe):
            def kp(s, b, half):
                for k in range(KC):
                    for h in range(2):
                        last = pe.matmul(kp_bank[DH * h:DH * (h + 1), 0:half], wi_sb[:, k, :],
                                         ctx_buf[:, b, k, h * half:(h + 1) * half], start=(k == 0), stop=(k == KC - 1))
                last.then_inc(kp_done, 1)

            def scores(s, st, half):
                if st == 0:
                    pe.wait_ge(k_hi_done, 2 * s + 2)
                    pe.wait_ge(k_lo_done, 2 * s + 2)
                for h in range(2):
                    o = score_banks[:, 2 * st + h, 0:half]
                    pe.matmul(o, q_hi[:, st * P:(st + 1) * P], k_split[:, h, 0:half], start=True, stop=False)
                    last = pe.matmul(o, q_lo[:, st * P:(st + 1) * P], k_split[:, h, 0:half], start=False, stop=True)
                last.then_inc(scores_ready, 1)

            def turn(slot, blocks):
                for c, block_in in enumerate(blocks):
                    last = pe.transpose(turn_bank[slot][:, c * P:(c + 1) * P], block_in, ident[:])
                last.then_inc(turned, 1)

            def step(s, b, first=False, next_half=HALF):
                half = HALF0 if first else HALF
                nt = half // P
                slot = 0 if first else b
                scores(s, 1, half)
                pe.wait_ge(k_full_done, s + 1)
                if not first:
                    pe.wait_ge(turn_out_dve, 2 * s - 1)
                turn(slot, [k_full[:, j * P:(j + 1) * P] for j in range(nt)])
                if next_half:
                    pe.wait_ge(ctx_in[1 - b], 8 * (s + 1) + (8 if b == 0 else 16))
                    kp(s + 1, 1 - b, next_half)
                else:
                    pe.wait_ge(ev("wo_summed"), 3)
                    pe.wait_ge(fold_done, 3)
                    pe.matmul(kp_bank[:], fold[:], wo_sum, start=True, stop=True).then_inc(ev("wo_folded"), 1)
                pe.wait_ge(probs_ready, 2 * s + 2)

                def turn_probs(g):
                    if first:
                        if g == 1:
                            pe.wait_ge(turn_out_act, 1)
                    elif g == 0:
                        pe.wait_ge(turn_out_act, 3 * s - 1)
                    elif g == 2:
                        pe.wait_ge(turn_out_dve, 2 * s)
                    else:
                        pe.wait_ge(turn_out_act, 3 * s + (g - 1) // 2)
                    turn((slot + 1 + g) % 2, [probs[:, st, h * half + g * P:h * half + (g + 1) * P]
                                              for h in range(2) for st in range(ST)])

                def spread_fade():
                    pe.wait_ge(diag_ready, 2 * s)
                    pe.wait_ge(o_added, s)
                    pe.matmul(of_bank[:, T:2 * T], ones[:], diag[:].rearrange("p s q -> p (s q)"), start=True, stop=True)

                def pv(g):
                    if first:
                        if g == 0:
                            pe.wait_ge(turn_out_dve, 1)
                            pe.wait_ge(turn_out_act, 1)
                        else:
                            pe.wait_ge(turn_out_act, 2)
                    elif g % 2 == 0:
                        pe.wait_ge(turn_out_dve, 2 * s + g // 2)
                        if g == 0:
                            pe.wait_ge(turn_out_act, 3 * s)
                    else:
                        pe.wait_ge(turn_out_act, 3 * s + 1 + g // 2)
                    for h in range(2):
                        last = pe.matmul(of_bank[DH * h:DH * (h + 1), 0:T], v_rows[:, g, DH * h:DH * (h + 1)],
                                         probsT[:, g, h * T:(h + 1) * T], start=(g == 0), stop=(g == nt - 1))
                    if g == nt - 1:
                        last.then_inc(o_ready, 1)

                turn_probs(0)
                turn_probs(1)
                if not first:
                    spread_fade()
                pv(0)
                for g in range(2, nt):
                    turn_probs(g)
                    pv(g - 1)
                if next_half:
                    scores(s + 1, 0, next_half)
                pv(nt - 1)

            def turn_rows(src, banks, name=None, tiles=range(ST)):
                for st in tiles:
                    if name:
                        pe.wait_ge(ev("ln_done"), normed(name, st))
                    for k in range(KC):
                        last = pe.transpose(banks[st][:, k * P:(k + 1) * P], src[:, st, k * P:(k + 1) * P], ident[:])
                    last.then_inc(ev("rows_turned"), 1)

            SB = [score_banks[:, i, :] for i in range(4)]
            pe.wait_ge(wi_in, 16)
            pe.wait_ge(ctx_in[0], 16)
            kp(0, 0, HALF0)
            pe.wait_ge(ident_done, 1)
            turn_rows(hln, SB, "x")
            pe.wait_ge(ev("hT_done"), 2 * (TURNS.index("xT") + 1))
            for k in range(KC):
                for h in range(2):
                    last = pe.matmul(turn_bank[0][DH * h:DH * (h + 1), 0:T], wi_sb[:, k, :], hT[:, k, :],
                                     start=(k == 0), stop=(k == KC - 1))
            last.then_inc(ev("q_ready"), 1)
            pe.wait_ge(ev("q_high"), 1)
            pe.wait_ge(ev("q_split"), 2)
            scores(0, 0, HALF0)
            step(0, 0, first=True)
            with pe.Fori(1, LAST - 1, 2) as s:
                step(s, 1)
                step(s + 1, 0)
            step(LAST - 1, 1)
            step(LAST, 0, next_half=0)

            pe.wait_ge(ev("wo_dup_ready"), 1)
            pe.wait_ge(bo_in, 16)
            pe.wait_ge(ones_done, 2)
            for st in range(ST):
                pe.matmul(SB[2 + st], ones[0:1, :], bo_row, start=True, stop=False)
                pe.matmul(SB[2 + st], q_full[0:DH, st * P:(st + 1) * P], wo_dup[0:DH, :], start=False,
                          stop=True).then_inc(ev("xattn_ready"), 1)
            pe.wait_ge(o_added, LAST + 1)
            for st in range(ST):
                pe.matmul(SB[st], o_acc[:, st * P:(st + 1) * P], wo_dup, start=True, stop=True).then_inc(ev("xattn_ready"), 1)

            THREE = ((0, 0), (0, 1), (1, 0))

            def split_ready(unit):
                pe.wait_ge(ev("attn_low"), 2 * SPLIT_UNITS.index(unit) + 2)

            def split_tile(unit, n):
                g = 2 * SPLIT_UNITS.index(unit) + n // 2
                return [w_split[:, g % 4, part, (n % 2) * 512:(n % 2 + 1) * 512] for part in range(2)]

            def key_scores(m, st, bk):
                if m != "p":
                    pe.wait_ge(ev("hT_done"), ST * TURNS.index("hT") + st + 1)
                split_ready(m + "K")
                for k in range(KC):
                    w = split_tile(m + "K", k)
                    if m == "p" and k % 2 == 0:
                        pe.wait_ge(ev("hT_done"), ST * TURNS.index("oT") + k // 2 + 1)
                    for a, (x, y) in enumerate(THREE):
                        last = pe.matmul(bk, hT_split[x][:, k, st * P:(st + 1) * P], w[y], start=(k == 0 and a == 0),
                                         stop=(k == KC - 1 and a == 2))
                last.then_inc(ev("key_scores"), 1)

            def rows_out(m, st, bk):
                split_ready(m + "V")
                pe.wait_ge(ev("key_probsT"), nth(m, st))
                for n in range(NT):
                    w = split_tile(m + "V", n)
                    for a, (x, y) in enumerate(THREE):
                        last = pe.matmul(bk, ET_split[m][x][:, n, st * P:(st + 1) * P], w[y], start=(n == 0 and a == 0),
                                         stop=(n == NT - 1 and a == 2))
                last.then_inc(ev(f"{m}_out_ready"), 1)

            def turn_key_probs(m, st, bk):
                for n in range(NT):
                    last = pe.transpose(bk[:, n * P:(n + 1) * P], E_sb[m][:, st, n * P:(n + 1) * P], ident[:])
                last.then_inc(ev("key_turned"), 1)

            T6, T7 = bank[2], bank[3]
            B = SB + [bank[0], bank[1]]
            turn_rows(hln, [T6, T7], "h", [0])

            def scores_of(m, st):
                i = 2 * "kqv".index(m) + st
                key_scores(m, st, B[i])

            def turns_of(m, st, free=None):
                if m in "kq":
                    pe.wait_ge(ev("key_normed"), nth(m, st))
                else:
                    pe.wait_ge(ev("key_exp"), nth(m, st))
                if free:
                    pe.wait_ge(ev("key_probsT"), free)
                turn_key_probs(m, st, (T6, T7)[st])

            def features_out(m, banks):
                split_ready(m + "V")
                for st in range(ST):
                    pe.wait_ge(ev("key_probsT"), nth(m, st))
                for c in range(KC):
                    for n in range(NT):
                        w = split_tile(m + "V", n)
                        for a, (x, y) in enumerate(THREE):
                            last = pe.matmul(banks[c // 2][:, (c % 2) * T:(c % 2 + 1) * T], w[y][:, c * P:(c + 1) * P],
                                             ET_split[m][x][:, n, :], start=(n == 0 and a == 0), stop=(n == NT - 1 and a == 2))
                last.then_inc(ev(f"{m}_out_ready"), 1)

            scores_of("k", 0)
            turn_rows(hln, [T6, T7], "h", [1])
            scores_of("k", 1)
            scores_of("q", 0)
            turns_of("k", 0)
            scores_of("q", 1)
            turns_of("k", 1)
            scores_of("v", 0)
            turns_of("q", 0, nth("k", 0))
            scores_of("v", 1)
            turns_of("q", 1, nth("k", 1))
            features_out("k", B[0:2])
            turns_of("v", 0, nth("q", 0))
            turns_of("v", 1, nth("q", 1))
            features_out("q", B[2:4])
            for st in range(ST):
                rows_out("v", st, B[4 + st])

            def head_scores(c):
                if c == 0:
                    pe.wait_ge(ev("kh_done"), 2)
                    pe.wait_ge(ev("qh_done"), 2)
                elif c == 1:
                    pe.wait_ge(ev("vh_done"), ST)
                for r, bk in enumerate(bank if c == 1 else SB):
                    rows = slice(D * r, D * (r + 1))
                    if c >= 2:
                        pe.wait_ge(ev("head_masked"), HPC * (0, 2)[c - 2] + r + 1)
                    pe.matmul(bk[:, 0:P], qh[rows, c, 0:P], kh[rows, c, 0:P], start=True, stop=True)
                    pe.matmul(bk[:, P:3 * P], qh[rows, c, P:T], kh[rows, c, :], start=True, stop=True).then_inc(ev("head_scores"), 1)

            def head_turns(c):
                pe.wait_ge(ev("head_normed"), 2 * c + 2)
                if c == 0:
                    pe.wait_ge(ev("head_masked"), 2 * HPC)
                for r in range(HPC):
                    i = HPC * c + r
                    if i >= 2:
                        pe.wait_ge(ev("head_turn_out"), i - 1)
                    bk = (T6, T7)[i % 2]
                    pe.transpose(bk[:, 0:P], hp0[:, c % 2, r, :], ident[:])
                    pe.transpose(bk[:, P:2 * P], hp1[:, c % 2, r, 0:P], ident[:])
                    pe.transpose(bk[:, 2 * P:3 * P], hp1[:, c % 2, r, P:2 * P], ident[:]).then_inc(ev("head_turned"), 1)

            def head_out(c):
                pe.wait_ge(ev("head_turn_out"), HPC * (c + 1))
                for a, keys, queries, start, stop in ((0, 0, 0, True, True), (1, 0, 1, True, False), (2, 1, 1, False, True)):
                    for r in range(HPC):
                        col = (c % 2) * T + queries * P
                        last = pe.matmul(B[4 + c // 2][D * r:D * (r + 1), col:col + P],
                                         vh[:, keys, (HPC * c + r) * D:(HPC * c + r + 1) * D],
                                         hpT[:, c % 2, r, a * P:(a + 1) * P], start=start, stop=stop)
                if c % 2:
                    last.then_inc(ev("rows_turned"), 1)

            for c in range(3):
                head_scores(c)
            head_turns(0)
            head_turns(1)
            head_scores(3)
            head_out(0)
            head_out(1)
            head_turns(2)
            head_turns(3)
            head_out(2)
            head_out(3)

            for st in range(ST):
                key_scores("p", st, B[st])
            for st in range(ST):
                turns_of("p", st)
            for st in range(ST):
                rows_out("p", st, B[2 + st])

            turn_rows(hln, [T6, T7], "f", [0])
            FB = [SB, bank]

            def f_scores(st, half):
                pe.wait_ge(ev("hT_done"), ST * TURNS.index("fT") + st + 1)
                for k in range(KC):
                    g = KC * half + k
                    pe.wait_ge(ev("ffk_low"), g + 1)
                    for j in range(2):
                        for a, (x, y) in enumerate(THREE):
                            last = pe.matmul(FB[st][2 * half + j], hT_split[x][:, k, st * P:(st + 1) * P],
                                             w_split[:, g % 4, y, 512 * j:512 * (j + 1)], start=(k == 0 and a == 0),
                                             stop=(k == KC - 1 and a == 2))
                        if k == KC - 1:
                            last.then_inc(ev("f_scores"), 1)
                    if st and k < KC - 1:
                        last.then_inc(ev("ffk_used"), 1)

            def f_turn(st):
                for n in range(NFT):
                    if n % 4 == 0:
                        pe.wait_ge(ev("f_exp"), 4 * st + n // 4 + 1)
                    last = pe.transpose(FB[st][n // 4][:, (n % 4) * P:(n % 4 + 1) * P], fE[:, st, n * P:(n + 1) * P], ident[:])
                    if n % 4 == 3:
                        last.then_inc(ev("f_turned"), 1)

            def f_out(st):
                for i in range(NFT // 2):
                    g = NFT // 2 * st + i
                    if i % 2 == 0:
                        pe.wait_ge(ev("f_turned_low"), 4 * st + i // 2 + 1)
                    pe.wait_ge(ev("ffv_low"), g + 1)
                    for n in (2 * i, 2 * i + 1):
                        for a, (probs_part, part) in enumerate(((fT_hi, 0), (fT_hi, 1), (fT_lo, 0))):
                            last = pe.matmul(FB[0][st], probs_part[:, n, :], w_split[:, g % 4, part, (n % 2) * C:(n % 2 + 1) * C],
                                             start=(n == 0 and a == 0), stop=(n == NFT - 1 and a == 2))
                    last.then_inc(ev("ffv_used"), 1)

            f_scores(0, 0)
            turn_rows(hln, [T6, T7], "f", [1])
            f_scores(1, 0)
            f_scores(0, 1)
            f_scores(1, 1)
            f_turn(0)
            f_out(0)
            f_turn(1)
            f_out(1)

            pe.wait_ge(gate_in, 16)
            for st in range(ST):
                turn_rows(hln, [T6, T7], "e", [st])
                pe.wait_ge(ev("hT_done"), ST * TURNS.index("eT") + st + 1)
                for k in range(KC):
                    last = pe.matmul(T6[:, st * E:(st + 1) * E], hT[:, k, st * P:(st + 1) * P], gate_sb[:, k, :],
                                     start=(k == 0), stop=(k == KC - 1))
            last.then_inc(ev("logits_ready"), 1)
            pe.wait_ge(ev("logits_taken"), 1)

            pe.wait_ge(ev("chosen_ready"), 1)
            counts = T6[:, ST * E:(2 * ST + 1) * E].rearrange("p (s e) -> p s e", e=E)
            pe.wait_ge(ev("counters_ready"), 2)
            earlier_r, ones_r = counters[:, 0, :], counters[:, 1, :]
            pe.matmul(counts[:, 0, :], earlier_r, chosen[:, 0, :], start=True, stop=True)
            pe.matmul(counts[:, 1, :], ones_r, chosen[:, 0, :], start=True, stop=False)
            pe.matmul(counts[:, 1, :], earlier_r, chosen[:, 1, :], start=False, stop=True)
            pe.matmul(counts[:, 2, :], ones_r, chosen[:, 0, :], start=True, stop=False)
            pe.matmul(counts[:, 2, :], ones_r, chosen[:, 1, :], start=False, stop=True).then_inc(ev("counted"), 1)

            def dense_expert(e, b):
                w12, w3 = expert_w(b)
                yb = [bank[2 * b], bank[2 * b + 1]]
                for i in range(6):
                    expert_arrived(pe, e, b, i)

                def hidden(j):
                    g = HT * e + j
                    if not isinstance(e, int) or g >= 4:
                        pe.wait_ge(hid_ready, g - 3)
                    for part in range(2):
                        col = 1024 * (j // 4) + 512 * part + (j % 4) * P
                        for k in range(KC):
                            last = pe.matmul(SB[j % 4][:, part * T:(part + 1) * T], w12[:, k, col:col + P], hT[:, k, :],
                                             start=(k == 0), stop=(k == KC - 1))
                    last.then_inc(h12_ready, 1)

                def down(j):
                    pe.wait_ge(hid_ready, HT * e + j + 1)
                    if j == 0 and (not isinstance(e, int) or e >= 2):
                        pe.wait_ge(ev("x_added"), 2 * (e - 1))
                    for st in range(ST):
                        last = pe.matmul(yb[st][:], hid[:, j, st * P:(st + 1) * P], w3[:, j, :],
                                         start=(j == 0), stop=(j == HT - 1))
                    if j == HT - 1:
                        last.then_inc(y_ready, 1)

                for j in range(HT):
                    hidden(j)
                    if j:
                        down(j - 1)
                down(HT - 1)

            y_b, acc_b = bank[1], bank[2:4]

            def gather(e):
                for k in range(KC):
                    if k == KC // 2 and (not isinstance(e, int) or e):
                        pe.wait_ge(ev("hid_made"), 2 * e)
                    for part, rows in enumerate((row_hi, row_lo)):
                        for st in range(ST):
                            last = pe.matmul(SB[2 * (k // 2) + part][:, (k % 2) * 2 * CAP:(k % 2 + 1) * 2 * CAP],
                                             rows[:, st, k * P:(k + 1) * P],
                                             sel[:, st, bass.ds(e, 2), :].rearrange("p e j -> p (e j)"),
                                             start=(st == 0), stop=(st == ST - 1))
                last.then_inc(ev("gathered"), 2)

            def turn_sel(e):
                pe.wait_ge(ev("sel_staged"), e + 2)
                for j in range(2):
                    for st in range(ST):
                        pe.transpose(SB[0][:, (ST * j + st) * P:(ST * j + st + 1) * P], sel_now[:, st, j, :].bitcast(F32), ident[:])
                        last = pe.matmul(SB[1][:, 2 * j:2 * j + 2], sel_now[:, st, j, :],
                                         route_split[:, st, bass.ds(e + j, 1), :].rearrange("p e a -> p (e a)"),
                                         start=(st == 0), stop=(st == ST - 1))
                last.then_inc(ev("sel_turned"), 2)

            def scatter(e, b, start=False, stop=False):
                pe.wait_ge(ev("y_low"), e + 1)
                for st in range(ST):
                    pe.matmul(acc_b[st], selT[:, b, st, :], y_hi, start=start, stop=False)
                    last = pe.matmul(acc_b[st], selT[:, b, st, :], y_lo, start=False, stop=stop)
                last.then_inc(ev("scattered"), 1)

            def sparse_expert(e, b, first=False, last_one=False):
                pe.wait_ge(ev("xg_high"), e - b + 2)
                pe.wait_ge(ev("xg_low"), e - b + 2)
                if b:
                    pe.wait_ge(ev("selT_out"), e + 1)
                    pe.wait_ge(ev("weights_ready"), e + 1)
                x_hi, x_lo = (xg[:, part, :, b * CAP:(b + 1) * CAP] for part in range(2))
                for i in range(2 * KC):
                    k, half = i // 2, i % 2
                    pe.wait_ge(part_low, 12 * e + i + 1)
                    w = w_split[:, i % 4]
                    for n, (lhs, part) in enumerate(((x_hi, 0), (x_hi, 1), (x_lo, 0))):
                        for h in range(2):
                            last = pe.matmul(SB[2 * half + h], lhs[:, k, :], w[:, part, 512 * h:512 * (h + 1)],
                                             start=(k == 0 and n == 0), stop=(k == KC - 1 and n == 2))
                    last.then_inc(part_used, 1)

                def turn_hidden(half):
                    pe.wait_ge(ev("hid_made"), 2 * e + half + 1)
                    if not (first and half == 0) and not (b == 0 and half):
                        pe.wait_ge(ev("hidT_low"), 2 * e + half)
                    for c in range(4):
                        last = pe.transpose(hidden_bank(b, half)[:, c * P:(c + 1) * P], hid_rows[:, half, c * P:(c + 1) * P], ident[:])
                    last.then_inc(ev("hid_turned"), 1)

                if not first:
                    scatter(e - 1, 1 - b, start=isinstance(e, int) and e == 1)
                turn_hidden(0)
                if b == 0:
                    if first:
                        pe.wait_ge(ev("route_parts"), 1)
                    turn_sel(e)
                elif not last_one:
                    if isinstance(e, int) and e == 1:
                        pe.wait_ge(ev("sel_ready"), 2)
                    gather(e + 1)
                turn_hidden(1)
                for i in range(2 * KC, 12):
                    pe.wait_ge(part_low, 12 * e + i + 1)
                    if i % 2 == 0:
                        pe.wait_ge(ev("hidT_low"), 2 * e + (i - 8) // 2 + 1)
                    w = w_split[:, i % 4].rearrange("p a (j n) -> p a j n", n=C)
                    for jj in range(2):
                        j = 2 * (i - 8) + jj
                        for n, (a, part) in enumerate(((0, 0), (0, 1), (1, 0))):
                            last = pe.matmul(y_b, hidT[:, a, j, :], w[:, part, jj, :], start=(j == 0 and n == 0),
                                             stop=(j == HT - 1 and n == 2))
                    last.then_inc(part_used, 1)

            pe.wait_ge(ev("flag_ready"), 1)
            crowded = pe.value_load(flag[0:1, 0:1], min_val=0, max_val=1)
            with pe.If(crowded < 1):
                pe.wait_ge(ev("rows_low"), ST)
                pe.wait_ge(ev("sel_ready"), 1)
                gather(0)
                sparse_expert(0, 0, first=True)
                sparse_expert(1, 1)
                with pe.Fori(2, E - 3, 2) as e:
                    sparse_expert(e, 0)
                    sparse_expert(e + 1, 1)
                sparse_expert(E - 2, 0)
                sparse_expert(E - 1, 1, last_one=True)
                scatter(E - 1, 1, stop=True)
            with pe.Else():
                dense_expert(0, 0)
                dense_expert(1, 1)
                with pe.Fori(2, E - 1, 2) as e:
                    dense_expert(e, 0)
                    dense_expert(e + 1, 1)

        @block.scalar
        def _(act):
            def k_high(s, half):
                for h in range(2):
                    rows = slice(DH * h, DH * (h + 1))
                    act.activation(k_split[rows, h, 0:half], kp_bank[rows, 0:half], ACT.Copy).then_inc(k_hi_done, 1)

            def k_copy(half):
                act.activation(k_full[:, 0:half], kp_bank[:, 0:half], ACT.Copy).then_inc(k_full_done, 1)

            def turn_out(slot, dst, n):
                act.activation(dst, turn_bank[slot][:, 0:n], ACT.Copy).then_inc(turn_out_act, 1)

            def step(s, b, first=False, next_half=HALF):
                half = HALF0 if first else HALF
                nt = half // P
                slot = 0 if first else b
                u = 0 if first else 5 * s - 2
                act.wait_ge(turned, u + 1)
                turn_out(slot, v_rows[:, 0:nt, :].rearrange("p g c -> p (g c)"), nt * P)
                if not first:
                    act.wait_ge(denom_done, s)
                for st in range(ST):
                    act.wait_ge(max_ready, 2 * s + st + 1)
                    act.activation(probs[:, st, 0:2 * half].rearrange("p (h n) -> p h n", h=2),
                                   score_banks[:, 2 * st:2 * st + 2, 0:half], ACT.Exp, bias=neg_max[b][:, st:st + 1],
                                   accum_out=row_sum[:, st:st + 1]).then_inc(probs_ready, 1)
                if not first:
                    act.wait_ge(delta_ready, s)
                    act.activation(fade, neg_delta, ACT.Exp).then_inc(fade_ready, 1)
                if next_half:
                    act.wait_ge(kp_done, s + 2)
                    k_copy(next_half)
                    k_high(s + 1, next_half)
                act.wait_ge(turned, u + 3)
                turn_out(slot, probsT[:, 1, :], 512)
                if nt == 4:
                    act.wait_ge(turned, u + 5)
                    turn_out(slot, probsT[:, 3, :], 512)

            def layer_norm_std(name, st):
                act.wait_ge(ev("ln_var"), normed(name, st))
                act.activation(std[:, st:st + 1], mv[:, st, 1:2], ACT.Sqrt, bias=eps_col).then_inc(ev("ln_std"), 1)

            def hT_out(name, banks, tiles=range(ST)):
                for st in tiles:
                    act.wait_ge(ev("rows_turned"), ST * TURNS.index(name) + st + 1)
                    parts = name in ("hT", "fT")
                    dst = hT_split[0] if parts else hT
                    act.activation(dst[:, :, st * P:(st + 1) * P], banks[st].rearrange("p (k t) -> p k t", k=KC),
                                   ACT.Copy).then_inc(ev("hT_high" if parts else "hT_done"), 1)

            SB = [score_banks[:, i, :] for i in range(4)]
            T6, T7 = bank[2], bank[3]
            B = SB + [bank[0][:], bank[1][:]]
            act.dma_start(xres[:], x.rearrange("(s p) c -> p s c", p=P)).then_inc(x_in, 16)
            act.wait_ge(ones_done, 2)
            for st in range(ST):
                layer_norm_std("x", st)
            act.wait_ge(kp_done, 1)
            k_copy(HALF0)
            k_high(0, HALF0)
            hT_out("xT", SB)
            act.wait_ge(ev("q_ready"), 1)
            act.activation(q_hi, turn_bank[0][:, 0:T], ACT.Copy, scale=XSCALE).then_inc(ev("q_high"), 1)
            act.activation(q_full[:], turn_bank[0][:, 0:T], ACT.Copy).then_inc(ev("q_split"), 1)
            step(0, 0, first=True)
            with act.Fori(1, LAST - 1, 2) as s:
                step(s, 1)
                step(s + 1, 0)
            step(LAST - 1, 1)
            step(LAST, 0, next_half=0)

            def attn_high(unit):
                at = SPLIT_UNITS.index(unit)
                if at >= 2:
                    m, kind = SPLIT_UNITS[at - 2]
                    if kind == "K":
                        act.wait_ge(ev("key_scores"), nth(m, 1))
                    else:
                        act.wait_ge(ev(f"{m}_out_ready"), 1 if m in "kq" else ST)
                slot = unit_slot[unit]
                act.wait_ge(unit_in[slot] if unit == "pV" else unit_first_in[slot], 16)
                for _, ring, raw in halves(unit):
                    act.activation(w_split[:, ring, 0, :], raw, ACT.Copy).then_inc(ev("attn_high"), 1)

            act.wait_ge(scores_ready, 2 * LAST + 2)
            attn_high("kK")
            attn_high("qK")
            for st in range(ST):
                layer_norm_std("x1", st)
                layer_norm_std("h", st)
                hT_out("hT", (T6, T7), [st])

            def high(e, b, i):
                if i % 2 == 0:
                    expert_arrived(act, e, b, i // 2)
                if not isinstance(e, int) or e or i >= 4:
                    act.wait_ge(part_used, 12 * e + i - 3)
                raw = arena[:, expert_slots(b)[i // 2], (i % 2) * 1024:(i % 2 + 1) * 1024]
                act.activation(w_split[:, i % 4, 0, :], raw, ACT.Copy).then_inc(part_high, 1)

            def soft_exp(m, st, src):
                act.wait_ge(ev("key_bias"), nth(m, st))
                act.activation(E_sb[m][:, st, :], src, ACT.Exp, bias=p_bias[m][:, st:st + 1], scale=PSCALE,
                               accum_out=p_sum[m][:, st:st + 1]).then_inc(ev("key_exp"), 1)

            def probsT_out(m, st):
                act.wait_ge(ev("key_turned"), nth(m, st))
                act.activation(ET_split[m][0][:, :, st * P:(st + 1) * P], (T6, T7)[st][:].rearrange("p (n t) -> p n t", n=NT),
                               ACT.Copy).then_inc(ev("key_probsT_high"), 1)

            soft_exp("k", 0, B[0])
            soft_exp("k", 1, B[1])
            attn_high("vK")
            probsT_out("k", 0)
            soft_exp("q", 0, B[2])
            probsT_out("k", 1)
            soft_exp("q", 1, B[3])
            attn_high("kV")
            probsT_out("q", 0)
            soft_exp("v", 0, B[4])
            probsT_out("q", 1)
            soft_exp("v", 1, B[5])
            attn_high("qV")
            act.wait_ge(ev("k_out_ready"), 1)
            act.activation(kh[:, 0:2, :].rearrange("p c t -> p (c t)"), B[0], ACT.Copy).then_inc(ev("kh_done"), 1)
            probsT_out("v", 0)
            probsT_out("v", 1)
            attn_high("vV")
            act.wait_ge(ev("q_out_ready"), 1)
            act.activation(qh[:, 0:2, :].rearrange("p c t -> p (c t)"), B[2], ACT.Copy).then_inc(ev("qh_done"), 1)
            attn_high("pK")
            attn_high("pV")

            def head_turn_out(c):
                for r in range(HPC):
                    i = HPC * c + r
                    act.wait_ge(ev("head_turned"), i + 1)
                    act.activation(hpT[:, c % 2, r, :], (T6, T7)[i % 2][:, 0:3 * P], ACT.Copy).then_inc(ev("head_turn_out"), 1)

            def head_exp(c):
                act.wait_ge(ev("head_bias"), c + 1)
                for r in range(HPC):
                    for half, part in enumerate((hp0, hp1)):
                        act.activation(part[:, c % 2, r, :], part[:, c % 2, r, :], ACT.Exp, bias=h_bias[:, c, half, r:r + 1],
                                       scale=HSCALE, accum_out=h_sum[:, c, half, r:r + 1]).then_inc(ev("head_probs"), 1)

            for pair in range(2):
                for c in (2 * pair, 2 * pair + 1):
                    head_exp(c)
                for c in (2 * pair, 2 * pair + 1):
                    head_turn_out(c)
            for pair in range(2):
                act.wait_ge(ev("rows_turned"), ST * TURNS.index("oT") + pair + 1)
                act.activation(hT_split[0][:, 2 * pair:2 * pair + 2, :].rearrange("p k t -> p (k t)"), B[4 + pair],
                               ACT.Copy).then_inc(ev("hT_high"), 1)

            soft_exp("p", 0, B[0])
            probsT_out("p", 0)
            soft_exp("p", 1, B[1])
            probsT_out("p", 1)
            def ffk_high(g):
                if g < 4:
                    act.wait_ge(unit_in[FK_SLOTS[g]], 16)
                    act.wait_ge(ev("key_scores" if g < 2 else "p_out_ready"), nth("p", 1) if g < 2 else ST)
                elif g < 7:
                    act.wait_ge(ev("ffk_used"), g - 3)
                else:
                    act.wait_ge(ev("f_scores"), f_place(1, 1))
                act.activation(w_split[:, g % 4, 0, :], ffk_raw(g), ACT.Copy).then_inc(ev("ffk_high"), 1)

            ffk_high(0)
            ffk_high(1)
            layer_norm_std("f", 0)
            hT_out("fT", (T6, T7), [0])
            layer_norm_std("f", 1)
            for g in (2, 3):
                ffk_high(g)
            hT_out("fT", (T6, T7), [1])
            for g in range(4, 8):
                ffk_high(g)
            fb = (SB, [b[:] for b in bank])

            def ffv_high(g):
                i = g % (NFT // 2)
                if g < NFT // 2 and i % 2 == 0:
                    act.wait_ge(unit_in[FV_SLOTS[i // 2]], 16)
                if g >= 4:
                    act.wait_ge(ev("ffv_used"), g - 3)
                elif g < 3:
                    act.wait_ge(ev("ffk_used"), KC - 1 + g + 1)
                else:
                    act.wait_ge(ev("f_scores"), f_place(1, 3))
                act.activation(w_split[:, g % 4, 0, :], ffv_raw(i), ACT.Copy).then_inc(ev("ffv_high"), 1)

            def f_exp(st, banks=range(4)):
                act.wait_ge(ev("f_bias"), st + 1)
                for n4 in banks:
                    act.activation(fE[:, st, n4 * 512:(n4 + 1) * 512], fb[st][n4], ACT.Exp, bias=p_bias["f"][:, st:st + 1],
                                   scale=PSCALE, accum_out=f_part[:, st, n4:n4 + 1]).then_inc(ev("f_exp"), 1)

            def f_turned_high(st, banks=range(4)):
                for n4 in banks:
                    act.wait_ge(ev("f_turned"), 4 * st + n4 + 1)
                    act.activation(fT_hi[:, 4 * n4:4 * n4 + 4, :].rearrange("p n t -> p (n t)"), fb[st][n4],
                                   ACT.Copy).then_inc(ev("f_turned_high"), 1)

            def first_high(i):
                act.wait_ge(ev("ffv_used"), NFT - 4 + i + 1)
                high(0, 0, i)

            f_exp(0, (0, 1))
            ffv_high(0)
            f_exp(0, (2, 3))
            ffv_high(1)
            f_turned_high(0, (0, 1))
            ffv_high(2)
            f_turned_high(0, (2, 3))
            ffv_high(3)
            ffv_high(4)
            ffv_high(5)
            f_exp(1, (0, 1))
            ffv_high(6)
            f_exp(1, (2, 3))
            for g in range(7, 11):
                ffv_high(g)
            f_turned_high(1)
            for g in range(11, 16):
                ffv_high(g)
            first_high(0)
            first_high(1)
            layer_norm_std("e", 0)
            first_high(2)
            hT_out("eT", (T6, T7), [0])
            layer_norm_std("e", 1)
            hT_out("eT", (T6, T7), [1])
            act.wait_ge(ids_done, 1)
            act.activation(counters[:, 0, :], earlier[:], ACT.Copy).then_inc(ev("counters_ready"), 1)
            act.activation(counters[:, 1, :], ones[:], ACT.Copy).then_inc(ev("counters_ready"), 1)
            for st in range(ST):
                act.wait_ge(ev("ln_done"), normed("e", st))
                act.wait_ge(ev("ffv_used"), NFT)
                act.activation(row_hi[:, st, :], hln[:, st, :], ACT.Copy).then_inc(ev("rows_high"), 1)
            first_high(3)
            act.wait_ge(ev("gap_ready"), 1)
            act.activation(second, gap, ACT.Exp).then_inc(ev("second_ready"), 1)

            def dense_expert(e):
                for j in range(HT):
                    g = HT * e + j
                    act.wait_ge(h12_ready, g + 1)
                    if not isinstance(e, int) or g >= 4:
                        act.wait_ge(hid_ready, g - 3)
                    act.activation(sil[:, j % 4, :], SB[j % 4][:, 0:T], ACT.Silu).then_inc(silu_ready, 1)

            y_b = bank[1]

            def gathered_high(e):
                act.wait_ge(ev("gathered"), e + 2)
                for a in range(2):
                    act.activation(xg[:, 0, 2 * a:2 * a + 2, :].rearrange("p k t -> p (k t)"), SB[2 * a],
                                   ACT.Copy).then_inc(ev("xg_high"), 1)

            def sparse_expert(e, b, last_one=False):
                def silu(half):
                    act.wait_ge(part_used, 12 * e + 7 + half)
                    act.activation(sil_g[:, half, :], SB[2 * half], ACT.Silu).then_inc(silu_ready, 1)

                def hidden_high(half):
                    act.wait_ge(ev("hid_turned"), 2 * e + half + 1)
                    act.activation(hidT[:, 0, 4 * half:4 * half + 4, :].rearrange("p j t -> p (j t)"), hidden_bank(b, half),
                                   ACT.Copy).then_inc(ev("hidT_high"), 1)

                if b == 0:
                    act.wait_ge(ev("sel_ready"), 1 if isinstance(e, int) and e == 0 else 2)
                    if not isinstance(e, int) or e:
                        act.wait_ge(ev("sel_turned"), e)
                    act.activation(sel_now, sel[:, :, bass.ds(e, 2), :].bitcast(F32), ACT.Copy).then_inc(ev("sel_staged"), 2)
                for i in range(4, 10):
                    high(e, b, i)
                silu(0)
                silu(1)
                hidden_high(0)
                high(e, b, 10)
                hidden_high(1)
                high(e, b, 11)
                if b == 0:
                    act.wait_ge(ev("sel_turned"), e + 2)
                    act.activation(selT.rearrange("p e s t -> p (e s t)"), SB[0], ACT.Copy).then_inc(ev("selT_out"), 2)
                elif not last_one:
                    gathered_high(e + 1)
                if not last_one:
                    for i in range(4):
                        high(e + 1, 1 - b, i)
                act.wait_ge(part_used, 12 * e + 12)
                act.wait_ge(ev("weights_ready"), e - b + 2)
                act.activation(y_hi, y_b, ACT.Copy, scale=place_weight[:, b:b + 1]).then_inc(ev("y_high"), 1)

            act.wait_ge(ev("flag_ready"), 1)
            crowded = act.value_load(flag[0:1, 0:1], min_val=0, max_val=1)
            with act.If(crowded < 1):
                gathered_high(0)
                sparse_expert(0, 0)
                sparse_expert(1, 1)
                with act.Fori(2, E - 3, 2) as e:
                    sparse_expert(e, 0)
                    sparse_expert(e + 1, 1)
                sparse_expert(E - 2, 0)
                sparse_expert(E - 1, 1, last_one=True)
            with act.Else():
                dense_expert(0)
                with act.Fori(1, E, 1) as e:
                    dense_expert(e)

        @block.vector
        def _(dve):
            dve_steps = ev("dve_steps")
            count = [0]

            def then(ins):
                count[0] += 1
                ins.then_inc(dve_steps, 1)
                dve.wait_ge(dve_steps, count[0])

            def layer_norm(name, src, st, dst=hln, between=None):
                n = normed(name, st)
                then(dve.bn_stats(stats[st], src[:, st, :]))
                dve.bn_aggr(mv[:, st, :], stats[st]).then_inc(ev("ln_var"), 1)
                if between:
                    between()
                dve.wait_ge(ev("ln_std"), n)
                then(dve.reciprocal(rstd[:, st:st + 1], std[:, st:st + 1]))
                dve.tensor_scalar(dst[:, st, :], src[:, st, :], mv[:, st, 0:1], rstd[:, st:st + 1],
                                  ALU.subtract, ALU.mult).then_inc(ev("ln_done"), 1)

            def k_low(h, s, half):
                rows, other = slice(DH * h, DH * (h + 1)), slice(DH * (1 - h), DH * (2 - h))
                dve.wait_ge(k_hi_done, 2 * s + h + 1)
                dve.tensor_tensor(k_split[other, h, 0:half], k_full[rows, 0:half], k_split[rows, h, 0:half].bitcast(F32),
                                  ALU.subtract).then_inc(k_lo_done, 1)

            def turn_out(slot, dst):
                dve.tensor_copy(dst, turn_bank[slot][:]).then_inc(turn_out_dve, 1)

            def maxima(s, b, half, first=False):
                for st in range(ST):
                    dve.wait_ge(scores_ready, 2 * s + st + 1)
                    tile_max = (neg_max[b] if first else neg_chunk)[:, st:st + 1]
                    dve.tensor_reduce(tile_max, score_banks[:, 2 * st:2 * st + 2, 0:half], AX.XY, ALU.max,
                                      negate=True).then_inc(max_ready if first else chunk_max, 1)
                    if not first:
                        dve.wait_ge(chunk_max, 2 * s + st - 1)
                        dve.tensor_tensor(neg_max[b][:, st:st + 1], neg_max[1 - b][:, st:st + 1], tile_max,
                                          ALU.min).then_inc(max_ready, 1)

            def fade_diagonal(s):
                dve.wait_ge(fade_ready, s)
                for st in range(ST):
                    dve.tensor_scalar(diag[:, st, :], ident[:], fade[:, st:st + 1], None, ALU.mult).then_inc(diag_ready, 1)

            def step(s, b, first=False, next_half=HALF):
                half = HALF0 if first else HALF
                nt = half // P
                slot = 0 if first else b
                u = 0 if first else 5 * s - 2
                dve.wait_ge(turned, u + 2)
                turn_out((slot + 1) % 2, probsT[:, 0, :])
                if next_half:
                    k_low(0, s + 1, next_half)
                if nt == 4:
                    dve.wait_ge(turned, u + 4)
                    turn_out((slot + 1) % 2, probsT[:, 2, :])
                if next_half:
                    k_low(1, s + 1, next_half)
                if first:
                    dve.wait_ge(probs_ready, ST)
                    dve.tensor_copy(denom, row_sum).then_inc(denom_done, 1)
                else:
                    dve.wait_ge(denom_done, s)
                    dve.tensor_tensor(denom, denom, fade, ALU.mult).then_inc(denom_scaled, 1)
                    dve.wait_ge(denom_scaled, s)
                    dve.tensor_tensor(denom, denom, row_sum, ALU.add).then_inc(denom_done, 1)
                if next_half:
                    maxima(s + 1, 1 - b, next_half)
                    dve.wait_ge(max_ready, 2 * s + 4)
                    dve.tensor_tensor(neg_delta, neg_max[1 - b], neg_max[b], ALU.subtract).then_inc(delta_ready, 1)
                dve.wait_ge(o_ready, s + 1)
                if first:
                    dve.tensor_copy(o_acc[:], of_bank[:, 0:T]).then_inc(o_added, 1)
                else:
                    dve.wait_ge(o_added, s)
                    dve.tensor_tensor(o_acc[:], o_acc[:], of_bank[:, T:2 * T], ALU.mult).then_inc(o_faded, 1)
                    dve.wait_ge(o_faded, s)
                    dve.tensor_tensor(o_acc[:], o_acc[:], of_bank[:, 0:T], ALU.add).then_inc(o_added, 1)
                if next_half:
                    fade_diagonal(s + 1)

            SB = [score_banks[:, i, :] for i in range(4)]
            T6, T7 = bank[2], bank[3]
            B = SB + [bank[0][:], bank[1][:]]
            dve.wait_ge(x_in, 16)
            for st in range(ST):
                layer_norm("x", xres, st)
            k_low(0, 0, HALF0)
            k_low(1, 0, HALF0)
            dve.wait_ge(ev("q_high"), 1)
            dve.wait_ge(ev("q_split"), 1)
            dve.scalar_tensor_tensor(out=q_lo, in0=turn_bank[0][:, 0:T], scalar=XSCALE, in1=q_hi.bitcast(F32),
                                     op0=ALU.mult, op1=ALU.subtract).then_inc(ev("q_split"), 1)
            maxima(0, 0, HALF0, first=True)
            step(0, 0, first=True)
            with dve.Fori(1, LAST - 1, 2) as s:
                step(s, 1)
                step(s + 1, 0)
            step(LAST - 1, 1)
            dve.wait_ge(ev("wo_folded"), 1)
            dve.tensor_copy(wo_dup, kp_bank[:]).then_inc(ev("wo_dup_ready"), 1)
            step(LAST, 0, next_half=0)

            dve.wait_ge(denom_done, LAST + 1)
            then(dve.reciprocal(rdenom, denom))
            def attn_low(unit, first=0, stop=2):
                for g, ring, raw in list(halves(unit))[first:stop]:
                    dve.wait_ge(ev("attn_high"), g + 1)
                    dve.tensor_tensor(w_split[:, ring, 1, :], raw, w_split[:, ring, 0, :].bitcast(F32),
                                      ALU.subtract).then_inc(ev("attn_low"), 1)

            attn_low("kK", 0, 1)
            for st in range(ST):
                dve.wait_ge(ev("xattn_ready"), st + 1)
                then(dve.tensor_tensor(xres[:, st, :], xres[:, st, :], SB[2 + st], ALU.add))

            def turned_low(st, before=0):
                dve.wait_ge(ev("hT_high"), before + st + 1)
                cols = slice(st * P, (st + 1) * P)
                dve.tensor_tensor(hT_split[1][:, :, cols], (T6, T7)[st][:].rearrange("p (k t) -> p k t", k=KC),
                                  hT_split[0][:, :, cols].bitcast(F32), ALU.subtract).then_inc(ev("hT_done"), 1)

            def probsT_low(m, st):
                dve.wait_ge(ev("key_probsT_high"), nth(m, st))
                cols = slice(st * P, (st + 1) * P)
                dve.tensor_tensor(ET_split[m][1][:, :, cols], (T6, T7)[st][:].rearrange("p (n t) -> p n t", n=NT),
                                  ET_split[m][0][:, :, cols].bitcast(F32), ALU.subtract).then_inc(ev("key_probsT"), 1)

            for st in range(ST):
                dve.wait_ge(ev("xattn_ready"), ST + st + 1)
                then(dve.scalar_tensor_tensor(out=xres[:, st, :], in0=SB[st], scalar=rdenom[:, st:st + 1], in1=xres[:, st, :],
                                              op0=ALU.mult, op1=ALU.add))
                layer_norm("x1", xres, st, h0, between=(lambda: turned_low(0)) if st else None)
                dve.wait_ge(ev("ln_done"), normed("x1", st))
                layer_norm("h", h0, st)
                if st == 0:
                    attn_low("kK", 1, 2)
            attn_low("qK")
            turned_low(1)

            def low_part(e, b, i):
                dve.wait_ge(part_high, 12 * e + i + 1)
                raw = arena[:, expert_slots(b)[i // 2], (i % 2) * 1024:(i % 2 + 1) * 1024]
                return dve.tensor_tensor(w_split[:, i % 4, 1, :], raw, w_split[:, i % 4, 0, :].bitcast(F32), ALU.subtract)

            def soft_max(m, st, src):
                dve.wait_ge(ev("key_scores"), nth(m, st))
                then(dve.tensor_reduce(p_max[m][:, st:st + 1], src, AX.X, ALU.max))
                dve.tensor_scalar(p_bias[m][:, st:st + 1], p_max[m][:, st:st + 1], -PSCALE, None, ALU.mult).then_inc(ev("key_bias"), 1)

            def soft_norm(m, st):
                dve.wait_ge(ev("key_exp"), nth(m, st))
                then(dve.reciprocal(p_rsum[m][:, st:st + 1], p_sum[m][:, st:st + 1]))
                if m in "kq":
                    dve.tensor_scalar(E_sb[m][:, st, :], E_sb[m][:, st, :], p_rsum[m][:, st:st + 1], None, ALU.mult).then_inc(ev("key_normed"), 1)

            soft_max("k", 0, B[0])
            soft_max("k", 1, B[1])
            soft_norm("k", 0)
            soft_norm("k", 1)
            attn_low("vK")
            soft_max("q", 0, B[2])
            probsT_low("k", 0)
            soft_max("q", 1, B[3])
            soft_norm("q", 0)
            soft_norm("q", 1)
            probsT_low("k", 1)
            attn_low("kV")
            soft_max("v", 0, B[4])
            probsT_low("q", 0)
            soft_max("v", 1, B[5])
            probsT_low("q", 1)
            soft_norm("v", 0)
            soft_norm("v", 1)
            attn_low("qV")
            dve.wait_ge(ev("k_out_ready"), 1)
            dve.tensor_copy(kh[:, 2:4, :].rearrange("p c t -> p (c t)"), B[1]).then_inc(ev("kh_done"), 1)
            probsT_low("v", 0)
            probsT_low("v", 1)
            attn_low("vV")
            dve.wait_ge(ev("q_out_ready"), 1)
            dve.tensor_copy(qh[:, 2:4, :].rearrange("p c t -> p (c t)"), B[3]).then_inc(ev("qh_done"), 1)
            attn_low("pK")
            for st in range(ST):
                dve.wait_ge(ev("v_out_ready"), st + 1)
                dve.tensor_scalar(vh[:, st, :], B[4 + st], p_rsum["v"][:, st:st + 1], None, ALU.mult).then_inc(ev("vh_done"), 1)

            def head_softmax(c):
                if c == 0:
                    dve.wait_ge(causal_done, 2)
                if c >= 2:
                    dve.wait_ge(ev("head_turned"), HPC * (c - 1))
                for r, bk in enumerate([b[:] for b in bank] if c == 1 else SB):
                    dve.wait_ge(ev("head_scores"), HPC * c + r + 1)
                    dve.tensor_tensor(hp[:, c % 2, r, :], bk[:, 0:3 * P], causal[:].rearrange("p b k -> p (b k)"),
                                      ALU.add).then_inc(ev("head_masked"), 1)
                dve.wait_ge(ev("head_masked"), HPC * (c + 1))
                dve.tensor_reduce(h_max[:, c, 0, :], hp0[:, c % 2], AX.X, ALU.max).then_inc(ev("head_max"), 1)
                dve.tensor_reduce(h_max[:, c, 1, :], hp1[:, c % 2], AX.X, ALU.max).then_inc(ev("head_max"), 1)
                dve.wait_ge(ev("head_max"), 2 * c + 2)
                dve.tensor_scalar(h_bias[:, c], h_max[:, c], -HSCALE, None, ALU.mult).then_inc(ev("head_bias"), 1)

            def head_norm(c):
                dve.wait_ge(ev("head_probs"), 2 * HPC * (c + 1))
                then(dve.reciprocal(h_rsum[:, c], h_sum[:, c]))
                for half, part in enumerate((hp0, hp1)):
                    dve.tensor_tensor(part[:, c % 2], part[:, c % 2],
                                      h_rsum[:, c, half, :].unsqueeze(2).broadcast_to([P, HPC, (half + 1) * P]),
                                      ALU.mult).then_inc(ev("head_normed"), 1)

            for pair in range(2):
                for c in (2 * pair, 2 * pair + 1):
                    head_softmax(c)
                for c in (2 * pair, 2 * pair + 1):
                    head_norm(c)

            attn_low("pV")
            for pair in range(2):
                dve.wait_ge(ev("hT_high"), ST + pair + 1)
                tiles = slice(2 * pair, 2 * pair + 2)
                dve.tensor_tensor(hT_split[1][:, tiles, :].rearrange("p k t -> p (k t)"), B[4 + pair],
                                  hT_split[0][:, tiles, :].rearrange("p k t -> p (k t)").bitcast(F32),
                                  ALU.subtract).then_inc(ev("hT_done"), 1)
            soft_max("p", 0, B[0])
            soft_max("p", 1, B[1])
            for st in range(ST):
                probsT_low("p", st)
                soft_norm("p", st)
            def ffk_low(g):
                dve.wait_ge(ev("ffk_high"), g + 1)
                dve.tensor_tensor(w_split[:, g % 4, 1, :], ffk_raw(g), w_split[:, g % 4, 0, :].bitcast(F32),
                                  ALU.subtract).then_inc(ev("ffk_low"), 1)

            ffk_low(0)
            for st in range(ST):
                dve.wait_ge(ev("p_out_ready"), st + 1)
                then(dve.scalar_tensor_tensor(out=h0[:, st, :], in0=B[2 + st], scalar=p_rsum["p"][:, st:st + 1],
                                              in1=h0[:, st, :], op0=ALU.mult, op1=ALU.add))
                layer_norm("f", h0, st, between=(lambda: turned_low(0, 2 * ST)) if st else None)
            for g in (1, 2, 3):
                ffk_low(g)
            turned_low(1, 2 * ST)
            for st in range(ST):
                then(dve.tensor_tensor(xres[:, st, :], xres[:, st, :], h0[:, st, :], ALU.add))
            fb = (SB, [b[:] for b in bank])
            def f_maximum(st, n4):
                dve.wait_ge(ev("f_scores"), f_place(st, n4))
                then(dve.tensor_reduce(f_max[:, st, n4:n4 + 1], fb[st][n4], AX.X, ALU.max))
                if n4 == 3:
                    then(dve.tensor_reduce(p_max["f"][:, st:st + 1], f_max[:, st, :], AX.X, ALU.max))
                    dve.tensor_scalar(p_bias["f"][:, st:st + 1], p_max["f"][:, st:st + 1], -PSCALE, None, ALU.mult).then_inc(ev("f_bias"), 1)

            def feed_forward_sum(st):
                dve.wait_ge(ev("f_exp"), 4 * st + 4)
                then(dve.tensor_reduce(p_sum["f"][:, st:st + 1], f_part[:, st, :], AX.X, ALU.add))
                then(dve.reciprocal(p_rsum["f"][:, st:st + 1], p_sum["f"][:, st:st + 1]))

            def f_turned_low(st, banks=range(4)):
                for n4 in banks:
                    dve.wait_ge(ev("f_turned_high"), 4 * st + n4 + 1)
                    tiles = slice(4 * n4, 4 * n4 + 4)
                    dve.tensor_tensor(fT_lo[:, tiles, :].rearrange("p n t -> p (n t)"), fb[st][n4],
                                      fT_hi[:, tiles, :].rearrange("p n t -> p (n t)").bitcast(F32),
                                      ALU.subtract).then_inc(ev("f_turned_low"), 1)

            def ffv_low(g):
                dve.wait_ge(ev("ffv_high"), g + 1)
                dve.tensor_tensor(w_split[:, g % 4, 1, :], ffv_raw(g % (NFT // 2)), w_split[:, g % 4, 0, :].bitcast(F32),
                                  ALU.subtract).then_inc(ev("ffv_low"), 1)

            def feed_forward_out(st):
                dve.wait_ge(ev("ffv_used"), NFT // 2 * (st + 1))
                then(dve.scalar_tensor_tensor(out=xres[:, st, :], in0=fb[0][st], scalar=p_rsum["f"][:, st:st + 1],
                                              in1=xres[:, st, :], op0=ALU.mult, op1=ALU.add))
                layer_norm("e", xres, st)

            f_maximum(0, 0)
            f_maximum(0, 1)
            for g in (4, 5, 6):
                ffk_low(g)
            f_maximum(1, 0)
            f_maximum(1, 1)
            ffk_low(7)
            f_maximum(0, 2)
            f_maximum(0, 3)
            ffv_low(0)
            f_maximum(1, 2)
            ffv_low(1)
            f_turned_low(0, (0, 1))
            ffv_low(2)
            f_turned_low(0, (2,))
            ffv_low(3)
            f_turned_low(0, (3,))
            f_maximum(1, 3)
            for g in range(4, 11):
                ffv_low(g)
            f_turned_low(1)
            for g in range(11, 16):
                ffv_low(g)
            for st in range(ST):
                feed_forward_sum(st)
            feed_forward_out(0)
            feed_forward_out(1)
            then(low_part(0, 0, 0))
            then(low_part(0, 0, 1))

            dve.wait_ge(ev("logits_ready"), 1)
            dve.wait_ge(ids_done, E + 2)
            dve.tensor_copy(logits, T6[:, 0:ST * E].rearrange("p (s e) -> p s e", s=ST)).then_inc(ev("logits_taken"), 1)
            dve.wait_ge(ev("logits_taken"), 1)
            ids = expert_id.unsqueeze(1).broadcast_to([P, ST, E])

            def wide(col):
                return col.unsqueeze(2).broadcast_to([P, ST, E])

            src = logits
            for n in range(2):
                then(dve.tensor_reduce(top[n], src, AX.X, ALU.max))
                then(dve.tensor_tensor(cand, src, wide(top[n]), ALU.is_lt))
                then(dve.scalar_tensor_tensor(out=cand, in0=cand, scalar=float(E), in1=ids, op0=ALU.mult, op1=ALU.add))
                then(dve.tensor_reduce(pick, cand, AX.X, ALU.min))
                then(dve.tensor_tensor(hot[n], ids, wide(pick), ALU.is_equal))
                if n == 0:
                    then(dve.scalar_tensor_tensor(out=rest, in0=hot[0], scalar=-BIG, in1=logits, op0=ALU.mult, op1=ALU.add))
                    src = rest
            dve.tensor_tensor(chosen[:], hot[0], hot[1], ALU.add).then_inc(ev("chosen_ready"), 1)
            dve.tensor_tensor(gap, top[1], top[0], ALU.subtract).then_inc(ev("gap_ready"), 1)
            dve.wait_ge(ev("second_ready"), 1)
            then(dve.tensor_scalar(both, second, 1.0, None, ALU.add))
            then(dve.reciprocal(first, both))
            then(dve.tensor_tensor(second, second, first, ALU.mult))
            then(dve.tensor_tensor(hot[0], hot[0], wide(first), ALU.mult))
            then(dve.tensor_tensor(hot[1], hot[1], wide(second), ALU.mult))
            then(dve.tensor_tensor(route, hot[0], hot[1], ALU.add))

            dve.wait_ge(ev("counted"), 1)
            counts = T6[:, ST * E:(2 * ST + 1) * E].rearrange("p (s e) -> p s e", e=E)
            then(dve.tensor_reduce(most, counts[:, 2, :], AX.X, ALU.max))
            dve.tensor_scalar(flag[:], most, float(CAP), None, ALU.is_gt).then_inc(ev("flag_ready"), 1)
            then(dve.scalar_tensor_tensor(out=place, in0=chosen[:].bitcast(F32), scalar=-FAR, in1=counts[:, 0:2, :], op0=ALU.mult,
                                          op1=ALU.add))

            def select(e):
                for st in range(ST):
                    last = dve.tensor_scalar(sel[:, st, e, :], slot_id[:], place[:, st, e:e + 1], None, ALU.is_equal)
                return last

            select(0)
            select(1).then_inc(ev("sel_ready"), 1)
            dve.wait_ge(ev("flag_ready"), 1)
            crowded = dve.value_load(flag[0:1, 0:1], min_val=0, max_val=1)

            def gate_hidden(e):
                for j in range(HT):
                    g = HT * e + j
                    dve.wait_ge(silu_ready, g + 1)
                    dve.tensor_tensor(hid[:, j, :], sil[:, j % 4, :], SB[j % 4][:, T:2 * T], ALU.mult).then_inc(hid_ready, 1)

            def add_expert(e, b, col):
                dve.wait_ge(y_ready, e + 1)
                for st in range(ST):
                    if st or not isinstance(e, int) or e:
                        dve.wait_ge(ev("x_added"), 2 * e + st)
                    last = dve.scalar_tensor_tensor(out=xres[:, st, :], in0=bank[2 * b + st][:], scalar=col[:, st, :],
                                                    in1=xres[:, st, :], op0=ALU.mult, op1=ALU.add)
                    last.then_inc(ev("x_added"), 1)
                dve.memset(most, 0.0).then_inc(part_low, 12)

            def low(e, b, i):
                low_part(e, b, i).then_inc(part_low, 1)

            def gathered_low(e):
                dve.wait_ge(ev("gathered"), e + 2)
                for a in range(2):
                    dve.tensor_copy(xg[:, 1, 2 * a:2 * a + 2, :].rearrange("p k t -> p (k t)"), SB[2 * a + 1]).then_inc(ev("xg_low"), 1)

            def sparse_expert(e, b, last_one=False):
                def gate(half):
                    dve.wait_ge(silu_ready, 2 * e + half + 1)
                    dve.wait_ge(part_used, 12 * e + 7 + half)
                    dve.tensor_tensor(hid_rows[:, half, :], sil_g[:, half, :], SB[2 * half + 1], ALU.mult).then_inc(ev("hid_made"), 1)

                def hidden_low(half):
                    dve.wait_ge(ev("hidT_high"), 2 * e + half + 1)
                    hi, lo = (hidT[:, part, 4 * half:4 * half + 4, :].rearrange("p j t -> p (j t)") for part in range(2))
                    dve.tensor_tensor(lo, hidden_bank(b, half), hi.bitcast(F32), ALU.subtract).then_inc(ev("hidT_low"), 1)

                for i in range(4, 10):
                    low(e, b, i)
                gate(0)
                gate(1)
                hidden_low(0)
                low(e, b, 10)
                hidden_low(1)
                low(e, b, 11)
                if b == 0:
                    dve.wait_ge(ev("sel_turned"), e + 2)
                    dve.tensor_reduce(place_weight, SB[1][:, 0:4].rearrange("p (j a) -> p j a", a=2), AX.X,
                                      ALU.add).then_inc(ev("weights_ready"), 2)
                elif not last_one:
                    gathered_low(e + 1)
                if not last_one:
                    for i in range(4):
                        low(e + 1, 1 - b, i)
                dve.wait_ge(ev("y_high"), e + 1)
                if b == 0:
                    dve.wait_ge(ev("weights_ready"), e + 2)
                dve.scalar_tensor_tensor(out=y_lo, in0=bank[1][:], scalar=place_weight[:, b:b + 1], in1=y_hi.bitcast(F32),
                                         op0=ALU.mult, op1=ALU.subtract).then_inc(ev("y_low"), 1)

            with dve.If(crowded < 1):
                dve.memset(most, 0.0).then_inc(part_low, 2)
                low(0, 0, 2)
                low(0, 0, 3)
                then(dve.tensor_copy(route_split[:, :, :, 0], route))
                dve.tensor_tensor(route_split[:, :, :, 1], route, route_split[:, :, :, 0].bitcast(F32),
                                  ALU.subtract).then_inc(ev("route_parts"), 1)
                gathered_low(0)
                for e in range(2, E):
                    last = select(e)
                last.then_inc(ev("sel_ready"), 1)
                sparse_expert(0, 0)
                sparse_expert(1, 1)
                with dve.Fori(2, E - 3, 2) as e:
                    sparse_expert(e, 0)
                    sparse_expert(e + 1, 1)
                sparse_expert(E - 2, 0)
                sparse_expert(E - 1, 1, last_one=True)
                dve.wait_ge(ev("scattered"), E)
                for st in range(ST):
                    dve.tensor_tensor(xres[:, st, :], xres[:, st, :], bank[2 + st], ALU.add).then_inc(
                        ev("x_added"), ST * (E - 1) + 1 if st == 0 else 1)
            with dve.Else():
                dve.wait_ge(ev("rows_low"), ST)
                for e in range(2):
                    gate_hidden(e)
                    add_expert(e, e, route[:, :, e:e + 1])
                with dve.Fori(2, E - 1, 2) as e:
                    for b in range(2):
                        gate_hidden(e + b)
                        add_expert(e + b, b, route[:, :, bass.ds(e + b, 1)])


def kernel(x, ctx_1024, L0_xattn_wi, L0_xattn_Wo, L0_xattn_bo, L0_attn_qK, L0_attn_qV, L0_attn_kK, L0_attn_kV,
           L0_attn_vK, L0_attn_vV, L0_attn_pK, L0_attn_pV, L0_attn_fK, L0_attn_fV, L0_ffn_w12, L0_ffn_w3, L0_ffn_gate_w):
    import numpy as np
    import concourse.bacc as bacc
    from concourse import mybir as mb
    from concourse.bass_utils import run_bass_kernel_spmd as run

    laid = {
        "x": np.asarray(x)[0], "ctxT": np.asarray(ctx_1024)[0].T, "wi": L0_xattn_wi, "Wo": L0_xattn_Wo, "bo": L0_xattn_bo,
        "qKT": np.asarray(L0_attn_qK).T, "qV": L0_attn_qV, "kKT": np.asarray(L0_attn_kK).T, "kV": L0_attn_kV,
        "vKT": np.asarray(L0_attn_vK).T, "vV": L0_attn_vV, "pKT": np.asarray(L0_attn_pK).T, "pV": L0_attn_pV,
        "fKT": np.asarray(L0_attn_fK).T, "fV": L0_attn_fV,
        "w12T": np.asarray(L0_ffn_w12).reshape(8, 2, 2, 512, 512).transpose(0, 4, 2, 1, 3).reshape(8, 512, 2048),
        "w3T": np.asarray(L0_ffn_w3).transpose(0, 2, 1), "gateT": np.asarray(L0_ffn_gate_w).T,
    }
    nc = bacc.Bacc("TRN2", target_bir_lowering=False, num_devices=1)
    arrays, args = {}, []
    for name, a in laid.items():
        a = np.ascontiguousarray(a)
        arrays["in_" + name] = a
        args.append(nc.dram_tensor("in_" + name, a.shape, mb.dt.from_np(a.dtype), kind="ExternalInput").ap())
    T, C = laid["x"].shape
    args.append(nc.dram_tensor("out_x", (T, C), mb.dt.float32, kind="ExternalOutput").ap())
    perceiver_layer(nc, *args)
    r = run(nc, [arrays], core_ids=[0])
    return r.results[0]["out_x"].reshape(1, T, C)
```
